# Optimizing a Trainium2 kernel written in Bass

```python
import numpy as np
import jax
import jax.numpy as jnp

def _softmax(x, axis=-1):
    return jax.nn.softmax(x, axis=axis)

def _gelu(x):
    return jax.nn.gelu(x, approximate=True)

def _silu(x):
    return jax.nn.silu(x)

def _sigmoid(x):
    return jax.nn.sigmoid(x)

def _layernorm(x, axis=-1, eps=1e-05):
    m = jnp.mean(x, axis=axis, keepdims=True)
    v = jnp.var(x, axis=axis, keepdims=True)
    return (x - m) / jnp.sqrt(v + eps)

def _scatter_add(tgt, idx, src, axis=0):
    return tgt.at[idx].add(src)

def _segment_sum(src, seg, n):
    return jax.ops.segment_sum(src, seg, n)
kernel_name = 'mk_flamingo_gated_d2_seqx_r4_04c359'

def setup_inputs(seed: int=0):
    np.random.seed(seed)
    _w = jnp.asarray

    def _rec_inputs():
        import jax
        import jax.numpy as jnp
        _rk = jax.random.key(seed)
        x = 7.22e-05 + 1 * jax.random.normal(jax.random.fold_in(_rk, 1), (16, 100, 256), jnp.float32)
        _lenS = 100 - jax.random.randint(jax.random.fold_in(_rk, 7), (16,), 0, max(1, 100 // 4) + 1, jnp.int32)
        _lenS2 = 361 - jax.random.randint(jax.random.fold_in(_rk, 8), (16,), 0, max(1, 361 // 4) + 1, jnp.int32)
        _ctx_1024P = jax.random.normal(jax.random.fold_in(_rk, 11), (16, 16, 256), jnp.float32)
        _ctx_1024c = jax.random.dirichlet(jax.random.fold_in(_rk, 511), 0.3 * jnp.ones((16,), jnp.float32), (16, 361))
        _ctx_1024t = jnp.einsum('bsk,bkd->bsd', _ctx_1024c, _ctx_1024P)
        _ctx_1024t = _ctx_1024t * jax.lax.rsqrt(jnp.mean(jnp.square(_ctx_1024t)) + 1e-12) * 0.953939
        ctx_1024 = 4.13588e-05 + 0.999923 * (_ctx_1024t + 0.3 * jax.random.normal(jax.random.fold_in(_rk, 611), (16, 361, 256), jnp.float32))
        _validS = jnp.arange(100)[None, :] < _lenS[:, None]
        _validS2 = jnp.arange(361)[None, :] < _lenS2[:, None]
        _causal = jnp.tril(jnp.ones((100, 100), dtype=bool))
        mask_Bx1x1xS2_ff0 = jnp.where(jnp.ones((16, 1, 1, 361), dtype=bool), 0.0, -1000000000.0).astype(jnp.float32)
        _g = jax.random.normal(jax.random.fold_in(_rk, 9001), (2, 2), jnp.float32)
        _g = jnp.sign(_g) * jnp.maximum(jnp.abs(_g), 1.0) + (_g == 0) * 1.0
        g_xattn = _g[0]
        g_ffn = _g[1]
        return (x, ctx_1024, mask_Bx1x1xS2_ff0, g_xattn, g_ffn)
    x, ctx_1024, mask_Bx1x1xS2_ff0, g_xattn, g_ffn = _rec_inputs()

    def _L0_xattn_setup():
        import jax, jax.numpy as jnp
        import numpy as np
        N_HEAD, MODEL_DIM, KEY_DIM, VALUE_DIM = (16, 256, 64, 64)
        B, S = (4, 512)
        EPS = 1e-05
        TEMP = float(np.sqrt(KEY_DIM))
        key = jax.random.key(seed)
        ks = jax.random.split(key, 12)
        d = {'query': jax.random.normal(ks[0], (B, S, MODEL_DIM), jnp.float32), 'key': jax.random.normal(ks[1], (B, S, MODEL_DIM), jnp.float32), 'value': jax.random.normal(ks[2], (B, S, MODEL_DIM), jnp.float32), 'Wq': jax.random.normal(ks[3], (MODEL_DIM, N_HEAD * KEY_DIM), jnp.float32) * np.sqrt(2.0 / (MODEL_DIM + KEY_DIM)), 'bq': jnp.zeros((N_HEAD * KEY_DIM,), jnp.float32), 'Wk': jax.random.normal(ks[4], (MODEL_DIM, N_HEAD * KEY_DIM), jnp.float32) * np.sqrt(2.0 / (MODEL_DIM + KEY_DIM)), 'bk': jnp.zeros((N_HEAD * KEY_DIM,), jnp.float32), 'Wv': jax.random.normal(ks[5], (MODEL_DIM, N_HEAD * VALUE_DIM), jnp.float32) * np.sqrt(2.0 / (MODEL_DIM + VALUE_DIM)), 'bv': jnp.zeros((N_HEAD * VALUE_DIM,), jnp.float32), 'Wo': jax.random.normal(ks[6], (N_HEAD * VALUE_DIM, MODEL_DIM), jnp.float32) * np.sqrt(2.0 / (N_HEAD * VALUE_DIM + MODEL_DIM)), 'bo': jnp.zeros((MODEL_DIM,), jnp.float32), 'ln_gamma': jnp.ones((MODEL_DIM,), jnp.float32), 'ln_beta': jnp.zeros((MODEL_DIM,), jnp.float32)}
        return d
    _L0_xattn_all = _L0_xattn_setup()
    _L0_xattn_in = {k: v for k, v in _L0_xattn_all.items() if k in ('Wq', 'bq', 'Wk', 'bk', 'Wv', 'bv', 'Wo', 'bo', 'ln_gamma', 'ln_beta')}
    del _L0_xattn_all

    def _L0_ffn_setup():
        import jax, jax.numpy as jnp
        import numpy as np
        NUM_EXPERTS = 8
        NUM_LANGS = 4
        TOP_K = 2
        D_MODEL = 256
        EXPERT_SIZE = 1024
        B, S = (2, 512)
        key = jax.random.key(seed)
        ks = jax.random.split(key, 6)

        def xavier(k, shape, fan_in, fan_out):
            a = float(np.sqrt(6.0 / (fan_in + fan_out)))
            return jax.random.uniform(k, shape, jnp.float32, -a, a)
        return {'x': jax.random.normal(ks[0], (B, S, D_MODEL), jnp.float32), 'router_w': xavier(ks[1], (NUM_EXPERTS, D_MODEL), D_MODEL, NUM_EXPERTS), 'router_b': jnp.zeros((NUM_EXPERTS,), jnp.float32), 'lang_w': xavier(ks[2], (NUM_LANGS, D_MODEL), D_MODEL, NUM_LANGS), 'lang_b': jnp.zeros((NUM_LANGS,), jnp.float32), 'w1': xavier(ks[3], (NUM_EXPERTS, D_MODEL, EXPERT_SIZE), D_MODEL, EXPERT_SIZE), 'b1': jnp.zeros((NUM_EXPERTS, EXPERT_SIZE), jnp.float32), 'w2': xavier(ks[4], (NUM_EXPERTS, EXPERT_SIZE, D_MODEL), EXPERT_SIZE, D_MODEL), 'b2': jnp.zeros((NUM_EXPERTS, D_MODEL), jnp.float32)}
    _L0_ffn_all = _L0_ffn_setup()
    _L0_ffn_in = {k: v for k, v in _L0_ffn_all.items() if k in ('router_w', 'router_b', 'lang_w', 'lang_b', 'w1', 'b1', 'w2', 'b2')}
    del _L0_ffn_all

    def _L1_xattn_setup():
        import jax, jax.numpy as jnp
        import numpy as np
        D_MODEL = 256
        NUM_HEADS = 16
        DEPTH = D_MODEL // NUM_HEADS

        def _split_heads(x):
            B, S, _ = x.shape
            return x.reshape(B, S, NUM_HEADS, DEPTH).transpose(0, 2, 1, 3)
        key = jax.random.key(seed)
        ks = jax.random.split(key, 12)
        B, S = (4, 512)
        scale = 1.0 / np.sqrt(D_MODEL)
        inp = {'query': jax.random.normal(ks[0], (B, S, D_MODEL), dtype=jnp.float32), 'key': jax.random.normal(ks[1], (B, S, D_MODEL), dtype=jnp.float32), 'value': jax.random.normal(ks[2], (B, S, D_MODEL), dtype=jnp.float32), 'mask': jnp.zeros((B, 1, 1, S), dtype=jnp.float32), 'Wq': jax.random.normal(ks[3], (D_MODEL, D_MODEL), dtype=jnp.float32) * scale, 'bq': jnp.zeros((D_MODEL,), dtype=jnp.float32), 'Wk': jax.random.normal(ks[4], (D_MODEL, D_MODEL), dtype=jnp.float32) * scale, 'bk': jnp.zeros((D_MODEL,), dtype=jnp.float32), 'Wv': jax.random.normal(ks[5], (D_MODEL, D_MODEL), dtype=jnp.float32) * scale, 'bv': jnp.zeros((D_MODEL,), dtype=jnp.float32), 'Wo': jax.random.normal(ks[6], (D_MODEL, D_MODEL), dtype=jnp.float32) * scale, 'bo': jnp.zeros((D_MODEL,), dtype=jnp.float32)}
        return inp
    _L1_xattn_all = _L1_xattn_setup()
    _L1_xattn_in = {k: v for k, v in _L1_xattn_all.items() if k in ('Wq', 'bq', 'Wk', 'bk', 'Wv', 'bv', 'Wo', 'bo')}
    del _L1_xattn_all

    def _L1_ffn_setup():
        import jax, jax.numpy as jnp
        import numpy as np
        D_MODEL = 256
        HIDDEN = 256
        NUM_EXPERTS = 8
        TOP_K = 2
        key = jax.random.key(seed)
        ks = jax.random.split(key, 10)
        s = 0.02
        return {'x': jax.random.normal(ks[0], (2, 512, D_MODEL), dtype=jnp.float32), 'gate_w': jax.random.normal(ks[1], (NUM_EXPERTS, D_MODEL), dtype=jnp.float32) * s, 'up_w': jax.random.normal(ks[2], (NUM_EXPERTS, D_MODEL, HIDDEN), dtype=jnp.float32) * s, 'up_b': jnp.zeros((NUM_EXPERTS, HIDDEN), dtype=jnp.float32), 'down_w': jax.random.normal(ks[3], (NUM_EXPERTS, HIDDEN, D_MODEL), dtype=jnp.float32) * s, 'down_b': jnp.zeros((NUM_EXPERTS, D_MODEL), dtype=jnp.float32), 'sh_up_w': jax.random.normal(ks[4], (D_MODEL, HIDDEN), dtype=jnp.float32) * s, 'sh_up_b': jnp.zeros((HIDDEN,), dtype=jnp.float32), 'sh_down_w': jax.random.normal(ks[5], (HIDDEN, D_MODEL), dtype=jnp.float32) * s, 'sh_down_b': jnp.zeros((D_MODEL,), dtype=jnp.float32)}
    _L1_ffn_all = _L1_ffn_setup()
    _L1_ffn_in = {k: v for k, v in _L1_ffn_all.items() if k in ('gate_w', 'up_w', 'up_b', 'down_w', 'down_b', 'sh_up_w', 'sh_up_b', 'sh_down_w', 'sh_down_b')}
    del _L1_ffn_all
    return {'x': x, 'ctx_1024': ctx_1024, 'mask_Bx1x1xS2_ff0': mask_Bx1x1xS2_ff0, 'g_xattn': g_xattn, 'g_ffn': g_ffn, 'L0_xattn_Wq': _L0_xattn_in['Wq'], 'L0_xattn_bq': _L0_xattn_in['bq'], 'L0_xattn_Wk': _L0_xattn_in['Wk'], 'L0_xattn_bk': _L0_xattn_in['bk'], 'L0_xattn_Wv': _L0_xattn_in['Wv'], 'L0_xattn_bv': _L0_xattn_in['bv'], 'L0_xattn_Wo': _L0_xattn_in['Wo'], 'L0_xattn_bo': _L0_xattn_in['bo'], 'L0_xattn_ln_gamma': _L0_xattn_in['ln_gamma'], 'L0_xattn_ln_beta': _L0_xattn_in['ln_beta'], 'L0_ffn_router_w': _L0_ffn_in['router_w'], 'L0_ffn_router_b': _L0_ffn_in['router_b'], 'L0_ffn_lang_w': _L0_ffn_in['lang_w'], 'L0_ffn_lang_b': _L0_ffn_in['lang_b'], 'L0_ffn_w1': _L0_ffn_in['w1'], 'L0_ffn_b1': _L0_ffn_in['b1'], 'L0_ffn_w2': _L0_ffn_in['w2'], 'L0_ffn_b2': _L0_ffn_in['b2'], 'L1_xattn_Wq': _L1_xattn_in['Wq'], 'L1_xattn_bq': _L1_xattn_in['bq'], 'L1_xattn_Wk': _L1_xattn_in['Wk'], 'L1_xattn_bk': _L1_xattn_in['bk'], 'L1_xattn_Wv': _L1_xattn_in['Wv'], 'L1_xattn_bv': _L1_xattn_in['bv'], 'L1_xattn_Wo': _L1_xattn_in['Wo'], 'L1_xattn_bo': _L1_xattn_in['bo'], 'L1_ffn_gate_w': _L1_ffn_in['gate_w'], 'L1_ffn_up_w': _L1_ffn_in['up_w'], 'L1_ffn_up_b': _L1_ffn_in['up_b'], 'L1_ffn_down_w': _L1_ffn_in['down_w'], 'L1_ffn_down_b': _L1_ffn_in['down_b'], 'L1_ffn_sh_up_w': _L1_ffn_in['sh_up_w'], 'L1_ffn_sh_up_b': _L1_ffn_in['sh_up_b'], 'L1_ffn_sh_down_w': _L1_ffn_in['sh_down_w'], 'L1_ffn_sh_down_b': _L1_ffn_in['sh_down_b']}

def reference(x, ctx_1024, mask_Bx1x1xS2_ff0, g_xattn, g_ffn, L0_xattn_Wq, L0_xattn_bq, L0_xattn_Wk, L0_xattn_bk, L0_xattn_Wv, L0_xattn_bv, L0_xattn_Wo, L0_xattn_bo, L0_xattn_ln_gamma, L0_xattn_ln_beta, L0_ffn_router_w, L0_ffn_router_b, L0_ffn_lang_w, L0_ffn_lang_b, L0_ffn_w1, L0_ffn_b1, L0_ffn_w2, L0_ffn_b2, L1_xattn_Wq, L1_xattn_bq, L1_xattn_Wk, L1_xattn_bk, L1_xattn_Wv, L1_xattn_bv, L1_xattn_Wo, L1_xattn_bo, L1_ffn_gate_w, L1_ffn_up_w, L1_ffn_up_b, L1_ffn_down_w, L1_ffn_down_b, L1_ffn_sh_up_w, L1_ffn_sh_up_b, L1_ffn_sh_down_w, L1_ffn_sh_down_b):
    import jax
    import jax.numpy as jnp

    def _L0_xattn_ref(query, key, value, Wq, bq, Wk, bk, Wv, bv, Wo, bo, ln_gamma, ln_beta):
        import jax, jax.numpy as jnp
        import numpy as np
        N_HEAD, MODEL_DIM, KEY_DIM, VALUE_DIM = (16, 256, 64, 64)
        B, S = (4, 512)
        EPS = 1e-05
        TEMP = float(np.sqrt(KEY_DIM))
        b, sq, _ = query.shape
        residual = query
        q = (query @ Wq + bq).reshape(b, sq, N_HEAD, KEY_DIM)
        k = (key @ Wk + bk).reshape(b, key.shape[1], N_HEAD, KEY_DIM)
        v = (value @ Wv + bv).reshape(b, value.shape[1], N_HEAD, VALUE_DIM)
        scores = jnp.einsum('bqhd,bkhd->bhqk', q, k) / TEMP
        attn = jax.nn.softmax(scores, axis=-1)
        out = jnp.einsum('bhqk,bkhd->bqhd', attn, v).reshape(b, sq, N_HEAD * VALUE_DIM)
        out = out @ Wo + bo + residual
        mu = jnp.mean(out, axis=-1, keepdims=True)
        var = jnp.var(out, axis=-1, keepdims=True)
        return (out - mu) * jax.lax.rsqrt(var + EPS) * ln_gamma + ln_beta

    def _L0_ffn_ref(x, router_w, router_b, lang_w, lang_b, w1, b1, w2, b2):
        import jax, jax.numpy as jnp
        import numpy as np
        NUM_EXPERTS = 8
        NUM_LANGS = 4
        TOP_K = 2
        D_MODEL = 256
        EXPERT_SIZE = 1024
        B, S = (2, 512)
        lang_logits = x @ lang_w.T + lang_b
        lang_probs = jax.nn.softmax(lang_logits, axis=-1)
        lp_pad = jnp.pad(lang_probs, ((0, 0), (0, 0), (0, 1)))
        idx = jnp.arange(NUM_EXPERTS) % NUM_LANGS
        expert_weights = lp_pad[..., idx] + lp_pad[..., idx + 1]
        router_logits = x @ router_w.T + router_b + 0.1 * expert_weights
        router_probs = jax.nn.softmax(router_logits, axis=-1)
        top_p, top_i = jax.lax.top_k(router_probs, TOP_K)
        top_p = top_p / top_p.sum(axis=-1, keepdims=True)
        h = jax.nn.gelu(jnp.einsum('bsd,edh->bseh', x, w1) + b1, approximate=False)
        expert_out = jnp.einsum('bseh,ehd->bsed', h, w2) + b2
        sel = jnp.take_along_axis(expert_out, top_i[..., None], axis=2)
        return (top_p[..., None] * sel).sum(axis=2)

    def _L1_xattn_ref(query, key, value, mask, Wq, bq, Wk, bk, Wv, bv, Wo, bo):
        import jax, jax.numpy as jnp
        import numpy as np
        D_MODEL = 256
        NUM_HEADS = 16
        DEPTH = D_MODEL // NUM_HEADS

        def _split_heads(x):
            B, S, _ = x.shape
            return x.reshape(B, S, NUM_HEADS, DEPTH).transpose(0, 2, 1, 3)
        B, Sq, _ = query.shape
        q = _split_heads(query @ Wq + bq)
        k = _split_heads(key @ Wk + bk)
        v = _split_heads(value @ Wv + bv)
        logits = jnp.einsum('bhqd,bhkd->bhqk', q, k) / jnp.sqrt(jnp.float32(DEPTH))
        logits = logits + mask * -1000000000.0
        attn = jax.nn.softmax(logits, axis=-1)
        ctx = jnp.einsum('bhqk,bhkd->bhqd', attn, v)
        ctx = ctx.transpose(0, 2, 1, 3).reshape(B, Sq, D_MODEL)
        return ctx @ Wo + bo

    def _L1_ffn_ref(x, gate_w, up_w, up_b, down_w, down_b, sh_up_w, sh_up_b, sh_down_w, sh_down_b):
        import jax, jax.numpy as jnp
        import numpy as np
        D_MODEL = 256
        HIDDEN = 256
        NUM_EXPERTS = 8
        TOP_K = 2
        b, s, d = x.shape
        xf = x.reshape(-1, d)
        shared = jax.nn.silu(x @ sh_up_w + sh_up_b) @ sh_down_w + sh_down_b
        logits = xf @ gate_w.T
        scores = jax.nn.softmax(logits, axis=-1)
        topk_w, topk_i = jax.lax.top_k(scores, TOP_K)
        topk_w = topk_w / (topk_w.sum(axis=-1, keepdims=True) + 1e-20)
        comb = (jax.nn.one_hot(topk_i, NUM_EXPERTS, dtype=xf.dtype) * topk_w[..., None]).sum(axis=1)
        h = jnp.einsum('nd,edh->neh', xf, up_w) + up_b
        h = jax.nn.silu(h)
        ye = jnp.einsum('neh,ehd->ned', h, down_w) + down_b
        y = jnp.einsum('ned,ne->nd', ye, comb).reshape(b, s, d)
        return y + shared
    x = x + jnp.tanh(g_xattn[0]) * _L0_xattn_ref(_layernorm(x, axis=-1), ctx_1024, ctx_1024, L0_xattn_Wq, L0_xattn_bq, L0_xattn_Wk, L0_xattn_bk, L0_xattn_Wv, L0_xattn_bv, L0_xattn_Wo, L0_xattn_bo, L0_xattn_ln_gamma, L0_xattn_ln_beta)
    x = x + jnp.tanh(g_ffn[0]) * _L0_ffn_ref(_layernorm(x, axis=-1), L0_ffn_router_w, L0_ffn_router_b, L0_ffn_lang_w, L0_ffn_lang_b, L0_ffn_w1, L0_ffn_b1, L0_ffn_w2, L0_ffn_b2)
    x = x + jnp.tanh(g_xattn[1]) * _L1_xattn_ref(_layernorm(x, axis=-1), ctx_1024, ctx_1024, mask_Bx1x1xS2_ff0, L1_xattn_Wq, L1_xattn_bq, L1_xattn_Wk, L1_xattn_bk, L1_xattn_Wv, L1_xattn_bv, L1_xattn_Wo, L1_xattn_bo)
    x = x + jnp.tanh(g_ffn[1]) * _L1_ffn_ref(_layernorm(x, axis=-1), L1_ffn_gate_w, L1_ffn_up_w, L1_ffn_up_b, L1_ffn_down_w, L1_ffn_down_b, L1_ffn_sh_up_w, L1_ffn_sh_up_b, L1_ffn_sh_down_w, L1_ffn_sh_down_b)
    return x

_drawn_inputs = setup_inputs


def setup_inputs(seed=0):
    import zlib

    import numpy as np

    out = dict(_drawn_inputs(seed))
    spreads = {'g_ffn': (-1.0, 0.6),
     'L0_xattn_bq': (0.0, 0.319),
     'L0_xattn_bk': (0.0, 0.8),
     'L0_xattn_bv': (0.0, 0.1),
     'L0_xattn_bo': (0.0, 0.1),
     'L0_xattn_ln_gamma': (1.0, 0.2),
     'L0_xattn_ln_beta': (0.0, 0.1),
     'L0_ffn_router_b': (0.0, 0.291),
     'L0_ffn_lang_b': (0.0, 0.8),
     'L0_ffn_b1': (0.0, 0.294),
     'L0_ffn_b2': (0.0, 0.1),
     'L1_xattn_bq': (0.0, 0.621),
     'L1_xattn_bk': (0.0, 0.8),
     'L1_xattn_bv': (0.0, 0.1),
     'L1_xattn_bo': (0.0, 0.1),
     'L1_ffn_up_b': (0.0, 0.8),
     'L1_ffn_down_b': (0.0, 0.1),
     'L1_ffn_sh_up_b': (0.0, 0.8),
     'L1_ffn_sh_down_b': (0.0, 0.1)}
    factors = {'L0_ffn_lang_w': 3.791, 'L1_ffn_up_w': 3.215, 'L1_ffn_down_w': 3.028}
    for name, (base, spread) in spreads.items():
        noise = np.random.default_rng([zlib.crc32(name.encode()), seed]).standard_normal(out[name].shape)
        drawn = base * np.exp(spread * noise) if base else spread * noise
        out[name] = jnp.asarray(drawn.astype(out[name].dtype))
    for name, factor in factors.items():
        out[name] = (out[name] * factor).astype(out[name].dtype)
    return out
```

```python
from contextlib import ExitStack

import concourse.bass as bass
from concourse import mybir

F32 = mybir.dt.float32
F32R = mybir.dt.float32r
U32 = mybir.dt.uint32
ALU = mybir.AluOpType
ACT = mybir.ActivationFunctionType
AX = mybir.AxisListType

P = 128
B, S, D = 16, 100, 256
NTOK = B * S
SC = 361
H = 16
DC = D // P
DK0, DK1 = 64, D // H
N0 = H * DK0
CH0 = N0 // P
KT = 3
KR = (SC + KT - 1) // KT
CW = 364
CM = 362
E = 8
HID0, HID1 = 1024, 256
HC0, HC1 = HID0 // P, HID1 // P
TC = 400
NTC = NTOK // TC
BPC = TC // S
LN_EPS = 1e-5
NR = E + 4

BIAS_COLS = {}
_at = 0
for _name, _n in (("b1", E * HC0), ("bq0", CH0), ("bk0", CH0), ("bq1", DC), ("bk1", DC),
                  ("up_b", E * HC1), ("sh_up", HC1), ("sh_down", DC)):
    BIAS_COLS[_name] = (_at, _n)
    _at += _n
NBIAS = _at


def span(name):
    at, n = BIAS_COLS[name]
    return at, at + n


def wait(eng, sem, value):
    if isinstance(value, int) and value <= 0:
        return
    eng.wait_ge(sem, value)


def wait_apart(eng, *waits):
    waits = [(sem, v if isinstance(v, int) else eng.snap(eng.to_reg(v))) for sem, v in waits if not isinstance(v, int) or v > 0]
    if not all(isinstance(v, int) for _, v in waits):
        eng.wait_ge(waits[0][0], 1)
    for sem, value in waits:
        eng.wait_ge(sem, value)


def three_pass(pe, out, left, right, first, last):
    pe.matmul(out, left[0], right[0], start=first, stop=False)
    pe.matmul(out, left[0], right[1], start=False, stop=False)
    return pe.matmul(out, left[1], right[0], start=False, stop=last)


class Core:
    pass


def allocate_persistent(nc, ctx, t):
    def sb(name, shape, dt=F32):
        return ctx.enter_context(nc.sbuf_tensor(name, shape, dt))

    t.x = sb("x_rows", [S, B, D])
    t.xT = [sb(f"xnormT_{k}", [P, DC, NTOK], F32R) for k in ("hi", "lo")]
    t.ident = sb("identity", [P, P])
    t.bias = sb("bias_cols", [P, NBIAS])
    t.bq0s = sb("bq0_scaled", [P, CH0])
    t.bq1s = sb("bq1_scaled", [P, DC])
    t.gate_rows = sb("g_rows", [S, 4])
    t.tanh_g = sb("tanh_g", [S, 4])
    t.minus_half = sb("minus_half", [S, B])
    t.mv0 = sb("mean_var0", [S, B, 2])
    t.rstd0 = sb("rstd0", [S, B])
    t.xn = sb("xnorm_rows", [S, D])


def prepare(nc, t, dram):
    with ExitStack() as ctx:
        def sem(name):
            return ctx.enter_context(nc.semaphore(name))

        x_in, g_in, bias_in = sem("pre_x_loaded"), sem("pre_g_loaded"), sem("pre_bias_loaded")
        pool_own, dve_own, act_own = sem("pre_pool_own"), sem("pre_dve_own"), sem("pre_act_own")
        rstd_ready, xn_ready = sem("pre_rstd_ready"), sem("pre_xn_ready")
        turned, high_ready, low_ready = sem("pre_turned"), sem("pre_high"), sem("pre_low")
        stats_ready, ident_ready = sem("pre_stats_ready"), sem("pre_ident_ready")
        stats = ctx.enter_context(nc.sbuf_tensor("pre_stats", [S, B, 6], F32))
        var_eps = ctx.enter_context(nc.sbuf_tensor("pre_var_eps", [S, B], F32))
        xn = [ctx.enter_context(nc.sbuf_tensor(f"pre_xn{k}", [S, D], F32)) for k in range(4)]
        ps = [ctx.enter_context(nc.psum_tensor(f"pre_ps{k}", [P, DC, S], F32)) for k in range(4)]
        block = ctx.enter_context(nc.Block())

        @block.sync
        def _(sp):
            sp.dma_start(t.x[:], dram["x"].rearrange("b s d -> s b d")).then_inc(x_in, 16)
            sp.dma_start(t.gate_rows[:, 0:2], dram["g_xattn"].rearrange("(a g) -> a g", a=1)
                         .to_broadcast([S, 2])).then_inc(g_in, 16)
            sp.dma_start(t.gate_rows[:, 2:4], dram["g_ffn"].rearrange("(a g) -> a g", a=1)
                         .to_broadcast([S, 2])).then_inc(g_in, 16)
            sp.dma_start(t.bias[:], dram["bias_cols"]).then_inc(bias_in, 16)

        @block.gpsimd
        def _(pool):
            pool.memset(t.ident[:], 0.0).then_inc(pool_own, 1)
            pool.memset(t.minus_half[:], -0.5).then_inc(pool_own, 1)
            pool.wait_ge(pool_own, 2)
            pool.affine_select(out=t.ident[:], in_=t.ident[:], compare_op=ALU.not_equal, fill=1.0,
                               base=0, pattern=[[-1, P]], channel_multiplier=1).then_inc(ident_ready, 1)
            pool.wait_ge(stats_ready, 1)
            pool.tensor_scalar(var_eps[:], t.mv0[:, :, 1], LN_EPS, None, ALU.add).then_inc(pool_own, 1)
            pool.wait_ge(pool_own, 3)
            pool.tensor_tensor(t.rstd0[:], var_eps[:], t.minus_half[:], ALU.pow).then_inc(rstd_ready, 1)

        @block.scalar
        def _(act):
            act.wait_ge(g_in, 32)
            act.activation(t.tanh_g[:], t.gate_rows[:], ACT.Tanh).then_inc(act_own, 1)
            act.wait_ge(bias_in, 16)
            q0, n0 = BIAS_COLS["bq0"]
            q1, n1 = BIAS_COLS["bq1"]
            act.mul(t.bq0s[:], t.bias[:, q0:q0 + n0], DK0 ** -0.5).then_inc(act_own, 1)
            act.mul(t.bq1s[:], t.bias[:, q1:q1 + n1], -(DK1 ** -0.5)).then_inc(act_own, 1)
            for b in range(B):
                act.wait_ge(turned, b + 1)
                act.copy(t.xT[0][:, :, b * S:(b + 1) * S], ps[b % 4][:]).then_inc(high_ready, 1)

        @block.vector
        def _(dve):
            dve.wait_ge(x_in, 16)
            for b in range(B):
                dve.bn_stats(stats[:, b, :], t.x[:, b, :]).then_inc(dve_own, 1)
            for b in range(B):
                dve.wait_ge(dve_own, b + 1)
                ins = dve.bn_aggr(t.mv0[:, b, :], stats[:, b, :])
            ins.then_inc(stats_ready, 1)
            dve.wait_ge(rstd_ready, 1)
            dve.wait_ge(stats_ready, 1)
            for b in range(B + 2):
                if b < B:
                    if b >= 4:
                        dve.wait_ge(turned, b - 3)
                    dve.tensor_scalar(xn[b % 4][:], t.x[:, b, :], t.mv0[:, b, 0:1], t.rstd0[:, b:b + 1],
                                      ALU.subtract, ALU.mult).then_inc(xn_ready, 1)
                if b >= 2:
                    c = b - 2
                    dve.wait_ge(high_ready, c + 1)
                    cols = slice(c * S, (c + 1) * S)
                    dve.tensor_tensor(t.xT[1][:, :, cols], ps[c % 4][:], t.xT[0][:, :, cols].bitcast(F32),
                                      ALU.subtract).then_inc(low_ready, 1)

        @block.tensor
        def _(pe):
            pe.wait_ge(ident_ready, 1)
            for b in range(B):
                pe.wait_ge(xn_ready, b + 1)
                if b >= 4:
                    pe.wait_ge(low_ready, b - 3)
                for c in range(DC):
                    ins = pe.transpose(ps[b % 4][:, c, :], xn[b % 4][:, c * P:(c + 1) * P], t.ident[0:S, 0:S])
                ins.then_inc(turned, 1)


LAG_T, LAG_V = 2, 3
RING = 3
PAIRS = B // 2


class Job:

    def __init__(self, part, kind, batch, args, step):
        self.part, self.kind, self.batch, self.args, self.step = part, kind, batch, args, step


def side_jobs0(batch, h, odd):
    nxt, prev = batch + 1, batch - 1
    jobs = []
    if h == 0:
        jobs.append(("K", batch, (CH0 - 1,)))
        if not odd:
            jobs += [("Q", batch, (CH0 - 1, half)) for half in range(2)]
    if h >= 2 and h % 2 == 0:
        jobs.append(("K", nxt, (h // 2 - 1,)))
    if h in (3, 5, 7):
        jobs.append(("V", batch, (1, (h - 3) // 2)))
    if h in (11, 13, 15):
        jobs.append(("V", nxt, (0, (h - 11) // 2)))
    if h == 4:
        jobs.append(("OT", prev, (1,)))
    if h == 9:
        jobs.append(("OP", prev, ()))
    if h == 12:
        jobs.append(("OT", batch, (0,)))
    if h == 14:
        jobs.append(("XT", prev, ()))
    if odd and h >= 3 and h % 2 == 1:
        jobs.append(("Q", nxt, ((h - 3) // 2, None)))
    return jobs


def side_jobs1(batch, h, odd):
    nxt, prev = batch + 1, batch - 1
    jobs = []
    if h in (2, 4):
        jobs.append(("K", nxt, (h // 2 - 1,)))
    if h in (6, 7, 8):
        jobs.append(("V", nxt, (h - 6,)))
    if h == 5:
        jobs.append(("OT", prev, (0,)))
    if h == 9:
        jobs.append(("OP", prev, ()))
    if h == 15:
        jobs.append(("XT", prev, ()))
    if odd and h in (1, 3):
        jobs.append(("Q", nxt, (h // 2, None)))
    return jobs


PARTS = ("prologue", "first", "middle", "last", "tail")
PAIR_OF = {"prologue": 0, "first": 0, "last": PAIRS - 1, "tail": PAIRS}


class Plan:

    def __init__(self, side_jobs, prologue, act_kinds, dve_kinds):
        self.kinds = {"act": act_kinds, "dve": dve_kinds}
        self.jobs, count = [], {"all": 0, "act": 0, "dve": 0}
        for part in PARTS:
            if part == "last":
                for key in count:
                    count[key] += (PAIRS - 3) * self.per[key]
            before = dict(count)
            for where, (kind, batch, args) in self._listed(part, side_jobs, prologue):
                job = Job(part, kind, batch, args, where)
                job.n, job.n_act, job.n_dve = count["all"], count["act"], count["dve"]
                count["all"] += 1
                count["act"] += kind in act_kinds
                count["dve"] += kind in dve_kinds
                self.jobs.append(job)
            if part == "middle":
                self.per = {key: count[key] - before[key] for key in count}
                assert self.per["all"] % RING == 0

    @staticmethod
    def _listed(part, side_jobs, prologue):
        if part == "prologue":
            return [(None, j) for j in prologue]
        pair = 1 if part == "middle" else PAIR_OF[part]
        return [((local, h), j)
                for local in range(1 if part == "tail" else 2) for h in range(H)
                for j in side_jobs(local, h, local == 1) if 0 <= 2 * pair + j[1] < B]

    def of(self, part, where=None):
        return [j for j in self.jobs if j.part == part and (where is None or j.step == where)]

    def count(self, part, pair, job, who):
        n = {"act": job.n_act, "dve": job.n_dve}[who] + 1
        if part == "middle":
            return pair * self.per[who] + (n - self.per[who])
        return n + (PAIRS - 3) * self.per[who] if part in ("last", "tail") and job.part == "middle" else n

    def number(self, part, pair, job):
        return pair * self.per["all"] + (job.n + 1 - self.per["all"]) if part == "middle" else job.n + 1

    def before(self, job, far=RING):
        k = self.jobs.index(job) - far
        return self.jobs[k] if k >= 0 else None

    def latest(self, part, where, kind, *args):
        if isinstance(where, Job):
            known = self.jobs[:self.jobs.index(where)]
        else:
            known = [j for j in self.jobs if PARTS.index(j.part) < PARTS.index(part)
                     or j.part == part and j.step < where]
        return [j for j in known if j.kind == kind and j.args[:len(args)] == args][-1]


def attention(nc, t, dram, layer):
    L0 = layer == 0
    nch = CH0 if L0 else DC
    hpc = H // nch
    width = nch * P
    dv = DK0 if L0 else DK1
    vw = dv if L0 else dv + 1
    o_per = 2 if L0 else 1
    hpo = H // o_per
    n = f"a{layer}_"
    if L0:
        prologue = [("K", 0, (c,)) for c in range(nch - 1)] + [("Q", 0, (c, None)) for c in range(nch - 1)]
        prologue += [("V", 0, (0, k)) for k in range(KT)]
        plan = Plan(side_jobs0, prologue, ("K", "Q", "V", "OT", "XT"), ("K", "Q", "OT", "OP", "XT"))
    else:
        prologue = [("K", 0, (c,)) for c in range(nch)] + [("Q", 0, (c, None)) for c in range(nch)]
        prologue += [("V", 0, (k,)) for k in range(KT)]
        plan = Plan(side_jobs1, prologue, ("K", "Q", "V", "OT", "XT"), ("K", "OT", "OP", "XT"))

    with ExitStack() as ctx:
        def sb(name, shape, dt=F32):
            return ctx.enter_context(nc.sbuf_tensor(n + name, shape, dt))

        def ps(name):
            return ctx.enter_context(nc.psum_tensor(n + name, [P, 512], F32))

        def parts(name, shape):
            return [sb(f"{name}_{k}", shape, F32R) for k in ("hi", "lo")]

        def sem(name):
            return ctx.enter_context(nc.semaphore(n + name))

        wq, wk, wv = (parts(w, [P, DC, width]) for w in ("wq", "wk", "wv"))
        wo = parts("wo", [P, nch, D])
        stage = [sb(f"stage{k}", [P, 1024]) for k in range(2)]
        ctx_raw = sb("ctx_raw", [P, DC, SC])
        cT = [parts(f"ctxT{k}", [P, DC, CW]) for k in range(2)]
        two = 1 if L0 else 2
        kT = [parts(f"kT{k}", [P, nch, CM]) for k in range(two)]
        V = [sb(f"values{k}", [KR, KT, H, vw]) for k in range(two)]
        probs = [sb(f"probs{k}", [S, KT * KR]) for k in range(4)]
        pT = [sb(f"probsT{k}", [KR, KT, S]) for k in range(4)]
        minus_max = sb("minus_max", [S, 4])
        row_inv = sb("row_inv", [S, H])
        o_rows = sb("o_rows", [S, width])
        oT = parts("oT", [P, nch, S])
        bv_rows = sb("bv_rows", [S, width])
        bo_rows = sb("bo_rows", [S, D])
        stats = sb("bn_stats", [S, 2, 6])
        mv = sb("mean_var", [S, 2, 2])
        var_eps = sb("var_eps", [S, 2])
        rstd = sb("rstd", [S, 2])
        if L0:
            qT = parts("qT", [P, nch, 2 * S])
            row_sum = sb("row_sum", [S, 2, H])
            xn_bo = sb("xn_plus_bo", [S, D])
            y = xn_bo
            z = sb("z_rows", [S, D])
            gamma = sb("gamma_rows", [S, D])
            beta = sb("beta_rows", [S, D])
        else:
            y = sb("y_rows", [S, D])
            q_flat = sb("q_flat", [P, nch, 2 * S])
            q_part = parts("q_part", [P, nch, 2 * S])
            qm = [parts(f"q_masked{k}", [P, H, S]) for k in range(2)]
            head_mask = sb("head_mask", [P, hpc])
            mask_rows = [sb(f"mask_rows{k}", [S, SC]) for k in range(2)]
            mask_big = [sb(f"mask_big{k}", [S, SC]) for k in range(2)]
            logits = [sb(f"minus_logits{k}", [S, SC]) for k in range(2)]
        s_ps = [ps(f"ps_scores{k}") for k in range(2)]
        t_ps = [ps(f"ps_probsT{k}") for k in range(2)]
        o_ps = ps("ps_o")
        r_ps = [ps(f"ps_ring{k}") for k in range(RING)]

        stage_in = [sem(f"stage_in{k}") for k in range(2)]
        w_high, w_low = sem("weights_high"), sem("weights_low")
        rows_in, ctx_in = sem("rows_loaded"), sem("ctx_loaded")
        ctx_high, ctx_low = sem("ctx_high"), sem("ctx_low")
        pads = sem("pads_written")
        scores, neg_max, exped = sem("scores_done"), sem("max_ready"), sem("probs_ready")
        turned, av = sem("probs_turned"), sem("values_done")
        copied = [sem(f"probsT_copied{k}") for k in range(1 if L0 else 2)]
        o_inv, o_scaled, o_biased = sem("o_inverse"), sem("o_scaled"), sem("o_biased")
        job_done, job_act, job_dve = sem("job_done"), sem("job_act_read"), sem("job_dve_read")
        chain, pool_chain = sem("dve_chain"), sem("pool_chain")
        x_ready, x_stats, x_rstd, xn_ready = sem("x_ready"), sem("x_stats"), sem("x_rstd"), sem("xn_ready")
        if L0:
            scaled, base_norm, base_ready = sem("rows_scaled"), sem("base_norm"), sem("base_ready")
            y_stats, y_rstd, z_ready = sem("y_stats"), sem("y_rstd"), sem("z_ready")
        else:
            mask_in = [sem(f"mask_loaded{k}") for k in range(2)]
            mask_ready, q_high, q_parts, q_masked = (
                sem("mask_ready"), sem("q_high"), sem("q_parts"), sem("q_masked"))

        pre = "L0_xattn_" if L0 else "L1_xattn_"
        q_scale = DK0 ** -0.5 if L0 else -(DK1 ** -0.5)
        pieces = []
        for key, w, scale in (("k", wk, 1.0), ("q", wq, q_scale), ("v", wv, 1.0)):
            for c in range(DC):
                pieces.append((dram[pre + "W" + key][c * P:(c + 1) * P, :], [x[:, c, :] for x in w], width, scale))
        rows_o = dram[pre + "Wo"].rearrange("(c p) d -> p c d", p=P)
        for c in range(0, nch, 4):
            m = min(4, nch - c)
            pieces.append((rows_o[:, c:c + m, :], [x[:, c:c + m, :] for x in wo], m * D, 1.0))
        pieces_of = {"K": DC, "Q": 2 * DC, "V": 3 * DC, "OP": len(pieces)}

        def staged(k):
            m = pieces[k][2]
            v = stage[k % 2][:, 0:m]
            return v if len(pieces[k][1][0].shape) == 2 else v.rearrange("p (c d) -> p c d", d=D)

        def G(pair, local, h):
            return 2 * H * pair + H * local + h

        def copied_at(pair, local, h):
            if L0:
                return copied[0], G(pair, local, h) + 1
            k = H * local + h
            return copied[k % 2], H * pair + k // 2 + 1

        def walk(eng, part):
            part("prologue", 0)
            part("first", 0)
            with eng.Fori(1, PAIRS - 1) as i:
                part("middle", i)
            part("last", PAIRS - 1)
            part("tail", PAIRS)

        def steps(name):
            if name == "prologue":
                return []
            return [(local, h) for local in range(1 if name == "tail" else 2) for h in range(H)]

        def lagged(name, local, h, lag):
            k = H * local + h - lag
            if name == "first" and k < 0 or name == "tail" and k >= 0:
                return None
            return (k // H, k % H)

        def xcols(b, m=S):
            return slice(b * S, b * S + m) if isinstance(b, int) else bass.ds(b * S, m)

        def brow(b):
            return t.x[:, b, :] if isinstance(b, int) else t.x[:, bass.ds(b, 1), :].rearrange("s a d -> s (a d)")

        def prev_of(name, pair, local):
            return None if name == "first" and local == 0 else 2 * pair + local - 1

        n_pads = 2 * 2 + 4 + (0 if L0 else 2)
        block = ctx.enter_context(nc.Block())

        @block.sync
        def _(sp):
            def load_context(b):
                wait(sp, ctx_high, b)
                wait(sp, ctx_low, b)
                src = dram["ctxT"][b] if isinstance(b, int) else \
                    dram["ctxT"][bass.ds(b, 1)].rearrange("a d s -> (a d) s")
                sp.dma_start(ctx_raw[:], src.rearrange("(c p) s -> p c s", p=P)).then_inc(ctx_in, 16)

            def load_mask(b, k):
                wait(sp, mask_ready, b - 1)
                src = dram["mask"][b:b + 1, :] if isinstance(b, int) else dram["mask"][bass.ds(b, 1), :]
                sp.dma_start(mask_rows[k][:], src.to_broadcast([S, SC])).then_inc(mask_in[k], 16)

            load_context(0)
            for k, piece in enumerate(pieces):
                if k >= 2:
                    sp.wait_ge(w_high, k - 1)
                    sp.wait_ge(w_low, k - 1)
                sp.dma_start(staged(k), piece[0]).then_inc(stage_in[k % 2], 16)
            sp.dma_start(bv_rows[:], dram[pre + "bv"].to_broadcast([S, width])).then_inc(rows_in, 16)
            sp.dma_start(bo_rows[:], dram[pre + "bo"].to_broadcast([S, D])).then_inc(rows_in, 16)
            if L0:
                sp.dma_start(gamma[:], dram["L0_xattn_ln_gamma"].to_broadcast([S, D])).then_inc(rows_in, 16)
                sp.dma_start(beta[:], dram["L0_xattn_ln_beta"].to_broadcast([S, D])).then_inc(rows_in, 16)
            load_context(1)
            if not L0:
                load_mask(0, 0)
                load_mask(1, 1)
            with sp.Fori(1, PAIRS) as i:
                for k in range(2):
                    load_context(2 * i + k)
                    if not L0:
                        load_mask(2 * i + k, k)

        @block.tensor
        def _(pe):
            def job(name, pair, j):
                b = 2 * pair + j.batch
                bank, old = r_ps[j.n % RING], plan.before(j)
                if old is not None:
                    who = "dve" if old.kind in plan.kinds["dve"] else "act"
                    pe.wait_ge({"act": job_act, "dve": job_dve}[who], plan.count(name, pair, old, who))
                if name == "prologue" or j.kind == "OP":
                    pe.wait_ge(w_low, pieces_of[j.kind])
                c_parts = cT[j.batch % 2]
                if j.kind in "KV":
                    pe.wait_ge(ctx_low, b + 1)
                if j.kind == "K":
                    (c,) = j.args
                    for d in range(DC):
                        ins = three_pass(pe, bank[:, 0:CM], [w[:, d, c * P:(c + 1) * P] for w in wk],
                                         [x[:, d, 0:CM] for x in c_parts], d == 0, d == DC - 1)
                elif j.kind == "V":
                    k = j.args[-1]
                    at, m = (j.args[0] * 512, 512) if L0 else (0, width)
                    for d in range(DC):
                        ins = three_pass(pe, bank[0:KR, 0:m], [x[:, d, k * KR:(k + 1) * KR] for x in c_parts],
                                         [w[:, d, at:at + m] for w in wv], d == 0, d == DC - 1)
                elif j.kind == "Q":
                    c, half = j.args
                    m = 2 * S if half is None else S
                    cols = xcols(b + (half or 0), m)
                    for d in range(DC):
                        ins = three_pass(pe, bank[:, 0:m], [w[:, d, c * P:(c + 1) * P] for w in wq],
                                         [x[:, d, cols] for x in t.xT], d == 0, d == DC - 1)
                elif j.kind == "OT":
                    c0, m = (4 * j.args[0], 4) if L0 else (0, DC)
                    pe.wait_ge(o_biased, o_per * b + j.args[0] + 1)
                    for c in range(m):
                        ins = pe.transpose(bank[:, c * S:(c + 1) * S],
                                           o_rows[:, (c0 + c) * P:(c0 + c + 1) * P], t.ident[0:S, 0:S])
                elif j.kind == "OP":
                    ot = plan.latest(name, j, "OT", 1 if L0 else 0)
                    pe.wait_ge(job_dve, plan.count(name, pair, ot, "dve"))
                    if L0:
                        first_half = plan.latest(name, j, "OT", 0)
                        pe.wait_ge(job_dve, plan.count(name, pair, first_half, "dve"))
                    for c in range(nch):
                        ins = three_pass(pe, bank[0:S, 0:D], [o[:, c, :] for o in oT],
                                         [w[:, c, :] for w in wo], c == 0, c == nch - 1)
                elif j.kind == "XT":
                    pe.wait_ge(xn_ready, b + 1)
                    for c in range(DC):
                        ins = pe.transpose(bank[:, c * S:(c + 1) * S], t.xn[:, c * P:(c + 1) * P],
                                           t.ident[0:S, 0:S])
                ins.then_inc(job_done, 1)

            def scores_of(name, pair, local, h):
                c, g = h // hpc, G(pair, local, h)
                if h % hpc == 0:
                    k_job = plan.latest(name, (local, h), "K", c)
                    pe.wait_ge(job_dve, plan.count(name, pair, k_job, "dve"))
                    if L0:
                        q_job = plan.latest(name, (local, h), "Q", c)
                        pe.wait_ge(job_dve, plan.count(name, pair, q_job, "dve"))
                    else:
                        pe.wait_ge(q_masked, 2 * nch * pair + nch * local + c + 1)
                wait(pe, exped if L0 else neg_max, g - 1)
                if L0:
                    rows = slice(DK0 * (h % hpc), DK0 * (h % hpc + 1))
                    q = [x[rows, c, local * S:(local + 1) * S] for x in qT]
                    k = [x[rows, c, :] for x in kT[0]]
                else:
                    q = [x[:, h, :] for x in qm[local]]
                    k = [x[:, c, :] for x in kT[local]]
                three_pass(pe, s_ps[h % 2][0:S, 0:CM], q, k, True, True).then_inc(scores, 1)

            def turn(name, pair, local, h):
                pe.wait_ge(exped, G(pair, local, h) + 1)
                back = lagged(name, local, h, 2)
                if back is not None:
                    pe.wait_ge(*copied_at(pair, *back))
                for k in range(KT):
                    ins = pe.transpose(t_ps[h % 2][0:KR, k * S:(k + 1) * S],
                                       probs[h % 4][:, k * KR:(k + 1) * KR], t.ident[0:S, 0:S])
                ins.then_inc(turned, 1)

            def values(name, pair, local, h):
                pe.wait_ge(*copied_at(pair, local, h))
                if h % hpo == 0:
                    wait(pe, o_scaled, o_per * (2 * pair + local) + h // hpo)
                if h == 0 or L0 and h == 8:
                    v_job = plan.latest(name, (local, h), "V", *((h // 8, KT - 1) if L0 else (KT - 1,)))
                    pe.wait_ge(job_act, plan.count(name, pair, v_job, "act"))
                v = V[0] if L0 else V[local % 2]
                at = (h % hpo) * vw
                for k in range(KT):
                    ins = pe.matmul(o_ps[0:S, at:at + vw], pT[h % 4][:, k, :], v[:, k, h, :],
                                    start=k == 0, stop=k == KT - 1)
                ins.then_inc(av, 1)

            pe.wait_ge(pads, n_pads)

            def part(name, pair):
                for j in plan.of(name) if name == "prologue" else ():
                    job(name, pair, j)
                for local, h in steps(name):
                    if name != "tail":
                        scores_of(name, pair, local, h)
                    for j in plan.of(name, (local, h)):
                        job(name, pair, j)
                    if (back := lagged(name, local, h, LAG_T)) is not None:
                        turn(name, pair, *back)
                    if (back := lagged(name, local, h, LAG_V)) is not None:
                        values(name, pair, *back)

            walk(pe, part)

        @block.gpsimd
        def _(pool):
            for k in range(2):
                for x in cT[k]:
                    pool.memset(x[:, :, SC:CW].bitcast(F32), 0.0).then_inc(pads, 1)
            for k in range(4):
                pool.memset(probs[k][:, SC:KT * KR], 0.0).then_inc(pads, 1)
            if not L0:
                for v in V:
                    pool.memset(v[:, :, :, dv:vw], 1.0).then_inc(pads, 1)
                pool.memset(head_mask[:], 1.0).then_inc(pool_chain, 1)
                pool.wait_ge(pool_chain, 1)
                pool.affine_select(out=head_mask[:], in_=head_mask[:], compare_op=ALU.is_ge, fill=0.0, base=0,
                                   pattern=[[-dv, hpc]], channel_multiplier=1).then_inc(pool_chain, 1)
                pool.wait_ge(pool_chain, 2)
                pool.affine_select(out=head_mask[:], in_=head_mask[:], compare_op=ALU.is_ge, fill=0.0,
                                   base=dv - 1, pattern=[[dv, hpc]], channel_multiplier=-1).then_inc(pool_chain, 1)
                pool.wait_ge(pool_chain, 3)
            pool.wait_ge(rows_in, 64 if L0 else 32)
            if L0:
                pool.tensor_scalar(gamma[:], gamma[:], t.tanh_g[:, 0:1], None, ALU.mult).then_inc(scaled, 1)
                pool.tensor_scalar(beta[:], beta[:], t.tanh_g[:, 0:1], None, ALU.mult).then_inc(scaled, 1)
                pool.wait_ge(scaled, 2)
            base = 0 if L0 else 3

            def split_low(b, k):
                pool.wait_ge(ctx_high, b + 1)
                pool.tensor_tensor(cT[k][1][:, :, 0:SC], ctx_raw[:], cT[k][0][:, :, 0:SC].bitcast(F32),
                                   ALU.subtract).then_inc(ctx_low, 1)

            def inverse_root(k, stats_sem, out_sem, b, links):
                wait_apart(pool, (stats_sem, b + 1))
                pool.tensor_scalar(var_eps[:, k:k + 1], mv[:, k, 1:2], LN_EPS, None, ALU.add).then_inc(pool_chain, 1)
                pool.wait_ge(pool_chain, links + 1)
                pool.tensor_tensor(rstd[:, k:k + 1], var_eps[:, k:k + 1], t.minus_half[:, 0:1],
                                   ALU.pow).then_inc(out_sem, 1)

            def add_bv(pair, local, half):
                cols = slice(half * 512, half * 512 + 512) if L0 else slice(0, width)
                pool.wait_ge(o_scaled, o_per * (2 * pair + local) + half + 1)
                pool.tensor_tensor(o_rows[:, cols], o_rows[:, cols], bv_rows[:, cols], ALU.add).then_inc(o_biased, 1)

            def mask_queries(pair, local):
                for c in range(nch):
                    pool.wait_ge(q_parts, nch * pair + c + 1)
                    wait(pool, scores, G(pair, local, 0) - H)
                    for k in range(2):
                        src = q_part[k][:, c, local * S:(local + 1) * S].bitcast(F32)
                        ins = pool.tensor_tensor(
                            qm[local][k][:, c * hpc:(c + 1) * hpc, :],
                            src[:, None, :].to_broadcast([P, hpc, S]),
                            head_mask[:, :, None].to_broadcast([P, hpc, S]), ALU.mult)
                    ins.then_inc(q_masked, 1)

            def enlarge_mask(b, k, loads):
                wait_apart(pool, (mask_in[k], 16 * loads), (neg_max, H * (b - 1)))
                pool.tensor_scalar(mask_big[k][:], mask_rows[k][:], 1e9, None, ALU.mult).then_inc(mask_ready, 1)

            def part(name, pair):
                if name == "prologue":
                    split_low(0, 0)
                    split_low(1, 1)
                    if not L0:
                        enlarge_mask(0, 0, 1)
                        mask_queries(0, 0)
                        mask_queries(0, 1)
                    return
                for local, h in steps(name):
                    b = 2 * pair + local
                    p = prev_of(name, pair, local)
                    if h == (3 if L0 else 3) and p is not None:
                        add_bv(pair, local - 1, o_per - 1)
                    if L0 and h == 6 and p is not None:
                        pool.wait_ge(base_norm, p + 1)
                        pool.tensor_tensor(xn_bo[:], xn_bo[:], bo_rows[:], ALU.add).then_inc(base_ready, 1)
                    if L0 and h == 10 and p is not None:
                        inverse_root(0, y_stats, y_rstd, p, base + 4 * p)
                    if L0 and h == 11 and name != "tail":
                        add_bv(pair, local, 0)
                    if L0 and h == 11 and p is not None:
                        pool.wait_ge(z_ready, p + 1)
                        pool.tensor_tensor(z[:], z[:], gamma[:], ALU.mult).then_inc(pool_chain, 1)
                        pool.wait_ge(pool_chain, base + 4 * p + 2)
                        pool.tensor_tensor(z[:], z[:], beta[:], ALU.add).then_inc(pool_chain, 1)
                        pool.wait_ge(pool_chain, base + 4 * p + 3)
                        pool.tensor_tensor(brow(p), brow(p), z[:], ALU.add).then_inc(x_ready, 1)
                    if h == (12 if L0 else 11) and p is not None:
                        inverse_root(1, x_stats, x_rstd, p, base + 4 * p + 3 if L0 else base + p)
                    if name != "tail" and not L0:
                        if h == 5 and local == 1 and name != "last":
                            mask_queries(pair + 1, 0)
                        if h == 5 and local == 0 and name != "first":
                            mask_queries(pair, 1)
                        if h == 8 and not (name == "last" and local == 1):
                            enlarge_mask(b + 1, 1 - local, pair + 1 + local)
                    if h == 14 and name not in ("last", "tail"):
                        split_low(b + 2, local)

            walk(pool, part)

        @block.scalar
        def _(act):
            for k, (_src, w, _m, scale) in enumerate(pieces):
                act.wait_ge(stage_in[k % 2], 16 * (k // 2 + 1))
                act.mul(w[0], staged(k), scale).then_inc(w_high, 1)
            biases = {"K": t.bias[:, slice(*span(f"bk{layer}"))], "Q": t.bq0s if L0 else t.bq1s}

            def split_high(b, k):
                act.wait_ge(ctx_in, 16 * (b + 1))
                if not isinstance(b, int) or b >= 2:
                    act.wait_ge(scores, H * (b - 2) + 9)
                act.copy(cT[k][0][:, :, 0:SC], ctx_raw[:]).then_inc(ctx_high, 1)

            def probabilities(name, pair, local, h):
                g = G(pair, local, h)
                act.wait_ge(neg_max, g + 1)
                wait(act, turned, g - 3)
                if L0:
                    act.activation(probs[h % 4][:, 0:SC], s_ps[h % 2][0:S, 0:SC], ACT.Exp,
                                   bias=minus_max[:, h % 4:h % 4 + 1],
                                   accum_out=row_sum[:, local, h:h + 1]).then_inc(exped, 1)
                else:
                    act.activation(probs[h % 4][:, 0:SC], logits[h % 2][:], ACT.Exp,
                                   bias=minus_max[:, h % 4:h % 4 + 1], scale=-1.0).then_inc(exped, 1)

            def copy_turned(pair, local, h):
                g = G(pair, local, h)
                act.wait_ge(turned, g + 1)
                wait(act, av, g - 3)
                act.copy(pT[h % 4][:], t_ps[h % 2][0:KR, 0:KT * S].rearrange("k (t s) -> k t s", s=S))\
                   .then_inc(copied[1], 1)

            def read(name, pair, j):
                b = 2 * pair + j.batch
                if j.kind not in plan.kinds["act"]:
                    return
                bank = r_ps[j.n % RING]
                act.wait_ge(job_done, plan.number(name, pair, j))
                if j.kind == "K":
                    (c,) = j.args
                    ins = act.activation(kT[0 if L0 else j.batch % 2][0][:, c, :], bank[:, 0:CM], ACT.Identity,
                                         bias=biases["K"][:, c:c + 1])
                elif j.kind == "Q":
                    c, half = j.args
                    m = 2 * S if half is None else S
                    at = S * (half or 0)
                    if not L0:
                        wait(act, q_parts, nch * (pair + int(j.batch == 2) - 1) + c + 1)
                    to = (qT[0] if L0 else q_flat)[:, c, at:at + m]
                    ins = act.activation(to, bank[:, 0:m], ACT.Identity, bias=biases["Q"][:, c:c + 1])
                elif j.kind == "V":
                    k = j.args[-1]
                    h0, m = (8 * j.args[0], 8) if L0 else (0, H)
                    ins = act.copy(V[0 if L0 else j.batch % 2][:, k, h0:h0 + m, 0:dv],
                                   bank[0:KR, 0:m * dv].rearrange("k (h v) -> k h v", v=dv))
                elif j.kind == "OT":
                    c0, m = (4 * j.args[0], 4) if L0 else (0, DC)
                    ins = act.copy(oT[0][:, c0:c0 + m, :], bank[:, 0:m * S].rearrange("p (c s) -> p c s", s=S))
                elif j.kind == "XT":
                    ins = act.copy(t.xT[0][:, :, xcols(b)], bank[:, 0:DC * S].rearrange("p (c s) -> p c s", s=S))
                ins.then_inc(job_act, 1)

            def part(name, pair):
                if name == "prologue":
                    split_high(0, 0)
                    split_high(1, 1)
                    for j in plan.of(name):
                        read(name, pair, j)
                    return
                for local, h in steps(name):
                    back = lagged(name, local, h, LAG_V)
                    if not L0 and back is not None and back[1] % 2:
                        copy_turned(pair, *back)
                    if name != "tail":
                        probabilities(name, pair, local, h)
                    for j in plan.of(name, (local, h)):
                        read(name, pair, j)
                    if h == 14 and name not in ("last", "tail"):
                        split_high(2 * pair + local + 2, local)

            walk(act, part)

        @block.vector
        def _(dve):
            for k, (_src, w, _m, scale) in enumerate(pieces):
                dve.wait_ge(w_high, k + 1)
                dve.scalar_tensor_tensor(out=w[1], in0=staged(k), scalar=scale, in1=w[0].bitcast(F32),
                                         op0=ALU.mult, op1=ALU.subtract).then_inc(w_low, 1)
            biases = {"K": t.bias[:, slice(*span(f"bk{layer}"))], "Q": t.bq0s if L0 else t.bq1s}
            CH = 2 if L0 else 1

            def link(ins, b, k):
                ins.then_inc(chain, 1)
                wait_apart(dve, (chain, CH * b + k + 1))

            def maximum(name, pair, local, h):
                g = G(pair, local, h)
                if L0:
                    dve.wait_ge(scores, g + 1)
                    wait(dve, exped, g - 3)
                    ins = dve.tensor_reduce(minus_max[:, h % 4:h % 4 + 1], s_ps[h % 2][0:S, 0:SC], AX.X, ALU.max,
                                            negate=True)
                else:
                    wait_apart(dve, (scores, g + 1), (exped, g - 1),
                               *([(mask_ready, 2 * pair + local + 1)] if h == 0 else []))
                    ins = dve.tensor_tensor_reduce(logits[h % 2][:], s_ps[h % 2][0:S, 0:SC], mask_big[local][:],
                                                   1.0, 3.0e38, ALU.add, ALU.min, minus_max[:, h % 4:h % 4 + 1])
                ins.then_inc(neg_max, 1)

            def copy_turned(pair, local, h):
                g = G(pair, local, h)
                dve.wait_ge(turned, g + 1)
                wait(dve, av, g - 3)
                dve.tensor_copy(pT[h % 4][:], t_ps[h % 2][0:KR, 0:KT * S].rearrange("k (t s) -> k t s", s=S))\
                   .then_inc(copied[0], 1)

            def scale_o(pair, local, half):
                m, b = hpo, 2 * pair + local
                dve.wait_ge(av, H * b + hpo * (half + 1))
                wait(dve, o_scaled, o_per * b + half)
                o = o_ps[0:S, 0:m * vw].rearrange("s (h v) -> s h v", v=vw)
                sums = row_sum[:, local % 2, half * m:(half + 1) * m] if L0 else o[:, :, dv]
                dve.reciprocal(row_inv[:, 0:m], sums).then_inc(o_inv, 1)
                dve.wait_ge(o_inv, o_per * b + half + 1)
                to = o_rows[:, half * m * dv:(half + 1) * m * dv].rearrange("s (h v) -> s h v", v=dv)
                dve.tensor_tensor(to, o[:, :, 0:dv], row_inv[:, 0:m, None].to_broadcast([S, m, dv]),
                                  ALU.mult).then_inc(o_scaled, 1)

            def read(name, pair, j):
                b = 2 * pair + j.batch
                bank = r_ps[j.n % RING]
                if j.kind == "Q" and not L0:
                    c = j.args[0]
                    k = nch * (pair + int(j.batch == 2)) + c
                    dve.wait_ge(job_act, plan.count(name, pair, j, "act"))
                    wait(dve, q_masked, 2 * nch * (pair + int(j.batch == 2)))
                    dve.tensor_copy(q_part[0][:, c, :], q_flat[:, c, :]).then_inc(q_high, 1)
                    dve.wait_ge(q_high, k + 1)
                    dve.tensor_tensor(q_part[1][:, c, :], q_flat[:, c, :], q_part[0][:, c, :].bitcast(F32),
                                      ALU.subtract).then_inc(q_parts, 1)
                    return
                if j.kind not in plan.kinds["dve"]:
                    return
                if j.kind == "OP":
                    dve.wait_ge(job_done, plan.number(name, pair, j))
                else:
                    dve.wait_ge(job_act, plan.count(name, pair, j, "act"))
                if j.kind == "K":
                    (c,) = j.args
                    k = kT[0 if L0 else j.batch % 2]
                    ins = dve.scalar_tensor_tensor(out=k[1][:, c, :], in0=bank[:, 0:CM],
                                                   scalar=biases["K"][:, c:c + 1], in1=k[0][:, c, :].bitcast(F32),
                                                   op0=ALU.add, op1=ALU.subtract)
                elif j.kind == "Q":
                    c, half = j.args
                    m = 2 * S if half is None else S
                    at = S * (half or 0)
                    ins = dve.scalar_tensor_tensor(out=qT[1][:, c, at:at + m], in0=bank[:, 0:m],
                                                   scalar=biases["Q"][:, c:c + 1],
                                                   in1=qT[0][:, c, at:at + m].bitcast(F32),
                                                   op0=ALU.add, op1=ALU.subtract)
                elif j.kind == "OT":
                    c0, m = (4 * j.args[0], 4) if L0 else (0, DC)
                    ins = dve.tensor_tensor(oT[1][:, c0:c0 + m, :],
                                            bank[:, 0:m * S].rearrange("p (c s) -> p c s", s=S),
                                            oT[0][:, c0:c0 + m, :].bitcast(F32), ALU.subtract)
                elif j.kind == "OP":
                    if L0:
                        dve.wait_ge(base_ready, b + 1)
                    ins = dve.tensor_tensor(y[:], bank[0:S, 0:D], (xn_bo if L0 else bo_rows)[:], ALU.add)
                    ins.then_inc(job_dve, 1)
                    dve.wait_ge(job_dve, plan.count(name, pair, j, "dve"))
                    if not L0:
                        dve.scalar_tensor_tensor(out=brow(b), in0=y[:], scalar=t.tanh_g[:, 1:2], in1=brow(b),
                                                 op0=ALU.mult, op1=ALU.add).then_inc(x_ready, 1)
                    return
                elif j.kind == "XT":
                    ins = dve.tensor_tensor(t.xT[1][:, :, xcols(b)],
                                            bank[:, 0:DC * S].rearrange("p (c s) -> p c s", s=S),
                                            t.xT[0][:, :, xcols(b)].bitcast(F32), ALU.subtract)
                ins.then_inc(job_dve, 1)

            def mean_var(k, rows, b, at, out):
                link(dve.bn_stats(stats[:, k, :], rows), b, at)
                dve.bn_aggr(mv[:, k, :], stats[:, k, :]).then_inc(out, 1)

            def part(name, pair):
                if name == "prologue":
                    dve.wait_ge(rows_in, 64 if L0 else 32)
                    for j in plan.of(name):
                        read(name, pair, j)
                    return
                for local, h in steps(name):
                    p = prev_of(name, pair, local)
                    back = lagged(name, local, h, LAG_V)
                    if back is not None and (L0 or back[1] % 2 == 0):
                        copy_turned(pair, *back)
                    if (back := lagged(name, local, h, LAG_V + 1)) is not None and back[1] % hpo == hpo - 1:
                        scale_o(pair, back[0], back[1] // hpo)
                    if name != "tail":
                        maximum(name, pair, local, h)
                    if p is not None:
                        if L0 and h == 5:
                            m = t.mv0[:, p, 0:1] if isinstance(p, int) else \
                                t.mv0[:, bass.ds(p, 1), 0:1].rearrange("s a c -> s (a c)")
                            r = t.rstd0[:, p:p + 1] if isinstance(p, int) else t.rstd0[:, bass.ds(p, 1)]
                            dve.tensor_scalar(xn_bo[:], brow(p), m, r, ALU.subtract, ALU.mult)\
                               .then_inc(base_norm, 1)
                        if L0 and h == 10:
                            mean_var(0, y[:], p, 0, y_stats)
                        if L0 and h == 11:
                            dve.wait_ge(y_rstd, p + 1)
                            dve.tensor_scalar(z[:], y[:], mv[:, 0, 0:1], rstd[:, 0:1], ALU.subtract, ALU.mult)\
                               .then_inc(z_ready, 1)
                        if h == (12 if L0 else 11):
                            wait_apart(dve, (x_ready, p + 1))
                            mean_var(1, brow(p), p, 1 if L0 else 0, x_stats)
                        if h == 13:
                            dve.wait_ge(x_rstd, p + 1)
                            dve.tensor_scalar(t.xn[:], brow(p), mv[:, 1, 0:1], rstd[:, 1:2],
                                              ALU.subtract, ALU.mult).then_inc(xn_ready, 1)
                    for j in plan.of(name, (local, h)):
                        read(name, pair, j)

            walk(dve, part)


def router(nc, t, dram, layer):
    L0 = layer == 0
    nr = NR if L0 else E
    n = f"r{layer}_"
    with ExitStack() as ctx:
        def sb(name, shape, dt=F32):
            return ctx.enter_context(nc.sbuf_tensor(n + name, shape, dt))

        def sem(name):
            return ctx.enter_context(nc.semaphore(n + name))

        w_raw = sb("w_raw", [P, DC, nr])
        w = [sb(f"w_{k}", [P, DC, nr], F32R) for k in ("hi", "lo")]
        bias = sb("bias_rows", [S, nr])
        logit = sb("logit", [S, B, nr])
        prob = sb("prob", [S, B, E])
        lang = sb("lang", [S, B, 4])
        mix = sb("mix", [S, B, 4])
        one = sb("one_per_token", [S, B])
        inv = sb("inverse", [S, B])
        top = sb("top8", [S, B, E])
        index = sb("index", [S, B, E], U32)
        index_f = sb("index_f", [S, B, 2])
        iota = sb("iota", [S, E])
        hit = sb("hit", [S, B, E])
        hit2 = sb("hit2", [S, B, E])
        gates = sb("gates", [S, B, E])
        lg_ps = ctx.enter_context(nc.psum_tensor(n + "ps_logit", [S, B, nr], F32))
        g_ps = [ctx.enter_context(nc.psum_tensor(f"{n}ps_gates{k}", [E, TC], F32)) for k in range(NTC)]
        w_in, w_split, logit_done, chain = sem("w_loaded"), sem("w_split"), sem("logit_done"), sem("dve_chain")
        ask_exp, exp_done, gates_turned, gates_out = (
            sem("ask_exp"), sem("exp_done"), sem("gates_turned"), sem("gates_stored"))
        gates_ready, gatesT_ready = sem("gates_ready"), sem("gatesT_ready")
        block = ctx.enter_context(nc.Block())

        @block.sync
        def _(sp):
            sp.dma_start(w_raw[:], dram[f"router{layer}"].rearrange("(c p) e -> p c e", p=P)).then_inc(w_in, 16)
            if L0:
                sp.dma_start(bias[:], dram["router_bias"].to_broadcast([S, nr])).then_inc(w_in, 16)
            sp.wait_ge(gatesT_ready, NTC)
            sp.dma_start(dram["gates"], t.gatesT[:]).then_inc(gates_out, 16)
            sp.wait_ge(gates_out, 16)

        @block.scalar
        def _(act):
            if L0:
                act.wait_ge(ask_exp, 1)
                act.activation(lang[:], lang[:], ACT.Exp).then_inc(exp_done, 1)
            act.wait_ge(ask_exp, 2 if L0 else 1)
            act.activation(prob[:], prob[:], ACT.Exp).then_inc(exp_done, 1)

        @block.tensor
        def _(pe):
            pe.wait_ge(w_split, 2)
            for b in range(B):
                for c in range(DC):
                    ins = three_pass(pe, lg_ps[:, b, :], [x[:, c, b * S:(b + 1) * S] for x in t.xT],
                                     [x[:, c, :] for x in w], c == 0, c == DC - 1)
            ins.then_inc(logit_done, 1)
            pe.wait_ge(gates_ready, 1)
            for k in range(NTC):
                for j in range(BPC):
                    ins = pe.transpose(g_ps[k][:, j * S:(j + 1) * S], gates[:, BPC * k + j, :], t.ident[0:S, 0:S])
                ins.then_inc(gates_turned, 1)

        @block.vector
        def _(dve):
            done = [0]

            def link(ins):
                ins.then_inc(chain, 1)
                done[0] += 1
                dve.wait_ge(chain, done[0])

            def per_token(x, m):
                return x[:, :, None].to_broadcast([S, B, m])

            def softmax_start(to, x, m):
                link(dve.tensor_reduce(one[:], x, AX.X, ALU.max))
                dve.tensor_tensor(to, x, per_token(one, m), ALU.subtract).then_inc(ask_exp, 1)

            def softmax_end(x, m):
                link(dve.tensor_reduce(one[:], x, AX.X, ALU.add))
                link(dve.reciprocal(inv[:], one[:]))
                link(dve.tensor_tensor(x, x, per_token(inv, m), ALU.mult))

            for e in range(E):
                link(dve.memset(iota[:, e:e + 1], float(e)))
            dve.wait_ge(w_in, 32 if L0 else 16)
            dve.tensor_copy(w[0][:], w_raw[:]).then_inc(w_split, 1)
            dve.wait_ge(w_split, 1)
            dve.tensor_tensor(w[1][:], w_raw[:], w[0][:].bitcast(F32), ALU.subtract).then_inc(w_split, 1)
            dve.wait_ge(logit_done, 1)
            if L0:
                link(dve.tensor_tensor(logit[:], lg_ps[:], bias[:, None, :].to_broadcast([S, B, nr]), ALU.add))
                softmax_start(lang[:], logit[:, :, E:NR], 4)
                dve.wait_ge(exp_done, 1)
                softmax_end(lang[:], 4)
                link(dve.tensor_tensor(mix[:, :, 0:3], lang[:, :, 0:3], lang[:, :, 1:4], ALU.add))
                link(dve.tensor_copy(mix[:, :, 3:4], lang[:, :, 3:4]))
                for k in range(0, E, 4):
                    link(dve.scalar_tensor_tensor(out=logit[:, :, k:k + 4], in0=mix[:], scalar=0.1,
                                                  in1=logit[:, :, k:k + 4], op0=ALU.mult, op1=ALU.add))
            else:
                link(dve.tensor_copy(logit[:], lg_ps[:]))
            softmax_start(prob[:], logit[:, :, 0:E], E)
            dve.wait_ge(exp_done, 2 if L0 else 1)
            softmax_end(prob[:], E)
            for b in range(B):
                link(dve.max(top[:, b, :], prob[:, b, :]))
                link(dve.max_index(index[:, b, :], top[:, b, :], prob[:, b, :]))
            link(dve.tensor_copy(index_f[:], index[:, :, 0:2]))
            link(dve.tensor_tensor(one[:], top[:, :, 0], top[:, :, 1], ALU.add))
            if not L0:
                link(dve.tensor_scalar(one[:], one[:], 1e-20, None, ALU.add))
            link(dve.reciprocal(inv[:], one[:]))
            link(dve.tensor_tensor(top[:, :, 0:2], top[:, :, 0:2], per_token(inv, 2), ALU.mult))
            for k, x in enumerate((hit, hit2)):
                link(dve.tensor_tensor(x[:], iota[:, None, :].to_broadcast([S, B, E]),
                                       per_token(index_f[:, :, k], E), ALU.is_equal))
                link(dve.tensor_tensor(x[:], x[:], per_token(top[:, :, k], E), ALU.mult))
            dve.tensor_tensor(gates[:], hit[:], hit2[:], ALU.add).then_inc(gates_ready, 1)
            for k in range(NTC):
                dve.wait_ge(gates_turned, k + 1)
                dve.tensor_copy(t.gatesT[:, k * TC:(k + 1) * TC], g_ps[k][:]).then_inc(gatesT_ready, 1)


LAG_Y = 2


def experts0(nc, t, dram):
    STEPS = NTC * HC0
    n = "e0_"
    with ExitStack() as ctx:
        def sb(name, shape, dt=F32):
            return ctx.enter_context(nc.sbuf_tensor(n + name, shape, dt))

        def ps(name):
            return ctx.enter_context(nc.psum_tensor(n + name, [P, 512], F32))

        def sem(name):
            return ctx.enter_context(nc.semaphore(n + name))

        w1 = [[sb(f"w1_{k}{p}", [P, DC, HID0], F32R) for p in ("hi", "lo")] for k in range(2)]
        w2 = [[sb(f"w2_{k}{p}", [P, HC0, D], F32R) for p in ("hi", "lo")] for k in range(2)]
        raw = [sb(f"w_raw{k}", [P, 1024]) for k in range(4)]
        b2 = sb("b2_rows", [E, D])
        gate = [sb(f"gate{k}", [P, NTOK]) for k in range(2)]
        h = [sb(f"hidden{k}", [P, TC]) for k in range(4)]
        h_parts = [[sb(f"hidden{k}{p}", [P, TC], F32R) for p in ("hi", "lo")] for k in range(4)]
        gated = [sb(f"gated{k}", [P, TC]) for k in range(DC)]
        h_ps = [ps(f"ps_hidden{k}") for k in range(4)]
        y_ps = [[ps(f"ps_y{k}{d}") for d in range(DC)] for k in range(2)]
        raw_in = [sem(f"raw_in{k}") for k in range(4)]
        w_high, w_low, b2_in = sem("w_high"), sem("w_low"), sem("b2_loaded")
        gate_in = [sem(f"gate_loaded{k}") for k in range(2)]
        init_done, init_read = sem("init_done"), sem("init_read")
        hidden, activated, high, split = sem("hidden_done"), sem("activated"), sem("hidden_high"), sem("hidden_split")
        y_done, y_read, summed = sem("y_done"), sem("y_read"), sem("summed")
        block = ctx.enter_context(nc.Block())

        def walk(eng, part):
            part("first", 0)
            with eng.Fori(1, E // 2 - 1) as i:
                part("middle", i)
            part("last", E // 2 - 1)
            part("tail", E // 2)

        def steps(name):
            return [(e, c, k) for e in range(2) for c in range(NTC) for k in range(HC0)]

        def step_no(pair, e, c, k):
            return 2 * STEPS * pair + STEPS * e + HC0 * c + k

        @block.sync
        def _(sp):
            def load(e, k):
                wait(sp, w_low, 4 * e + k - 3)
                e_ = slice(e, e + 1) if isinstance(e, int) else bass.ds(e, 1)
                if k < 2:
                    sp.dma_start(raw[k][:], dram["L0_ffn_w1"][e_, k * P:(k + 1) * P, :]
                                 .rearrange("a p n -> (a p) n")).then_inc(raw_in[k], 16)
                else:
                    rows = slice((k - 2) * 4 * P, (k - 1) * 4 * P)
                    sp.dma_start(raw[k][:].rearrange("p (c d) -> p c d", d=D),
                                 dram["L0_ffn_w2"][e_, rows, :].rearrange("a (c p) d -> p (a c) d", p=P))\
                        .then_inc(raw_in[k], 16)

            def load_gate(e, slot):
                wait(sp, y_read, NTC * (e - 1))
                src = dram["gates"][e:e + 1, :] if isinstance(e, int) else dram["gates"][bass.ds(e, 1), :]
                sp.dma_start(gate[slot][:], src.to_broadcast([P, NTOK])).then_inc(gate_in[slot], 16)

            for k in range(4):
                load(0, k)
            sp.dma_start(b2[:], dram["L0_ffn_b2"]).then_inc(b2_in, 16)
            load_gate(0, 0)
            for k in range(4):
                load(1, k)
            load_gate(1, 1)
            with sp.Fori(1, E // 2) as i:
                for e in range(2):
                    load_gate(2 * i + e, e)
                    for k in range(4):
                        load(2 * i + e, k)

        def w_piece(slot, k):
            return [x[:, k, :] for x in w1[slot]] if k < 2 else [x[:, (k - 2) * 4:(k - 1) * 4, :] for x in w2[slot]]

        def raw_piece(k):
            return raw[k][:] if k < 2 else raw[k][:].rearrange("p (c d) -> p c d", d=D)

        @block.gpsimd
        def _(pool):
            def low(e, slot, k):
                pool.wait_ge(w_high, 4 * e + k + 1)
                to = w_piece(slot, k)
                pool.tensor_tensor(to[1], raw_piece(k), to[0].bitcast(F32), ALU.subtract).then_inc(w_low, 1)

            def add_up(name, pair, e, c):
                m = NTC * (2 * pair + e) + c
                for d in range(DC):
                    pool.wait_ge(y_read, m + 1)
                    acc = t.accT[:, d, c * TC:(c + 1) * TC]
                    ins = pool.tensor_tensor(acc, acc, gated[d][:], ALU.add)
                ins.then_inc(summed, 1)

            for k in range(4):
                low(0, 0, k)
            pool.wait_ge(init_read, NTC * DC)

            def part(name, pair):
                for e, c in ((e, c) for e in range(2) for c in range(NTC)):
                    if name == "tail":
                        if (e, c) == (0, 0):
                            add_up(name, pair, -1, NTC - 1)
                        continue
                    if not (name == "first" and e == 0 and c == 0):
                        add_up(name, pair, e if c else e - 1, (c - 1) % NTC)
                    if not (name == "last" and e == 1):
                        low(2 * pair + e + 1, 1 - e, c)

            walk(pool, part)

        @block.scalar
        def _(act):
            def high_of(e, slot, k):
                act.wait_ge(raw_in[k], 16 * (e + 1))
                wait(act, y_done, STEPS * (e - 1))
                act.copy(w_piece(slot, k)[0], raw_piece(k)).then_inc(w_high, 1)

            for k in range(4):
                high_of(0, 0, k)

            def part(name, pair):
                for e, c, k in steps(name) if name != "tail" else ():
                    s = step_no(pair, e, c, k)
                    wait_apart(act, (hidden, s + 1), (split, s - 3))
                    at = (2 * pair + e) * HC0 + k
                    b = t.bias[:, at:at + 1] if isinstance(at, int) else t.bias[:, bass.ds(at, 1)]
                    act.activation(h[k % 4][:], h_ps[k % 4][:, 0:TC], ACT.Gelu, bias=b).then_inc(activated, 1)
                    if k == 5 and not (name == "last" and e == 1):
                        high_of(2 * pair + e + 1, 1 - e, c)

            walk(act, part)

        @block.vector
        def _(dve):
            for c in range(NTC):
                for d in range(DC):
                    dve.wait_ge(init_done, DC * c + d + 1)
                    dve.tensor_copy(t.accT[:, d, c * TC:(c + 1) * TC], y_ps[c % 2][d][:, 0:TC])\
                       .then_inc(init_read, 1)

            def read_y(pair, e, c):
                m = NTC * (2 * pair + e) + c
                dve.wait_ge(y_done, HC0 * (m + 1))
                dve.wait_ge(gate_in[e % 2], 16 * (pair + 1 + e // 2))
                wait(dve, summed, m)
                for d in range(DC):
                    ins = dve.tensor_tensor(gated[d][:], y_ps[c % 2][d][:, 0:TC],
                                            gate[e % 2][:, c * TC:(c + 1) * TC], ALU.mult)
                ins.then_inc(y_read, 1)

            def part(name, pair):
                for e, c, k in steps(name):
                    if name == "tail":
                        if (e, c, k) == (0, 0, 0):
                            read_y(pair, -1, NTC - 1)
                        continue
                    s = step_no(pair, e, c, k)
                    dve.wait_ge(activated, s + 1)
                    wait(dve, y_done, s - 3)
                    dve.tensor_copy(h_parts[k % 4][0][:], h[k % 4][:]).then_inc(high, 1)
                    dve.wait_ge(high, s + 1)
                    dve.tensor_tensor(h_parts[k % 4][1][:], h[k % 4][:], h_parts[k % 4][0][:].bitcast(F32),
                                      ALU.subtract).then_inc(split, 1)
                    if k == 2 and not (name == "first" and e == 0 and c == 0):
                        read_y(pair, e if c else e - 1, (c - 1) % NTC)

            walk(dve, part)

        @block.tensor
        def _(pe):
            pe.wait_ge(b2_in, 16)
            for c in range(NTC):
                for d in range(DC):
                    if c >= 2:
                        pe.wait_ge(init_read, DC * (c - 2) + d + 1)
                    pe.matmul(y_ps[c % 2][d][:, 0:TC], b2[:, d * P:(d + 1) * P],
                              t.gatesT[:, c * TC:(c + 1) * TC], start=True, stop=True).then_inc(init_done, 1)

            def hidden_of(pair, e, c, k):
                s = step_no(pair, e, c, k)
                if c == 0 and k == 0:
                    pe.wait_ge(w_low, 4 * (2 * pair + e + 1))
                wait(pe, activated, s - 3)
                for d in range(DC):
                    ins = three_pass(pe, h_ps[k % 4][:, 0:TC], [x[:, d, k * P:(k + 1) * P] for x in w1[e]],
                                     [x[:, d, c * TC:(c + 1) * TC] for x in t.xT], d == 0, d == DC - 1)
                ins.then_inc(hidden, 1)

            def output_of(name, pair, e, c, k):
                s = step_no(pair, e, c, k)
                m = NTC * (2 * pair + e) + c
                pe.wait_ge(split, s + 1)
                if k == 0:
                    wait(pe, y_read, m - 1)
                    if name == "first" and m < 2:
                        pe.wait_ge(init_read, NTC * DC)
                for d in range(DC):
                    ins = three_pass(pe, y_ps[c % 2][d][:, 0:TC], [x[:, k, d * P:(d + 1) * P] for x in w2[e % 2]],
                                     [x[:] for x in h_parts[k % 4]], k == 0, k == HC0 - 1)
                ins.then_inc(y_done, 1)

            def part(name, pair):
                for e, c, k in steps(name):
                    if name != "tail":
                        hidden_of(pair, e, c, k)
                    back = STEPS * e + HC0 * c + k - LAG_Y
                    if name == "first" and back < 0 or name == "tail" and back >= 0:
                        continue
                    output_of(name, pair, back // STEPS, back % STEPS // HC0, back % HC0)

            walk(pe, part)


def close_layer0(nc, t):
    with ExitStack() as ctx:
        def sem(name):
            return ctx.enter_context(nc.semaphore("c_" + name))

        stats = [ctx.enter_context(nc.sbuf_tensor(f"c_stats{k}", [S, 6], F32)) for k in range(2)]
        mv = [ctx.enter_context(nc.sbuf_tensor(f"c_mv{k}", [S, 2], F32)) for k in range(4)]
        var_eps = ctx.enter_context(nc.sbuf_tensor("c_var_eps", [S, 4], F32))
        rstd = ctx.enter_context(nc.sbuf_tensor("c_rstd", [S, 4], F32))
        xn = [ctx.enter_context(nc.sbuf_tensor(f"c_xn{k}", [S, D], F32)) for k in range(2)]
        y_ps = [ctx.enter_context(nc.psum_tensor(f"c_ps_y{k}", [S, D], F32)) for k in range(3)]
        x_ps = [ctx.enter_context(nc.psum_tensor(f"c_ps_x{k}", [P, DC, S], F32)) for k in range(3)]
        y_turned, x_done, stats_done = sem("y_turned"), sem("x_done"), sem("stats_done")
        mv_done, eps_done, root_done, xn_done = sem("mv_done"), sem("eps_done"), sem("root_done"), sem("xn_done")
        x_turned, high_done, low_done = sem("x_turned"), sem("high_done"), sem("low_done")
        block = ctx.enter_context(nc.Block())
        L2, L3 = 2, 3

        @block.tensor
        def _(pe):
            for b in range(B + L2):
                if b < B:
                    if b >= 3:
                        pe.wait_ge(x_done, b - 2)
                    for d in range(DC):
                        ins = pe.transpose(y_ps[b % 3][:, d * P:(d + 1) * P], t.accT[:, d, b * S:(b + 1) * S],
                                           t.ident[:])
                    ins.then_inc(y_turned, 1)
                if b >= L2:
                    c = b - L2
                    pe.wait_ge(xn_done, c + 1)
                    if c >= 3:
                        pe.wait_ge(low_done, c - 2)
                    for d in range(DC):
                        ins = pe.transpose(x_ps[c % 3][:, d, :], xn[c % 2][:, d * P:(d + 1) * P],
                                           t.ident[0:S, 0:S])
                    ins.then_inc(x_turned, 1)

        @block.vector
        def _(dve):
            for b in range(B + L3):
                if b < B:
                    dve.wait_ge(y_turned, b + 1)
                    dve.scalar_tensor_tensor(out=t.x[:, b, :], in0=y_ps[b % 3][:], scalar=t.tanh_g[:, 2:3],
                                             in1=t.x[:, b, :], op0=ALU.mult, op1=ALU.add).then_inc(x_done, 1)
                    dve.wait_ge(x_done, b + 1)
                    dve.bn_stats(stats[b % 2][:], t.x[:, b, :]).then_inc(stats_done, 1)
                    dve.wait_ge(stats_done, b + 1)
                    if b >= 4:
                        dve.wait_ge(xn_done, b - 3)
                    dve.bn_aggr(mv[b % 4][:], stats[b % 2][:]).then_inc(mv_done, 1)
                if 1 <= b <= B:
                    c = b - 1
                    dve.wait_ge(root_done, c + 1)
                    if c >= 2:
                        dve.wait_ge(x_turned, c - 1)
                    dve.tensor_scalar(xn[c % 2][:], t.x[:, c, :], mv[c % 4][:, 0:1], rstd[:, c % 4:c % 4 + 1],
                                      ALU.subtract, ALU.mult).then_inc(xn_done, 1)
                if b >= L3:
                    c = b - L3
                    cols = slice(c * S, (c + 1) * S)
                    dve.wait_ge(high_done, c + 1)
                    dve.tensor_tensor(t.xT[1][:, :, cols], x_ps[c % 3][:], t.xT[0][:, :, cols].bitcast(F32),
                                      ALU.subtract).then_inc(low_done, 1)

        @block.gpsimd
        def _(pool):
            for b in range(B):
                k = b % 4
                pool.wait_ge(mv_done, b + 1)
                pool.tensor_scalar(var_eps[:, k:k + 1], mv[k][:, 1:2], LN_EPS, None, ALU.add).then_inc(eps_done, 1)
                pool.wait_ge(eps_done, b + 1)
                pool.tensor_tensor(rstd[:, k:k + 1], var_eps[:, k:k + 1], t.minus_half[:, 0:1],
                                   ALU.pow).then_inc(root_done, 1)

        @block.scalar
        def _(act):
            for b in range(B):
                act.wait_ge(x_turned, b + 1)
                act.copy(t.xT[0][:, :, b * S:(b + 1) * S], x_ps[b % 3][:]).then_inc(high_done, 1)


def experts1(nc, t, dram, out):
    NE = E + 1
    STEPS = NE * HC1
    W = DC * HID1 + HC1 * D
    n = "e1_"
    with ExitStack() as ctx:
        def sb(name, shape, dt=F32):
            return ctx.enter_context(nc.sbuf_tensor(n + name, shape, dt))

        def ps(name):
            return ctx.enter_context(nc.psum_tensor(n + name, [P, 512], F32))

        def sem(name):
            return ctx.enter_context(nc.semaphore(n + name))

        w = [sb(f"w_{p}", [P, NE, W], F32R) for p in ("hi", "lo")]
        raw = [sb(f"w_raw{k}", [P, W]) for k in range(2)]
        b2 = sb("b2_rows", [E, D])
        gate = [sb(f"gate{k}", [P, E, TC]) for k in range(2)]
        h = [sb(f"hidden{k}", [P, TC]) for k in range(3)]
        hg = [sb(f"gated{k}", [P, TC]) for k in range(3)]
        h_parts = [[sb(f"hidden{k}{p}", [P, TC], F32R) for p in ("hi", "lo")] for k in range(3)]
        yT = sb("yT", [P, DC, TC])
        h_ps = [ps(f"ps_hidden{k}") for k in range(3)]
        y_ps = [[ps(f"ps_y{k}{d}") for d in range(DC)] for k in range(2)]
        o_ps = ps("ps_out")
        raw_in = [sem(f"raw_in{k}") for k in range(2)]
        w_high, w_low, b2_in = sem("w_high"), sem("w_low"), sem("b2_loaded")
        gate_in = [sem(f"gate_loaded{k}") for k in range(2)]
        hidden, activated, gated, high, split = (
            sem("hidden_done"), sem("activated"), sem("gated"), sem("hidden_high"), sem("hidden_split"))
        y_done, y_read, turned, x_done, stored = (
            sem("y_done"), sem("y_read"), sem("turned"), sem("x_done"), sem("stored"))
        block = ctx.enter_context(nc.Block())
        up = [x[:, :, 0:DC * HID1].rearrange("p e (c n) -> p e c n", c=DC) for x in w]
        down = [x[:, :, DC * HID1:W].rearrange("p e (c n) -> p e c n", c=HC1) for x in w]
        OUT_STEPS = [6, 8, 10, 12]

        def walk(eng, part):
            part("first", 0)
            part("middle", 1)
            part("middle", 2)
            part("last", NTC - 1)
            part("tail", NTC)

        steps = [(e, k) for e in range(NE) for k in range(HC1)]

        @block.sync
        def _(sp):
            def load(e):
                if e >= 2:
                    sp.wait_ge(w_low, e - 1)
                r = raw[e % 2]
                a = dram["L1_ffn_up_w"][e] if e < E else dram["L1_ffn_sh_up_w"]
                b = dram["L1_ffn_down_w"][e] if e < E else dram["L1_ffn_sh_down_w"]
                sp.dma_start(r[:, 0:DC * HID1].rearrange("p (c n) -> p c n", c=DC),
                             a.rearrange("(c p) n -> p c n", p=P)).then_inc(raw_in[e % 2], 16)
                sp.dma_start(r[:, DC * HID1:W].rearrange("p (c n) -> p c n", c=HC1),
                             b.rearrange("(c p) n -> p c n", p=P)).then_inc(raw_in[e % 2], 16)

            def load_gates(c):
                wait(sp, gated, E * HC1 * (c - 1))
                sp.dma_start(gate[c % 2][:], dram["gates"][None, :, c * TC:(c + 1) * TC].to_broadcast([P, E, TC]))\
                    .then_inc(gate_in[c % 2], 16)

            sp.dma_start(b2[:], dram["L1_ffn_down_b"]).then_inc(b2_in, 16)
            load(0)
            load_gates(0)
            for e in range(1, NE):
                load(e)
            for c in range(1, NTC):
                load_gates(c)
            for b in range(B):
                sp.wait_ge(x_done, b + 1)
                sp.dma_start(out[b], t.x[:, b, :]).then_inc(stored, 16)
            sp.wait_ge(stored, 16 * B)

        @block.gpsimd
        def _(pool):
            for e in range(NE):
                pool.wait_ge(w_high, e + 1)
                pool.tensor_tensor(w[1][:, e, :], raw[e % 2][:], w[0][:, e, :].bitcast(F32),
                                   ALU.subtract).then_inc(w_low, 1)

        @block.scalar
        def _(act):
            def high_of(e):
                act.wait_ge(raw_in[e % 2], 32 * (e // 2 + 1))
                act.copy(w[0][:, e, :], raw[e % 2][:]).then_inc(w_high, 1)

            high_of(0)
            high_of(1)

            def read_y(c):
                act.wait_ge(y_done, STEPS * (c + 1))
                wait(act, turned, BPC * c)
                at = BIAS_COLS["sh_down"][0]
                for d in range(DC):
                    ins = act.activation(yT[:, d, :], y_ps[c % 2][d][:, 0:TC], ACT.Identity,
                                         bias=t.bias[:, at + d:at + d + 1])
                ins.then_inc(y_read, 1)

            def part(name, c):
                for e, k in steps if name != "tail" else ():
                    s = STEPS * c + HC1 * e + k
                    act.wait_ge(hidden, s + 1)
                    wait(act, split, s - 2)
                    at = BIAS_COLS["up_b"][0] + HC1 * e + k if e < E else BIAS_COLS["sh_up"][0] + k
                    act.activation(h[s % 3][:], h_ps[s % 3][:, 0:TC], ACT.Silu,
                                   bias=t.bias[:, at:at + 1]).then_inc(activated, 1)
                    if name == "first" and k == 1 and e + 2 < NE:
                        high_of(e + 2)
                    if (e, k) == (1, 1) and c > 0:
                        read_y(c - 1)
                if name == "tail":
                    read_y(c - 1)

            walk(act, part)

        @block.vector
        def _(dve):
            def finish(b):
                dve.wait_ge(turned, b + 1)
                dve.scalar_tensor_tensor(out=t.x[:, b, :], in0=o_ps[0:S, 0:D], scalar=t.tanh_g[:, 3:4],
                                         in1=t.x[:, b, :], op0=ALU.mult, op1=ALU.add).then_inc(x_done, 1)

            def part(name, c):
                for e, k in steps if name != "tail" else ():
                    s = STEPS * c + HC1 * e + k
                    dve.wait_ge(activated, s + 1)
                    wait(dve, y_done, s - 2)
                    src = h[s % 3]
                    if e < E:
                        if e == 0 and k == 0:
                            dve.wait_ge(gate_in[c % 2], 16 * (c // 2 + 1))
                        src = hg[s % 3]
                        dve.tensor_tensor(src[:], h[s % 3][:], gate[c % 2][:, e, :], ALU.mult).then_inc(gated, 1)
                        dve.wait_ge(gated, E * HC1 * c + HC1 * e + k + 1)
                    dve.tensor_copy(h_parts[s % 3][0][:], src[:]).then_inc(high, 1)
                    dve.wait_ge(high, s + 1)
                    dve.tensor_tensor(h_parts[s % 3][1][:], src[:], h_parts[s % 3][0][:].bitcast(F32),
                                      ALU.subtract).then_inc(split, 1)
                    if c > 0 and HC1 * e + k - 1 in OUT_STEPS:
                        finish(BPC * (c - 1) + OUT_STEPS.index(HC1 * e + k - 1))
                if name == "tail":
                    for j in range(BPC):
                        finish(BPC * (c - 1) + j)

            walk(dve, part)

        @block.tensor
        def _(pe):
            pe.wait_ge(b2_in, 16)

            def hidden_of(c, e, k):
                s = STEPS * c + HC1 * e + k
                if c == 0 and k == 0:
                    pe.wait_ge(w_low, e + 1)
                wait(pe, activated, s - 2)
                for d in range(DC):
                    ins = three_pass(pe, h_ps[s % 3][:, 0:TC], [x[:, e, d, k * P:(k + 1) * P] for x in up],
                                     [x[:, d, c * TC:(c + 1) * TC] for x in t.xT], d == 0, d == DC - 1)
                ins.then_inc(hidden, 1)

            def output_of(c, e, k):
                s = STEPS * c + HC1 * e + k
                if e == 0 and k == 0:
                    wait(pe, y_read, c - 1)
                    for d in range(DC):
                        pe.matmul(y_ps[c % 2][d][:, 0:TC], b2[:, d * P:(d + 1) * P],
                                  t.gatesT[:, c * TC:(c + 1) * TC], start=True, stop=False)
                pe.wait_ge(split, s + 1)
                for d in range(DC):
                    ins = three_pass(pe, y_ps[c % 2][d][:, 0:TC], [x[:, e, k, d * P:(d + 1) * P] for x in down],
                                     [x[:] for x in h_parts[s % 3]], False, (e, k) == (NE - 1, HC1 - 1))
                ins.then_inc(y_done, 1)

            def turn(b):
                c, j = b // BPC, b % BPC
                pe.wait_ge(y_read, c + 1)
                wait(pe, x_done, b)
                for d in range(DC):
                    ins = pe.transpose(o_ps[0:S, d * P:(d + 1) * P], yT[:, d, j * S:(j + 1) * S], t.ident[:])
                ins.then_inc(turned, 1)

            def part(name, c):
                for e, k in steps:
                    at = HC1 * e + k
                    if name != "tail":
                        hidden_of(c, e, k)
                    back = at - LAG_Y
                    if not (name == "first" and back < 0 or name == "tail" and back >= 0):
                        output_of(c + back // STEPS, back % STEPS // HC1, back % HC1)
                    if name not in ("first", "tail") and at in OUT_STEPS:
                        turn(BPC * (c - 1) + OUT_STEPS.index(at))
                if name == "tail":
                    for j in range(BPC):
                        turn(BPC * (c - 1) + j)

            walk(pe, part)


def flamingo_layers(nc, dram, out):
    t = Core()
    with ExitStack() as persistent:
        allocate_persistent(nc, persistent, t)
        prepare(nc, t, dram)
        for layer in range(2):
            attention(nc, t, dram, layer)
            with ExitStack() as ctx:
                t.gatesT = ctx.enter_context(nc.sbuf_tensor(f"gatesT{layer}", [E, NTOK], F32))
                router(nc, t, dram, layer)
                if layer == 0:
                    t.accT = ctx.enter_context(nc.sbuf_tensor("accT", [P, DC, NTOK], F32))
                    experts0(nc, t, dram)
                    close_layer0(nc, t)
                else:
                    experts1(nc, t, dram, out)


_PLAIN = ["x", "g_xattn", "g_ffn"] + [f"L{l}_xattn_W{k}" for l in range(2) for k in "qkvo"] + [
    "L0_ffn_w1", "L0_ffn_w2", "L0_ffn_b2", "L1_ffn_up_w", "L1_ffn_down_w", "L1_ffn_down_b",
    "L1_ffn_sh_up_w", "L1_ffn_sh_down_w"]
_ROWS = ["L0_xattn_bv", "L0_xattn_bo", "L0_xattn_ln_gamma", "L0_xattn_ln_beta", "L1_xattn_bv", "L1_xattn_bo"]


def kernel(**inputs):
    import numpy as _np
    import concourse.bacc as _bacc
    from concourse import mybir as _mybir
    from concourse.bass_utils import run_bass_kernel_spmd as _run

    a = {k: _np.asarray(v) for k, v in inputs.items()}
    sent = {k: a[k] for k in _PLAIN}
    for k in _ROWS:
        sent[k] = a[k].reshape(1, -1)
    sent["ctxT"] = a["ctx_1024"].transpose(0, 2, 1)
    sent["mask"] = a["mask_Bx1x1xS2_ff0"].reshape(B, SC)
    columns = {"b1": "L0_ffn_b1", "bq0": "L0_xattn_bq", "bk0": "L0_xattn_bk", "bq1": "L1_xattn_bq",
               "bk1": "L1_xattn_bk", "up_b": "L1_ffn_up_b", "sh_up": "L1_ffn_sh_up_b", "sh_down": "L1_ffn_sh_down_b"}
    sent["bias_cols"] = _np.concatenate([a[columns[k]].reshape(-1, P).T for k in BIAS_COLS], axis=1)
    sent["router0"] = _np.concatenate([a["L0_ffn_router_w"], a["L0_ffn_lang_w"]], axis=0).T
    sent["router_bias"] = _np.concatenate([a["L0_ffn_router_b"], a["L0_ffn_lang_b"]]).reshape(1, NR)
    sent["router1"] = a["L1_ffn_gate_w"].T

    nc = _bacc.Bacc("TRN2", target_bir_lowering=False, num_devices=1)
    arrays, dram = {}, {}
    for name, v in sent.items():
        v = _np.ascontiguousarray(v)
        arrays[f"in_{name}_dram"] = v
        dram[name] = nc.dram_tensor(f"in_{name}_dram", v.shape, _mybir.dt.from_np(v.dtype), kind="ExternalInput").ap()
    dram["gates"] = nc.dram_tensor("gates_scratch", (E, NTOK), _mybir.dt.float32, kind="Internal").ap()
    out = nc.dram_tensor("out_0_dram", (B, S, D), _mybir.dt.float32, kind="ExternalOutput").ap()
    flamingo_layers(nc, dram, out)
    r = _run(nc, [arrays], core_ids=[0])
    return r.results[0]["out_0_dram"]
```

```python
from contextlib import ExitStack

import concourse.bass as bass
from concourse import mybir

F32 = mybir.dt.float32
F32R = mybir.dt.float32r
U32 = mybir.dt.uint32
ALU = mybir.AluOpType
ACT = mybir.ActivationFunctionType
AX = mybir.AxisListType

P = 128
B, S, D = 16, 100, 256
NTOK = B * S
SC = 361
H = 16
DC = D // P
DK0, DK1 = 64, D // H
N0 = H * DK0
CH0 = N0 // P
KT = 3
KR = (SC + KT - 1) // KT
CW = 364
CM = 362
E = 8
HID0, HID1 = 1024, 256
HC0, HC1 = HID0 // P, HID1 // P
TC = 400
NTC = NTOK // TC
BPC = TC // S
LN_EPS = 1e-5
NR = E + 4

BIAS_COLS = {}
_at = 0
for _name, _n in (("b1", E * HC0), ("bq0", CH0), ("bk0", CH0), ("bq1", DC), ("bk1", DC),
                  ("up_b", E * HC1), ("sh_up", HC1), ("sh_down", DC)):
    BIAS_COLS[_name] = (_at, _n)
    _at += _n
NBIAS = _at


def span(name):
    at, n = BIAS_COLS[name]
    return at, at + n


def wait(eng, sem, value):
    if isinstance(value, int) and value <= 0:
        return
    eng.wait_ge(sem, value)


def wait_apart(eng, *waits):
    waits = [(sem, v if isinstance(v, int) else eng.snap(eng.to_reg(v))) for sem, v in waits if not isinstance(v, int) or v > 0]
    if not all(isinstance(v, int) for _, v in waits):
        eng.wait_ge(waits[0][0], 1)
    for sem, value in waits:
        eng.wait_ge(sem, value)


def three_pass(pe, out, left, right, first, last):
    pe.matmul(out, left[0], right[0], start=first, stop=False)
    pe.matmul(out, left[0], right[1], start=False, stop=False)
    return pe.matmul(out, left[1], right[0], start=False, stop=last)


class Core:
    pass


def allocate_persistent(nc, ctx, t):
    def sb(name, shape, dt=F32):
        return ctx.enter_context(nc.sbuf_tensor(name, shape, dt))

    t.x = sb("x_rows", [S, B, D])
    t.xT = [sb(f"xnormT_{k}", [P, DC, NTOK], F32R) for k in ("hi", "lo")]
    t.ident = sb("identity", [P, P])
    t.bias = sb("bias_cols", [P, NBIAS])
    t.bq0s = sb("bq0_scaled", [P, CH0])
    t.bq1s = sb("bq1_scaled", [P, DC])
    t.gate_rows = sb("g_rows", [S, 4])
    t.tanh_g = sb("tanh_g", [S, 4])
    t.minus_half = sb("minus_half", [S, B])
    t.mv0 = sb("mean_var0", [S, B, 2])
    t.rstd0 = sb("rstd0", [S, B])
    t.xn = sb("xnorm_rows", [S, D])


def prepare(nc, t, dram, inputs):
    with ExitStack() as ctx:
        def sem(name):
            return ctx.enter_context(nc.semaphore(name))

        x_in = [sem(f"pre_x_loaded{k}") for k in range(2)]
        g_in, bias_in = sem("pre_g_loaded"), sem("pre_bias_loaded")
        pool_own, dve_own, act_own = sem("pre_pool_own"), sem("pre_dve_own"), sem("pre_act_own")
        rstd_ready, xn_ready = sem("pre_rstd_ready"), sem("pre_xn_ready")
        turned, high_ready, low_ready = sem("pre_turned"), sem("pre_high"), sem("pre_low")
        stats_ready, ident_ready = sem("pre_stats_ready"), sem("pre_ident_ready")
        weights_low, q_low = sem("pre_weights_low"), sem("pre_q_low")
        stats = ctx.enter_context(nc.sbuf_tensor("pre_stats", [S, B, 6], F32))
        var_eps = ctx.enter_context(nc.sbuf_tensor("pre_var_eps", [S, B], F32))
        xn = [ctx.enter_context(nc.sbuf_tensor(f"pre_xn{k}", [S, D], F32)) for k in range(4)]
        ps = [ctx.enter_context(nc.psum_tensor(f"pre_ps{k}", [P, DC, S], F32)) for k in range(4)]
        inputs.stage(ctx)
        HALF = B // 2
        block = ctx.enter_context(nc.Block())

        @block.sync
        def _(sp):
            for k in range(2):
                half = slice(k * HALF, (k + 1) * HALF)
                sp.dma_start(t.x[:, half, :], dram["x"][half].rearrange("b s d -> s b d")).then_inc(x_in[k], 16)
            sp.dma_start(t.gate_rows[:, 0:2], dram["g_xattn"].rearrange("(a g) -> a g", a=1)
                         .to_broadcast([S, 2])).then_inc(g_in, 16)
            sp.dma_start(t.gate_rows[:, 2:4], dram["g_ffn"].rearrange("(a g) -> a g", a=1)
                         .to_broadcast([S, 2])).then_inc(g_in, 16)
            sp.dma_start(t.bias[:], dram["bias_cols"]).then_inc(bias_in, 16)
            inputs.load(sp)
            sp.wait_ge(inputs.rows_in, 64)

        @block.gpsimd
        def _(pool):
            pool.memset(t.ident[:], 0.0).then_inc(pool_own, 1)
            pool.memset(t.minus_half[:], -0.5).then_inc(pool_own, 1)
            pool.wait_ge(pool_own, 2)
            pool.affine_select(out=t.ident[:], in_=t.ident[:], compare_op=ALU.not_equal, fill=1.0,
                               base=0, pattern=[[-1, P]], channel_multiplier=1).then_inc(ident_ready, 1)
            for k in range(2):
                half = slice(k * HALF, (k + 1) * HALF)
                pool.wait_ge(stats_ready, k + 1)
                pool.tensor_scalar(var_eps[:, half], t.mv0[:, half, 1], LN_EPS, None, ALU.add)\
                    .then_inc(pool_own, 1)
                pool.wait_ge(pool_own, k + 3)
                pool.tensor_tensor(t.rstd0[:, half], var_eps[:, half], t.minus_half[:, half], ALU.pow)\
                    .then_inc(rstd_ready, 1)
            inputs.split_context_low(pool)
            for k in "kvo":
                inputs.split_low(pool, k, weights_low)

        @block.scalar
        def _(act):
            act.wait_ge(g_in, 32)
            act.activation(t.tanh_g[:], t.gate_rows[:], ACT.Tanh).then_inc(act_own, 1)
            act.wait_ge(bias_in, 16)
            q0, n0 = BIAS_COLS["bq0"]
            q1, n1 = BIAS_COLS["bq1"]
            act.mul(t.bq0s[:], t.bias[:, q0:q0 + n0], DK0 ** -0.5).then_inc(act_own, 1)
            act.mul(t.bq1s[:], t.bias[:, q1:q1 + n1], -(DK1 ** -0.5)).then_inc(act_own, 1)
            inputs.split_context_high(act)
            inputs.split_high(act, "k")
            inputs.split_high(act, "q")
            for b in range(B):
                if b == B // 4:
                    inputs.split_high(act, "v")
                if b == B // 2:
                    inputs.split_high(act, "o")
                act.wait_ge(turned, b + 1)
                act.copy(t.xT[0][:, :, b * S:(b + 1) * S], ps[b % 4][:]).then_inc(high_ready, 1)

        @block.vector
        def _(dve):
            for k in range(2):
                dve.wait_ge(x_in[k], 16)
                for b in range(k * HALF, (k + 1) * HALF):
                    dve.bn_stats(stats[:, b, :], t.x[:, b, :]).then_inc(dve_own, 1)
                for b in range(k * HALF, (k + 1) * HALF):
                    dve.wait_ge(dve_own, b + 1)
                    ins = dve.bn_aggr(t.mv0[:, b, :], stats[:, b, :])
                ins.then_inc(stats_ready, 1)
            for b in range(B + 2):
                if b % HALF == 0 and b < B:
                    dve.wait_ge(rstd_ready, b // HALF + 1)
                    dve.wait_ge(stats_ready, b // HALF + 1)
                if b < B:
                    if b >= 4:
                        dve.wait_ge(turned, b - 3)
                    dve.tensor_scalar(xn[b % 4][:], t.x[:, b, :], t.mv0[:, b, 0:1], t.rstd0[:, b:b + 1],
                                      ALU.subtract, ALU.mult).then_inc(xn_ready, 1)
                if b >= 2:
                    c = b - 2
                    dve.wait_ge(high_ready, c + 1)
                    cols = slice(c * S, (c + 1) * S)
                    dve.tensor_tensor(t.xT[1][:, :, cols], ps[c % 4][:], t.xT[0][:, :, cols].bitcast(F32),
                                      ALU.subtract).then_inc(low_ready, 1)
            inputs.split_low(dve, "q", q_low)

        @block.tensor
        def _(pe):
            pe.wait_ge(ident_ready, 1)
            for b in range(B):
                pe.wait_ge(xn_ready, b + 1)
                if b >= 4:
                    pe.wait_ge(low_ready, b - 3)
                for c in range(DC):
                    ins = pe.transpose(ps[b % 4][:, c, :], xn[b % 4][:, c * P:(c + 1) * P], t.ident[0:S, 0:S])
                ins.then_inc(turned, 1)


LAG_T, LAG_V = 2, 3
RING = 3
PAIRS = B // 2


class Job:

    def __init__(self, part, kind, batch, args, step):
        self.part, self.kind, self.batch, self.args, self.step = part, kind, batch, args, step


def side_jobs0(batch, h, odd):
    nxt, prev = batch + 1, batch - 1
    jobs = []
    if h == 0:
        jobs.append(("K", batch, (CH0 - 1,)))
        if not odd:
            jobs += [("Q", batch, (CH0 - 1, half)) for half in range(2)]
    if h >= 2 and h % 2 == 0:
        jobs.append(("K", nxt, (h // 2 - 1,)))
    if h in (3, 5, 7):
        jobs.append(("V", batch, (1, (h - 3) // 2)))
    if h in (11, 13, 15):
        jobs.append(("V", nxt, (0, (h - 11) // 2)))
    if h == 4:
        jobs.append(("OT", prev, (1,)))
    if h == 9:
        jobs.append(("OP", prev, ()))
    if h == 12:
        jobs.append(("OT", batch, (0,)))
    if h == 14:
        jobs.append(("XT", prev, ()))
    if odd and h >= 3 and h % 2 == 1:
        jobs.append(("Q", nxt, ((h - 3) // 2, None)))
    return jobs


def side_jobs1(batch, h, odd):
    nxt, prev = batch + 1, batch - 1
    jobs = []
    if h in (2, 4):
        jobs.append(("K", nxt, (h // 2 - 1,)))
    if h in (6, 7, 8):
        jobs.append(("V", nxt, (h - 6,)))
    if h == 5:
        jobs.append(("OT", prev, (0,)))
    if h == 9:
        jobs.append(("OP", prev, ()))
    if h == 15:
        jobs.append(("XT", prev, ()))
    if odd and h in (1, 3):
        jobs.append(("Q", nxt, (h // 2, None)))
    return jobs


PARTS = ("prologue", "first", "middle", "last", "tail")
PAIR_OF = {"prologue": 0, "first": 0, "last": PAIRS - 1, "tail": PAIRS}


class Plan:

    def __init__(self, side_jobs, prologue, act_kinds, dve_kinds):
        self.kinds = {"act": act_kinds, "dve": dve_kinds}
        self.jobs, count = [], {"all": 0, "act": 0, "dve": 0}
        for part in PARTS:
            if part == "last":
                for key in count:
                    count[key] += (PAIRS - 3) * self.per[key]
            before = dict(count)
            for where, (kind, batch, args) in self._listed(part, side_jobs, prologue):
                job = Job(part, kind, batch, args, where)
                job.n, job.n_act, job.n_dve = count["all"], count["act"], count["dve"]
                count["all"] += 1
                count["act"] += kind in act_kinds
                count["dve"] += kind in dve_kinds
                self.jobs.append(job)
            if part == "middle":
                self.per = {key: count[key] - before[key] for key in count}
                assert self.per["all"] % RING == 0

    @staticmethod
    def _listed(part, side_jobs, prologue):
        if part == "prologue":
            return [(None, j) for j in prologue]
        pair = 1 if part == "middle" else PAIR_OF[part]
        return [((local, h), j)
                for local in range(1 if part == "tail" else 2) for h in range(H)
                for j in side_jobs(local, h, local == 1) if 0 <= 2 * pair + j[1] < B]

    def of(self, part, where=None):
        return [j for j in self.jobs if j.part == part and (where is None or j.step == where)]

    def count(self, part, pair, job, who):
        n = {"act": job.n_act, "dve": job.n_dve}[who] + 1
        if part == "middle":
            return pair * self.per[who] + (n - self.per[who])
        return n + (PAIRS - 3) * self.per[who] if part in ("last", "tail") and job.part == "middle" else n

    def number(self, part, pair, job):
        return pair * self.per["all"] + (job.n + 1 - self.per["all"]) if part == "middle" else job.n + 1

    def before(self, job, far=RING):
        k = self.jobs.index(job) - far
        return self.jobs[k] if k >= 0 else None

    def latest(self, part, where, kind, *args):
        if isinstance(where, Job):
            known = self.jobs[:self.jobs.index(where)]
        else:
            known = [j for j in self.jobs if PARTS.index(j.part) < PARTS.index(part)
                     or j.part == part and j.step < where]
        return [j for j in known if j.kind == kind and j.args[:len(args)] == args][-1]


class AttentionInputs:

    def __init__(self, nc, ctx, t, dram, layer):
        L0 = layer == 0
        n = f"a{layer}_"
        nch = CH0 if L0 else DC
        width = nch * P

        def sb(name, shape, dt=F32):
            return ctx.enter_context(nc.sbuf_tensor(n + name, shape, dt))

        def parts(name, shape):
            return [sb(f"{name}_{k}", shape, F32R) for k in ("hi", "lo")]

        def sem(name):
            return ctx.enter_context(nc.semaphore(n + name))

        self.nc, self.t, self.dram, self.n = nc, t, dram, n
        self.L0, self.nch, self.width, self.pre = L0, nch, width, f"L{layer}_xattn_"
        self.wq, self.wk, self.wv = (parts(w, [P, DC, width]) for w in ("wq", "wk", "wv"))
        self.wo = parts("wo", [P, nch, D])
        self.ctx_raw = sb("ctx_raw", [P, DC, SC])
        self.cT = [parts(f"ctxT{k}", [P, DC, CW]) for k in range(2)]
        self.bv_rows, self.bo_rows = sb("bv_rows", [S, width]), sb("bo_rows", [S, D])
        if L0:
            self.gamma, self.beta = sb("gamma_rows", [S, D]), sb("beta_rows", [S, D])
        self.w_in = {k: sem(f"w{k}_loaded") for k in "kqvo"}
        self.w_high, self.rows_in = sem("weights_high"), sem("rows_loaded")
        self.ctx_in, self.ctx_high, self.ctx_low = sem("ctx_loaded"), sem("ctx_high"), sem("ctx_low")
        self.scale = {"k": 1.0, "q": DK0 ** -0.5 if L0 else -(DK1 ** -0.5), "v": 1.0, "o": 1.0}
        self.parts = {"k": self.wk, "q": self.wq, "v": self.wv, "o": self.wo}

    def stage(self, ctx):
        self.raw = {k: ctx.enter_context(self.nc.sbuf_tensor(f"{self.n}raw_w{k}", list(w[0].shape), F32))
                    for k, w in self.parts.items()}

    def load(self, sp):
        sp.dma_start(self.ctx_raw[:], self.dram["ctxT"][0].rearrange("(c p) s -> p c s", p=P))\
            .then_inc(self.ctx_in, 16)
        for k, raw in self.raw.items():
            sp.dma_start(raw[:], self.dram[self.pre + "W" + k].rearrange("(c p) n -> p c n", p=P))\
                .then_inc(self.w_in[k], 16)
        sp.dma_start(self.bv_rows[:], self.dram[self.pre + "bv"].to_broadcast([S, self.width]))\
            .then_inc(self.rows_in, 16)
        sp.dma_start(self.bo_rows[:], self.dram[self.pre + "bo"].to_broadcast([S, D])).then_inc(self.rows_in, 16)
        if self.L0:
            sp.dma_start(self.gamma[:], self.dram["L0_xattn_ln_gamma"].to_broadcast([S, D]))\
                .then_inc(self.rows_in, 16)
            sp.dma_start(self.beta[:], self.dram["L0_xattn_ln_beta"].to_broadcast([S, D]))\
                .then_inc(self.rows_in, 16)

    def split_context_high(self, act):
        act.wait_ge(self.ctx_in, 16)
        act.copy(self.cT[0][0][:, :, 0:SC], self.ctx_raw[:]).then_inc(self.ctx_high, 1)

    def split_context_low(self, pool):
        pool.wait_ge(self.ctx_high, 1)
        pool.tensor_tensor(self.cT[0][1][:, :, 0:SC], self.ctx_raw[:], self.cT[0][0][:, :, 0:SC].bitcast(F32),
                           ALU.subtract).then_inc(self.ctx_low, 1)

    def split_high(self, act, k):
        act.wait_ge(self.w_in[k], 16)
        act.mul(self.parts[k][0][:], self.raw[k][:], self.scale[k]).then_inc(self.w_high, 1)

    def split_low(self, eng, k, done):
        eng.wait_ge(self.w_high, "kqvo".index(k) + 1)
        if self.scale[k] == 1.0:
            ins = eng.tensor_tensor(self.parts[k][1][:], self.raw[k][:], self.parts[k][0][:].bitcast(F32),
                                    ALU.subtract)
        else:
            ins = eng.scalar_tensor_tensor(out=self.parts[k][1][:], in0=self.raw[k][:], scalar=self.scale[k],
                                           in1=self.parts[k][0][:].bitcast(F32),
                                           op0=ALU.mult, op1=ALU.subtract)
        ins.then_inc(done, 1)


def attention(nc, t, dram, layer, inputs):
    L0 = layer == 0
    nch = CH0 if L0 else DC
    hpc = H // nch
    width = nch * P
    dv = DK0 if L0 else DK1
    vw = dv if L0 else dv + 1
    o_per = 2 if L0 else 1
    hpo = H // o_per
    n = f"a{layer}_"
    if L0:
        prologue = [("K", 0, (c,)) for c in range(nch - 1)] + [("Q", 0, (c, None)) for c in range(nch - 1)]
        prologue += [("V", 0, (0, k)) for k in range(KT)]
        plan = Plan(side_jobs0, prologue, ("K", "Q", "V", "OT", "XT"), ("K", "Q", "OT", "OP", "XT"))
    else:
        prologue = [("K", 0, (c,)) for c in range(nch)] + [("Q", 0, (c, None)) for c in range(nch)]
        prologue += [("V", 0, (k,)) for k in range(KT)]
        plan = Plan(side_jobs1, prologue, ("K", "Q", "V", "OT", "XT"), ("K", "OT", "OP", "XT"))

    with ExitStack() as ctx:
        def sb(name, shape, dt=F32):
            return ctx.enter_context(nc.sbuf_tensor(n + name, shape, dt))

        def ps(name):
            return ctx.enter_context(nc.psum_tensor(n + name, [P, 512], F32))

        def parts(name, shape):
            return [sb(f"{name}_{k}", shape, F32R) for k in ("hi", "lo")]

        def sem(name):
            return ctx.enter_context(nc.semaphore(n + name))

        wq, wk, wv, wo = inputs.wq, inputs.wk, inputs.wv, inputs.wo
        ctx_raw, cT, bv_rows, bo_rows = inputs.ctx_raw, inputs.cT, inputs.bv_rows, inputs.bo_rows
        ctx_in, ctx_high, ctx_low = inputs.ctx_in, inputs.ctx_high, inputs.ctx_low
        two = 1 if L0 else 2
        kT = [parts(f"kT{k}", [P, nch, CM]) for k in range(two)]
        V = [sb(f"values{k}", [KR, KT, H, vw]) for k in range(two)]
        probs = [sb(f"probs{k}", [S, KT * KR]) for k in range(4)]
        pT = [sb(f"probsT{k}", [KR, KT, S]) for k in range(4)]
        minus_max = sb("minus_max", [S, 4])
        row_inv = sb("row_inv", [S, H])
        o_rows = sb("o_rows", [S, width])
        oT = parts("oT", [P, nch, S])
        stats = sb("bn_stats", [S, 2, 6])
        mv = sb("mean_var", [S, 2, 2])
        var_eps = sb("var_eps", [S, 2])
        rstd = sb("rstd", [S, 2])
        if L0:
            qT = parts("qT", [P, nch, 2 * S])
            row_sum = sb("row_sum", [S, 2, H])
            xn_bo = sb("xn_plus_bo", [S, D])
            y = xn_bo
            z = sb("z_rows", [S, D])
            gamma, beta = inputs.gamma, inputs.beta
        else:
            y = sb("y_rows", [S, D])
            q_flat = sb("q_flat", [P, nch, 2 * S])
            q_part = parts("q_part", [P, nch, 2 * S])
            qm = [parts(f"q_masked{k}", [P, H, S]) for k in range(2)]
            head_mask = sb("head_mask", [P, hpc])
            mask_rows = [sb(f"mask_rows{k}", [S, SC]) for k in range(2)]
            mask_big = [sb(f"mask_big{k}", [S, SC]) for k in range(2)]
            logits = [sb(f"minus_logits{k}", [S, SC]) for k in range(2)]
        s_ps = [ps(f"ps_scores{k}") for k in range(2)]
        t_ps = [ps(f"ps_probsT{k}") for k in range(2)]
        o_ps = ps("ps_o")
        r_ps = [ps(f"ps_ring{k}") for k in range(RING)]

        pads = sem("pads_written")
        scores, neg_max, exped = sem("scores_done"), sem("max_ready"), sem("probs_ready")
        turned, av = sem("probs_turned"), sem("values_done")
        copied = [sem(f"probsT_copied{k}") for k in range(1 if L0 else 2)]
        o_inv, o_scaled, o_biased = sem("o_inverse"), sem("o_scaled"), sem("o_biased")
        job_done, job_act, job_dve = sem("job_done"), sem("job_act_read"), sem("job_dve_read")
        chain, pool_chain = sem("dve_chain"), sem("pool_chain")
        x_ready, x_stats, x_rstd, xn_ready = sem("x_ready"), sem("x_stats"), sem("x_rstd"), sem("xn_ready")
        if L0:
            scaled, base_norm, base_ready = sem("rows_scaled"), sem("base_norm"), sem("base_ready")
            y_stats, y_rstd, z_ready = sem("y_stats"), sem("y_rstd"), sem("z_ready")
        else:
            mask_in = [sem(f"mask_loaded{k}") for k in range(2)]
            mask_ready, q_high, q_parts, q_masked = (
                sem("mask_ready"), sem("q_high"), sem("q_parts"), sem("q_masked"))

        def G(pair, local, h):
            return 2 * H * pair + H * local + h

        def copied_at(pair, local, h):
            if L0:
                return copied[0], G(pair, local, h) + 1
            k = H * local + h
            return copied[k % 2], H * pair + k // 2 + 1

        def walk(eng, part):
            part("prologue", 0)
            part("first", 0)
            with eng.Fori(1, PAIRS - 1) as i:
                part("middle", i)
            part("last", PAIRS - 1)
            part("tail", PAIRS)

        def steps(name):
            if name == "prologue":
                return []
            return [(local, h) for local in range(1 if name == "tail" else 2) for h in range(H)]

        def lagged(name, local, h, lag):
            k = H * local + h - lag
            if name == "first" and k < 0 or name == "tail" and k >= 0:
                return None
            return (k // H, k % H)

        def xcols(b, m=S):
            return slice(b * S, b * S + m) if isinstance(b, int) else bass.ds(b * S, m)

        def brow(b):
            return t.x[:, b, :] if isinstance(b, int) else t.x[:, bass.ds(b, 1), :].rearrange("s a d -> s (a d)")

        def prev_of(name, pair, local):
            return None if name == "first" and local == 0 else 2 * pair + local - 1

        n_pads = 2 * 2 + 4 + (0 if L0 else 2)
        block = ctx.enter_context(nc.Block())

        @block.sync
        def _(sp):
            def load_context(b):
                wait(sp, ctx_high, b)
                wait(sp, ctx_low, b)
                src = dram["ctxT"][b] if isinstance(b, int) else \
                    dram["ctxT"][bass.ds(b, 1)].rearrange("a d s -> (a d) s")
                sp.dma_start(ctx_raw[:], src.rearrange("(c p) s -> p c s", p=P)).then_inc(ctx_in, 16)

            def load_mask(b, k):
                wait(sp, mask_ready, b - 1)
                src = dram["mask"][b:b + 1, :] if isinstance(b, int) else dram["mask"][bass.ds(b, 1), :]
                sp.dma_start(mask_rows[k][:], src.to_broadcast([S, SC])).then_inc(mask_in[k], 16)

            load_context(1)
            if not L0:
                load_mask(0, 0)
                load_mask(1, 1)
            with sp.Fori(1, PAIRS) as i:
                for k in range(2):
                    load_context(2 * i + k)
                    if not L0:
                        load_mask(2 * i + k, k)

        @block.tensor
        def _(pe):
            def job(name, pair, j):
                b = 2 * pair + j.batch
                bank, old = r_ps[j.n % RING], plan.before(j)
                if old is not None:
                    who = "dve" if old.kind in plan.kinds["dve"] else "act"
                    pe.wait_ge({"act": job_act, "dve": job_dve}[who], plan.count(name, pair, old, who))
                c_parts = cT[j.batch % 2]
                if j.kind in "KV":
                    pe.wait_ge(ctx_low, b + 1)
                if j.kind == "K":
                    (c,) = j.args
                    for d in range(DC):
                        ins = three_pass(pe, bank[:, 0:CM], [w[:, d, c * P:(c + 1) * P] for w in wk],
                                         [x[:, d, 0:CM] for x in c_parts], d == 0, d == DC - 1)
                elif j.kind == "V":
                    k = j.args[-1]
                    at, m = (j.args[0] * 512, 512) if L0 else (0, width)
                    for d in range(DC):
                        ins = three_pass(pe, bank[0:KR, 0:m], [x[:, d, k * KR:(k + 1) * KR] for x in c_parts],
                                         [w[:, d, at:at + m] for w in wv], d == 0, d == DC - 1)
                elif j.kind == "Q":
                    c, half = j.args
                    m = 2 * S if half is None else S
                    cols = xcols(b + (half or 0), m)
                    for d in range(DC):
                        ins = three_pass(pe, bank[:, 0:m], [w[:, d, c * P:(c + 1) * P] for w in wq],
                                         [x[:, d, cols] for x in t.xT], d == 0, d == DC - 1)
                elif j.kind == "OT":
                    c0, m = (4 * j.args[0], 4) if L0 else (0, DC)
                    pe.wait_ge(o_biased, o_per * b + j.args[0] + 1)
                    for c in range(m):
                        ins = pe.transpose(bank[:, c * S:(c + 1) * S],
                                           o_rows[:, (c0 + c) * P:(c0 + c + 1) * P], t.ident[0:S, 0:S])
                elif j.kind == "OP":
                    ot = plan.latest(name, j, "OT")
                    if plan.jobs.index(ot) > plan.jobs.index(old):
                        pe.wait_ge(job_dve, plan.count(name, pair, ot, "dve"))
                    for c in range(nch):
                        ins = three_pass(pe, bank[0:S, 0:D], [o[:, c, :] for o in oT],
                                         [w[:, c, :] for w in wo], c == 0, c == nch - 1)
                elif j.kind == "XT":
                    pe.wait_ge(xn_ready, b + 1)
                    for c in range(DC):
                        ins = pe.transpose(bank[:, c * S:(c + 1) * S], t.xn[:, c * P:(c + 1) * P],
                                           t.ident[0:S, 0:S])
                ins.then_inc(job_done, 1)

            def scores_of(name, pair, local, h):
                c, g = h // hpc, G(pair, local, h)
                if h % hpc == 0:
                    k_job = plan.latest(name, (local, h), "K", c)
                    pe.wait_ge(job_dve, plan.count(name, pair, k_job, "dve"))
                    if L0:
                        q_job = plan.latest(name, (local, h), "Q", c)
                        pe.wait_ge(job_dve, plan.count(name, pair, q_job, "dve"))
                    else:
                        pe.wait_ge(q_masked, 2 * nch * pair + nch * local + c + 1)
                wait(pe, exped if L0 else neg_max, g - 1)
                if L0:
                    rows = slice(DK0 * (h % hpc), DK0 * (h % hpc + 1))
                    q = [x[rows, c, local * S:(local + 1) * S] for x in qT]
                    k = [x[rows, c, :] for x in kT[0]]
                else:
                    q = [x[:, h, :] for x in qm[local]]
                    k = [x[:, c, :] for x in kT[local]]
                three_pass(pe, s_ps[h % 2][0:S, 0:CM], q, k, True, True).then_inc(scores, 1)

            def turn(name, pair, local, h):
                pe.wait_ge(exped, G(pair, local, h) + 1)
                back = lagged(name, local, h, 2)
                if back is not None:
                    pe.wait_ge(*copied_at(pair, *back))
                for k in range(KT):
                    ins = pe.transpose(t_ps[h % 2][0:KR, k * S:(k + 1) * S],
                                       probs[h % 4][:, k * KR:(k + 1) * KR], t.ident[0:S, 0:S])
                ins.then_inc(turned, 1)

            def values(name, pair, local, h):
                pe.wait_ge(*copied_at(pair, local, h))
                if h % hpo == 0:
                    wait(pe, o_scaled, o_per * (2 * pair + local) + h // hpo)
                if h == 0 or L0 and h == 8:
                    v_job = plan.latest(name, (local, h), "V", *((h // 8, KT - 1) if L0 else (KT - 1,)))
                    pe.wait_ge(job_act, plan.count(name, pair, v_job, "act"))
                v = V[0] if L0 else V[local % 2]
                at = (h % hpo) * vw
                for k in range(KT):
                    ins = pe.matmul(o_ps[0:S, at:at + vw], pT[h % 4][:, k, :], v[:, k, h, :],
                                    start=k == 0, stop=k == KT - 1)
                ins.then_inc(av, 1)

            pe.wait_ge(pads, n_pads)

            def part(name, pair):
                for j in plan.of(name) if name == "prologue" else ():
                    job(name, pair, j)
                for local, h in steps(name):
                    if name != "tail":
                        scores_of(name, pair, local, h)
                    if (back := lagged(name, local, h, LAG_T)) is not None:
                        turn(name, pair, *back)
                    for j in plan.of(name, (local, h)):
                        job(name, pair, j)
                    if (back := lagged(name, local, h, LAG_V)) is not None:
                        values(name, pair, *back)

            walk(pe, part)

        @block.gpsimd
        def _(pool):
            for k in range(2):
                for x in cT[k]:
                    pool.memset(x[:, :, SC:CW].bitcast(F32), 0.0).then_inc(pads, 1)
            for k in range(4):
                pool.memset(probs[k][:, SC:KT * KR], 0.0).then_inc(pads, 1)
            if not L0:
                for v in V:
                    pool.memset(v[:, :, :, dv:vw], 1.0).then_inc(pads, 1)
                pool.memset(head_mask[:], 1.0).then_inc(pool_chain, 1)
                pool.wait_ge(pool_chain, 1)
                pool.affine_select(out=head_mask[:], in_=head_mask[:], compare_op=ALU.is_ge, fill=0.0, base=0,
                                   pattern=[[-dv, hpc]], channel_multiplier=1).then_inc(pool_chain, 1)
                pool.wait_ge(pool_chain, 2)
                pool.affine_select(out=head_mask[:], in_=head_mask[:], compare_op=ALU.is_ge, fill=0.0,
                                   base=dv - 1, pattern=[[dv, hpc]], channel_multiplier=-1).then_inc(pool_chain, 1)
                pool.wait_ge(pool_chain, 3)
            if L0:
                pool.tensor_scalar(gamma[:], gamma[:], t.tanh_g[:, 0:1], None, ALU.mult).then_inc(scaled, 1)
                pool.tensor_scalar(beta[:], beta[:], t.tanh_g[:, 0:1], None, ALU.mult).then_inc(scaled, 1)
                pool.wait_ge(scaled, 2)
            base = 0 if L0 else 3

            def split_low(b, k):
                pool.wait_ge(ctx_high, b + 1)
                pool.tensor_tensor(cT[k][1][:, :, 0:SC], ctx_raw[:], cT[k][0][:, :, 0:SC].bitcast(F32),
                                   ALU.subtract).then_inc(ctx_low, 1)

            def inverse_root(k, stats_sem, out_sem, b, links):
                wait_apart(pool, (stats_sem, b + 1))
                pool.tensor_scalar(var_eps[:, k:k + 1], mv[:, k, 1:2], LN_EPS, None, ALU.add).then_inc(pool_chain, 1)
                pool.wait_ge(pool_chain, links + 1)
                pool.tensor_tensor(rstd[:, k:k + 1], var_eps[:, k:k + 1], t.minus_half[:, 0:1],
                                   ALU.pow).then_inc(out_sem, 1)

            def add_bv(pair, local, half):
                cols = slice(half * 512, half * 512 + 512) if L0 else slice(0, width)
                pool.wait_ge(o_scaled, o_per * (2 * pair + local) + half + 1)
                pool.tensor_tensor(o_rows[:, cols], o_rows[:, cols], bv_rows[:, cols], ALU.add).then_inc(o_biased, 1)

            def mask_queries(pair, local):
                for c in range(nch):
                    pool.wait_ge(q_parts, nch * pair + c + 1)
                    wait(pool, scores, G(pair, local, 0) - H)
                    for k in range(2):
                        src = q_part[k][:, c, local * S:(local + 1) * S].bitcast(F32)
                        ins = pool.tensor_tensor(
                            qm[local][k][:, c * hpc:(c + 1) * hpc, :],
                            src[:, None, :].to_broadcast([P, hpc, S]),
                            head_mask[:, :, None].to_broadcast([P, hpc, S]), ALU.mult)
                    ins.then_inc(q_masked, 1)

            def enlarge_mask(b, k, loads):
                wait_apart(pool, (mask_in[k], 16 * loads), (neg_max, H * (b - 1)))
                pool.tensor_scalar(mask_big[k][:], mask_rows[k][:], 1e9, None, ALU.mult).then_inc(mask_ready, 1)

            def part(name, pair):
                if name == "prologue":
                    split_low(1, 1)
                    if not L0:
                        enlarge_mask(0, 0, 1)
                        mask_queries(0, 0)
                        mask_queries(0, 1)
                    return
                for local, h in steps(name):
                    b = 2 * pair + local
                    p = prev_of(name, pair, local)
                    if h == (3 if L0 else 3) and p is not None:
                        add_bv(pair, local - 1, o_per - 1)
                    if L0 and h == 6 and p is not None:
                        pool.wait_ge(base_norm, p + 1)
                        pool.tensor_tensor(xn_bo[:], xn_bo[:], bo_rows[:], ALU.add).then_inc(base_ready, 1)
                    if L0 and h == 10 and p is not None:
                        inverse_root(0, y_stats, y_rstd, p, base + 4 * p)
                    if L0 and h == 11 and name != "tail":
                        add_bv(pair, local, 0)
                    if L0 and h == 11 and p is not None:
                        pool.wait_ge(z_ready, p + 1)
                        pool.tensor_tensor(z[:], z[:], gamma[:], ALU.mult).then_inc(pool_chain, 1)
                        pool.wait_ge(pool_chain, base + 4 * p + 2)
                        pool.tensor_tensor(z[:], z[:], beta[:], ALU.add).then_inc(pool_chain, 1)
                        pool.wait_ge(pool_chain, base + 4 * p + 3)
                        pool.tensor_tensor(brow(p), brow(p), z[:], ALU.add).then_inc(x_ready, 1)
                    if h == (12 if L0 else 11) and p is not None:
                        inverse_root(1, x_stats, x_rstd, p, base + 4 * p + 3 if L0 else base + p)
                    if name != "tail" and not L0:
                        if h == 5 and local == 1 and name != "last":
                            mask_queries(pair + 1, 0)
                        if h == 5 and local == 0 and name != "first":
                            mask_queries(pair, 1)
                        if h == 8 and not (name == "last" and local == 1):
                            enlarge_mask(b + 1, 1 - local, pair + 1 + local)
                    if h == 14 and name not in ("last", "tail"):
                        split_low(b + 2, local)

            walk(pool, part)

        @block.scalar
        def _(act):
            biases = {"K": t.bias[:, slice(*span(f"bk{layer}"))], "Q": t.bq0s if L0 else t.bq1s}

            def split_high(b, k):
                act.wait_ge(ctx_in, 16 * (b + 1))
                if not isinstance(b, int) or b >= 2:
                    act.wait_ge(scores, H * (b - 2) + 9)
                act.copy(cT[k][0][:, :, 0:SC], ctx_raw[:]).then_inc(ctx_high, 1)

            def probabilities(name, pair, local, h):
                g = G(pair, local, h)
                act.wait_ge(neg_max, g + 1)
                wait(act, turned, g - 3)
                if L0:
                    act.activation(probs[h % 4][:, 0:SC], s_ps[h % 2][0:S, 0:SC], ACT.Exp,
                                   bias=minus_max[:, h % 4:h % 4 + 1],
                                   accum_out=row_sum[:, local, h:h + 1]).then_inc(exped, 1)
                else:
                    act.activation(probs[h % 4][:, 0:SC], logits[h % 2][:], ACT.Exp,
                                   bias=minus_max[:, h % 4:h % 4 + 1], scale=-1.0).then_inc(exped, 1)

            def copy_turned(pair, local, h):
                g = G(pair, local, h)
                act.wait_ge(turned, g + 1)
                wait(act, av, g - 3)
                act.copy(pT[h % 4][:], t_ps[h % 2][0:KR, 0:KT * S].rearrange("k (t s) -> k t s", s=S))\
                   .then_inc(copied[1], 1)

            def read(name, pair, j):
                b = 2 * pair + j.batch
                if j.kind not in plan.kinds["act"]:
                    return
                bank = r_ps[j.n % RING]
                act.wait_ge(job_done, plan.number(name, pair, j))
                if j.kind == "K":
                    (c,) = j.args
                    ins = act.activation(kT[0 if L0 else j.batch % 2][0][:, c, :], bank[:, 0:CM], ACT.Identity,
                                         bias=biases["K"][:, c:c + 1])
                elif j.kind == "Q":
                    c, half = j.args
                    m = 2 * S if half is None else S
                    at = S * (half or 0)
                    if not L0:
                        wait(act, q_parts, nch * (pair + int(j.batch == 2) - 1) + c + 1)
                    to = (qT[0] if L0 else q_flat)[:, c, at:at + m]
                    ins = act.activation(to, bank[:, 0:m], ACT.Identity, bias=biases["Q"][:, c:c + 1])
                elif j.kind == "V":
                    k = j.args[-1]
                    h0, m = (8 * j.args[0], 8) if L0 else (0, H)
                    ins = act.copy(V[0 if L0 else j.batch % 2][:, k, h0:h0 + m, 0:dv],
                                   bank[0:KR, 0:m * dv].rearrange("k (h v) -> k h v", v=dv))
                elif j.kind == "OT":
                    c0, m = (4 * j.args[0], 4) if L0 else (0, DC)
                    ins = act.copy(oT[0][:, c0:c0 + m, :], bank[:, 0:m * S].rearrange("p (c s) -> p c s", s=S))
                elif j.kind == "XT":
                    ins = act.copy(t.xT[0][:, :, xcols(b)], bank[:, 0:DC * S].rearrange("p (c s) -> p c s", s=S))
                ins.then_inc(job_act, 1)

            def part(name, pair):
                if name == "prologue":
                    split_high(1, 1)
                    for j in plan.of(name):
                        read(name, pair, j)
                    return
                for local, h in steps(name):
                    back = lagged(name, local, h, LAG_T)
                    if not L0 and back is not None and back[1] % 2:
                        copy_turned(pair, *back)
                    if name != "tail":
                        probabilities(name, pair, local, h)
                    for j in plan.of(name, (local, h)):
                        read(name, pair, j)
                    if h == 14 and name not in ("last", "tail"):
                        split_high(2 * pair + local + 2, local)

            walk(act, part)

        @block.vector
        def _(dve):
            biases = {"K": t.bias[:, slice(*span(f"bk{layer}"))], "Q": t.bq0s if L0 else t.bq1s}
            CH = 2 if L0 else 1

            def link(ins, b, k):
                ins.then_inc(chain, 1)
                wait_apart(dve, (chain, CH * b + k + 1))

            def maximum(name, pair, local, h):
                g = G(pair, local, h)
                if L0:
                    dve.wait_ge(scores, g + 1)
                    wait(dve, exped, g - 3)
                    ins = dve.tensor_reduce(minus_max[:, h % 4:h % 4 + 1], s_ps[h % 2][0:S, 0:SC], AX.X, ALU.max,
                                            negate=True)
                else:
                    wait_apart(dve, (scores, g + 1), (exped, g - 1),
                               *([(mask_ready, 2 * pair + local + 1)] if h == 0 else []))
                    ins = dve.tensor_tensor_reduce(logits[h % 2][:], s_ps[h % 2][0:S, 0:SC], mask_big[local][:],
                                                   1.0, 3.0e38, ALU.add, ALU.min, minus_max[:, h % 4:h % 4 + 1])
                ins.then_inc(neg_max, 1)

            def copy_turned(pair, local, h):
                g = G(pair, local, h)
                dve.wait_ge(turned, g + 1)
                wait(dve, av, g - 3)
                dve.tensor_copy(pT[h % 4][:], t_ps[h % 2][0:KR, 0:KT * S].rearrange("k (t s) -> k t s", s=S))\
                   .then_inc(copied[0], 1)

            def scale_o(pair, local, half):
                m, b = hpo, 2 * pair + local
                dve.wait_ge(av, H * b + hpo * (half + 1))
                wait(dve, o_scaled, o_per * b + half)
                o = o_ps[0:S, 0:m * vw].rearrange("s (h v) -> s h v", v=vw)
                sums = row_sum[:, local % 2, half * m:(half + 1) * m] if L0 else o[:, :, dv]
                dve.reciprocal(row_inv[:, 0:m], sums).then_inc(o_inv, 1)
                dve.wait_ge(o_inv, o_per * b + half + 1)
                to = o_rows[:, half * m * dv:(half + 1) * m * dv].rearrange("s (h v) -> s h v", v=dv)
                dve.tensor_tensor(to, o[:, :, 0:dv], row_inv[:, 0:m, None].to_broadcast([S, m, dv]),
                                  ALU.mult).then_inc(o_scaled, 1)

            def read(name, pair, j):
                b = 2 * pair + j.batch
                bank = r_ps[j.n % RING]
                if j.kind == "Q" and not L0:
                    c = j.args[0]
                    k = nch * (pair + int(j.batch == 2)) + c
                    dve.wait_ge(job_act, plan.count(name, pair, j, "act"))
                    wait(dve, q_masked, 2 * nch * (pair + int(j.batch == 2)))
                    dve.tensor_copy(q_part[0][:, c, :], q_flat[:, c, :]).then_inc(q_high, 1)
                    dve.wait_ge(q_high, k + 1)
                    dve.tensor_tensor(q_part[1][:, c, :], q_flat[:, c, :], q_part[0][:, c, :].bitcast(F32),
                                      ALU.subtract).then_inc(q_parts, 1)
                    return
                if j.kind not in plan.kinds["dve"]:
                    return
                if j.kind == "OP":
                    dve.wait_ge(job_done, plan.number(name, pair, j))
                else:
                    dve.wait_ge(job_act, plan.count(name, pair, j, "act"))
                if j.kind == "K":
                    (c,) = j.args
                    k = kT[0 if L0 else j.batch % 2]
                    ins = dve.scalar_tensor_tensor(out=k[1][:, c, :], in0=bank[:, 0:CM],
                                                   scalar=biases["K"][:, c:c + 1], in1=k[0][:, c, :].bitcast(F32),
                                                   op0=ALU.add, op1=ALU.subtract)
                elif j.kind == "Q":
                    c, half = j.args
                    m = 2 * S if half is None else S
                    at = S * (half or 0)
                    ins = dve.scalar_tensor_tensor(out=qT[1][:, c, at:at + m], in0=bank[:, 0:m],
                                                   scalar=biases["Q"][:, c:c + 1],
                                                   in1=qT[0][:, c, at:at + m].bitcast(F32),
                                                   op0=ALU.add, op1=ALU.subtract)
                elif j.kind == "OT":
                    c0, m = (4 * j.args[0], 4) if L0 else (0, DC)
                    ins = dve.tensor_tensor(oT[1][:, c0:c0 + m, :],
                                            bank[:, 0:m * S].rearrange("p (c s) -> p c s", s=S),
                                            oT[0][:, c0:c0 + m, :].bitcast(F32), ALU.subtract)
                elif j.kind == "OP":
                    if L0:
                        dve.wait_ge(base_ready, b + 1)
                    ins = dve.tensor_tensor(y[:], bank[0:S, 0:D], (xn_bo if L0 else bo_rows)[:], ALU.add)
                    ins.then_inc(job_dve, 1)
                    dve.wait_ge(job_dve, plan.count(name, pair, j, "dve"))
                    if not L0:
                        dve.scalar_tensor_tensor(out=brow(b), in0=y[:], scalar=t.tanh_g[:, 1:2], in1=brow(b),
                                                 op0=ALU.mult, op1=ALU.add).then_inc(x_ready, 1)
                    return
                elif j.kind == "XT":
                    ins = dve.tensor_tensor(t.xT[1][:, :, xcols(b)],
                                            bank[:, 0:DC * S].rearrange("p (c s) -> p c s", s=S),
                                            t.xT[0][:, :, xcols(b)].bitcast(F32), ALU.subtract)
                ins.then_inc(job_dve, 1)

            def mean_var(k, rows, b, at, out):
                link(dve.bn_stats(stats[:, k, :], rows), b, at)
                dve.bn_aggr(mv[:, k, :], stats[:, k, :]).then_inc(out, 1)

            def part(name, pair):
                if name == "prologue":
                    for j in plan.of(name):
                        read(name, pair, j)
                    return
                for local, h in steps(name):
                    p = prev_of(name, pair, local)
                    if name != "tail":
                        maximum(name, pair, local, h)
                    back = lagged(name, local, h, LAG_T)
                    if back is not None and (L0 or back[1] % 2 == 0):
                        copy_turned(pair, *back)
                    if (back := lagged(name, local, h, LAG_V + 1)) is not None and back[1] % hpo == hpo - 1:
                        scale_o(pair, back[0], back[1] // hpo)
                    if p is not None:
                        if L0 and h == 5:
                            m = t.mv0[:, p, 0:1] if isinstance(p, int) else \
                                t.mv0[:, bass.ds(p, 1), 0:1].rearrange("s a c -> s (a c)")
                            r = t.rstd0[:, p:p + 1] if isinstance(p, int) else t.rstd0[:, bass.ds(p, 1)]
                            dve.tensor_scalar(xn_bo[:], brow(p), m, r, ALU.subtract, ALU.mult)\
                               .then_inc(base_norm, 1)
                        if L0 and h == 10:
                            mean_var(0, y[:], p, 0, y_stats)
                        if L0 and h == 11:
                            dve.wait_ge(y_rstd, p + 1)
                            dve.tensor_scalar(z[:], y[:], mv[:, 0, 0:1], rstd[:, 0:1], ALU.subtract, ALU.mult)\
                               .then_inc(z_ready, 1)
                        if h == (12 if L0 else 11):
                            wait_apart(dve, (x_ready, p + 1))
                            mean_var(1, brow(p), p, 1 if L0 else 0, x_stats)
                        if h == 13:
                            dve.wait_ge(x_rstd, p + 1)
                            dve.tensor_scalar(t.xn[:], brow(p), mv[:, 1, 0:1], rstd[:, 1:2],
                                              ALU.subtract, ALU.mult).then_inc(xn_ready, 1)
                    for j in plan.of(name, (local, h)):
                        read(name, pair, j)

            walk(dve, part)


class Router:

    LAST = 8

    def __init__(self, nc, ctx, t, dram, layer, banks):
        def sb(name, shape, dt=F32):
            return ctx.enter_context(nc.sbuf_tensor(n + name, shape, dt))

        def sem(name):
            return ctx.enter_context(nc.semaphore(n + name))

        n = f"r{layer}_"
        self.t, self.dram, self.layer, self.banks = t, dram, layer, banks
        self.nr = nr = NR if layer == 0 else E
        self.w_raw = sb("w_raw", [P, DC, nr])
        self.w = [sb(f"w_{k}", [P, DC, nr], F32R) for k in ("hi", "lo")]
        self.bias = sb("bias_rows", [S, nr])
        self.logitT = sb("logitT", [nr, NTOK])
        self.logit = sb("logit", [S, B, nr])
        self.prob = sb("prob", [S, B, E])
        self.lang = sb("lang", [S, B, 4])
        self.mix = sb("mix", [S, B, 4])
        self.one = sb("one_per_token", [S, B])
        self.inv = sb("inverse", [S, B])
        self.top = sb("top8", [S, B, E])
        self.index = sb("index", [S, B, E], U32)
        self.index_f = sb("index_f", [S, B, 2])
        self.iota = sb("iota", [S, E])
        self.hit = [sb(f"hit{k}", [S, B, E]) for k in range(2)]
        self.gates = sb("gates", [S, B, E])
        self.w_in, self.w_split, self.chain = sem("w_loaded"), sem("w_split"), sem("dve_chain")
        self.logits_done, self.logits_read, self.logit_turned = (
            sem("logits_done"), sem("logits_read"), sem("logit_turned"))
        self.ask_exp, self.exp_done = sem("ask_exp"), sem("exp_done")
        self.gates_ready, self.gates_turned, self.gatesT_ready, self.gates_out = (
            sem("gates_ready"), sem("gates_turned"), sem("gatesT_ready"), sem("gates_stored"))
        self.links = 0

    def load(self, sp):
        sp.dma_start(self.w_raw[:], self.dram[f"router{self.layer}"].rearrange("(c p) e -> p c e", p=P))\
            .then_inc(self.w_in, 16)
        if self.layer == 0:
            sp.dma_start(self.bias[:], self.dram["router_bias"].to_broadcast([S, self.nr]))\
                .then_inc(self.w_in, 16)

    def store_gates(self, sp):
        sp.wait_ge(self.gatesT_ready, NTC)
        sp.dma_start(self.dram["gates"], self.t.gatesT[:]).then_inc(self.gates_out, 16)
        sp.wait_ge(self.gates_out, 16)

    def logits(self, pe):
        pe.wait_ge(self.w_split, 2)
        for c in range(NTC):
            if c >= 2:
                pe.wait_ge(self.logits_read, c - 1)
            for d in range(DC):
                ins = three_pass(pe, self.banks[c % 2][0:self.nr, 0:TC], [x[:, d, :] for x in self.w],
                                 [x[:, d, c * TC:(c + 1) * TC] for x in self.t.xT], d == 0, d == DC - 1)
            ins.then_inc(self.logits_done, 1)

    def turn_logits(self, pe):
        pe.wait_ge(self.logits_read, NTC)
        for b in range(B):
            ins = pe.transpose(self.banks[0][0:S, b * self.nr:(b + 1) * self.nr],
                               self.logitT[:, b * S:(b + 1) * S], self.t.ident[0:self.nr, 0:self.nr])
        ins.then_inc(self.logit_turned, 1)

    def turn_gates(self, pe, chunks):
        pe.wait_ge(self.gates_ready, 1)
        for c in chunks:
            if c >= 2:
                pe.wait_ge(self.gatesT_ready, c - 1)
            for j in range(BPC):
                ins = pe.transpose(self.banks[c % 2][0:E, j * S:(j + 1) * S], self.gates[:, BPC * c + j, :],
                                   self.t.ident[0:S, 0:S])
            ins.then_inc(self.gates_turned, 1)

    def exponents(self, act, k):
        act.wait_ge(self.ask_exp, k + 1)
        x = self.lang if self.layer == 0 and k == 0 else self.prob
        act.activation(x[:], x[:], ACT.Exp).then_inc(self.exp_done, 1)

    def split_weights(self, dve):
        for e in range(E):
            ins = dve.memset(self.iota[:, e:e + 1], float(e))
        self.link(dve, ins)
        dve.wait_ge(self.w_in, 32 if self.layer == 0 else 16)
        dve.tensor_copy(self.w[0][:], self.w_raw[:]).then_inc(self.w_split, 1)
        dve.wait_ge(self.w_split, 1)
        dve.tensor_tensor(self.w[1][:], self.w_raw[:], self.w[0][:].bitcast(F32), ALU.subtract)\
            .then_inc(self.w_split, 1)

    def copy_logits(self, dve):
        for c in range(NTC):
            dve.wait_ge(self.logits_done, c + 1)
            dve.tensor_copy(self.logitT[:, c * TC:(c + 1) * TC], self.banks[c % 2][0:self.nr, 0:TC])\
                .then_inc(self.logits_read, 1)

    def copy_gates(self, dve, chunks):
        for c in chunks:
            dve.wait_ge(self.gates_turned, c + 1)
            dve.tensor_copy(self.t.gatesT[:, c * TC:(c + 1) * TC], self.banks[c % 2][0:E, 0:TC])\
                .then_inc(self.gatesT_ready, 1)

    def link(self, dve, ins):
        ins.then_inc(self.chain, 1)
        self.links += 1
        dve.wait_ge(self.chain, self.links)

    def softmax_start(self, dve, to, x, m):
        self.link(dve, dve.tensor_reduce(self.one[:], x, AX.X, ALU.max))
        dve.tensor_tensor(to, x, self.per_token(self.one, m), ALU.subtract).then_inc(self.ask_exp, 1)

    def softmax_end(self, dve, x, m, k):
        dve.wait_ge(self.exp_done, k + 1)
        self.link(dve, dve.tensor_reduce(self.one[:], x, AX.X, ALU.add))
        self.link(dve, dve.reciprocal(self.inv[:], self.one[:]))
        self.link(dve, dve.tensor_tensor(x, x, self.per_token(self.inv, m), ALU.mult))

    @staticmethod
    def per_token(x, m):
        return x[:, :, None].to_broadcast([S, B, m])

    def stage(self, dve, k):
        L0, logit, mix, lang, prob, top = self.layer == 0, self.logit, self.mix, self.lang, self.prob, self.top
        turned = self.banks[0][0:S, 0:B * self.nr].rearrange("s (b e) -> s b e", e=self.nr)
        if k == 0:
            dve.wait_ge(self.logit_turned, 1)
            if L0:
                self.link(dve, dve.tensor_tensor(
                    logit[:], turned, self.bias[:, None, :].to_broadcast([S, B, self.nr]), ALU.add))
                self.softmax_start(dve, lang[:], logit[:, :, E:NR], 4)
            else:
                self.link(dve, dve.tensor_copy(logit[:], turned))
        if L0 and k == 1:
            self.softmax_end(dve, lang[:], 4, 0)
            self.link(dve, dve.tensor_tensor(mix[:, :, 0:3], lang[:, :, 0:3], lang[:, :, 1:4], ALU.add))
            self.link(dve, dve.tensor_copy(mix[:, :, 3:4], lang[:, :, 3:4]))
        if k == 2:
            if L0:
                for e in range(0, E, 4):
                    ins = dve.scalar_tensor_tensor(out=logit[:, :, e:e + 4], in0=mix[:], scalar=0.1,
                                                   in1=logit[:, :, e:e + 4], op0=ALU.mult, op1=ALU.add)
                self.link(dve, ins)
            self.softmax_start(dve, prob[:], logit[:, :, 0:E], E)
        if k == 3:
            self.softmax_end(dve, prob[:], E, 1 if L0 else 0)
        if k == 4:
            for b in range(B):
                ins = dve.max(top[:, b, :], prob[:, b, :])
            self.link(dve, ins)
        if k == 5:
            for b in range(B):
                ins = dve.max_index(self.index[:, b, :], top[:, b, :], prob[:, b, :])
            self.link(dve, ins)
        if k == 6:
            dve.tensor_copy(self.index_f[:], self.index[:, :, 0:2])
            self.link(dve, dve.tensor_tensor(self.one[:], top[:, :, 0], top[:, :, 1], ALU.add))
            if not L0:
                self.link(dve, dve.tensor_scalar(self.one[:], self.one[:], 1e-20, None, ALU.add))
            self.link(dve, dve.reciprocal(self.inv[:], self.one[:]))
        if k == 7:
            dve.tensor_tensor(top[:, :, 0:2], top[:, :, 0:2], self.per_token(self.inv, 2), ALU.mult)
            for i in range(2):
                ins = dve.tensor_tensor(self.hit[i][:], self.iota[:, None, :].to_broadcast([S, B, E]),
                                        self.per_token(self.index_f[:, :, i], E), ALU.is_equal)
            self.link(dve, ins)
        if k == 8:
            for i in range(2):
                ins = dve.tensor_tensor(self.hit[i][:], self.hit[i][:], self.per_token(top[:, :, i], E), ALU.mult)
            self.link(dve, ins)
            dve.tensor_tensor(self.gates[:], self.hit[0][:], self.hit[1][:], ALU.add).then_inc(self.gates_ready, 1)


LAG_Y = 2


def experts0(nc, t, dram):
    STEPS = NTC * HC0
    n = "e0_"
    with ExitStack() as ctx:
        def sb(name, shape, dt=F32):
            return ctx.enter_context(nc.sbuf_tensor(n + name, shape, dt))

        def ps(name):
            return ctx.enter_context(nc.psum_tensor(n + name, [P, 512], F32))

        def sem(name):
            return ctx.enter_context(nc.semaphore(n + name))

        w1 = [[sb(f"w1_{k}{p}", [P, DC, HID0], F32R) for p in ("hi", "lo")] for k in range(2)]
        w2 = [[sb(f"w2_{k}{p}", [P, HC0, D], F32R) for p in ("hi", "lo")] for k in range(2)]
        raw = [sb(f"w_raw{k}", [P, 1024]) for k in range(4)]
        b2 = sb("b2_rows", [E, D])
        gate = [sb(f"gate{k}", [P, NTOK]) for k in range(2)]
        h = [sb(f"hidden{k}", [P, TC]) for k in range(4)]
        h_parts = [[sb(f"hidden{k}{p}", [P, TC], F32R) for p in ("hi", "lo")] for k in range(4)]
        gated = [sb(f"gated{k}", [P, TC]) for k in range(DC)]
        h_ps = [ps(f"ps_hidden{k}") for k in range(2)]
        spare = [ps(f"ps_spare{k}") for k in range(2)]
        y_ps = [[ps(f"ps_y{k}{d}") for d in range(DC)] for k in range(2)]
        raw_in = [sem(f"raw_in{k}") for k in range(4)]
        w_high, w_low, b2_in = sem("w_high"), sem("w_low"), sem("b2_loaded")
        gate_in = [sem(f"gate_loaded{k}") for k in range(2)]
        init_done, init_read = sem("init_done"), sem("init_read")
        hidden, activated, high, split = sem("hidden_done"), sem("activated"), sem("hidden_high"), sem("hidden_split")
        y_done, y_read, summed = sem("y_done"), sem("y_read"), sem("summed")
        router = Router(nc, ctx, t, dram, 0, spare)
        block = ctx.enter_context(nc.Block())
        STAGE_AT = {0: 0, 2: 1, 3: 2, 5: 3, 6: 4, 7: 5, 8: 6, 9: 7, 10: 8}
        EXP_AT = {1: 0, 4: 1}
        TURN_AT, COPY_AT = {11: (0, 1), 12: (2, 3)}, {12: (0, 1), 13: (2, 3)}
        INIT_AT = {14 + c: c for c in range(NTC)}

        def walk(eng, part):
            part("first", 0)
            with eng.Fori(1, E // 2 - 1) as i:
                part("middle", i)
            part("last", E // 2 - 1)
            part("tail", E // 2)

        def steps(name):
            return [(e, c, k) for e in range(2) for c in range(NTC) for k in range(HC0)]

        def step_no(pair, e, c, k):
            return 2 * STEPS * pair + STEPS * e + HC0 * c + k

        @block.sync
        def _(sp):
            def load(e, k):
                wait(sp, w_low, 4 * e + k - 3)
                e_ = slice(e, e + 1) if isinstance(e, int) else bass.ds(e, 1)
                if k < 2:
                    sp.dma_start(raw[k][:], dram["L0_ffn_w1"][e_, k * P:(k + 1) * P, :]
                                 .rearrange("a p n -> (a p) n")).then_inc(raw_in[k], 16)
                else:
                    rows = slice((k - 2) * 4 * P, (k - 1) * 4 * P)
                    sp.dma_start(raw[k][:].rearrange("p (c d) -> p c d", d=D),
                                 dram["L0_ffn_w2"][e_, rows, :].rearrange("a (c p) d -> p (a c) d", p=P))\
                        .then_inc(raw_in[k], 16)

            def load_gate(e, slot):
                wait(sp, y_read, NTC * (e - 1))
                src = dram["gates"][e:e + 1, :] if isinstance(e, int) else dram["gates"][bass.ds(e, 1), :]
                sp.dma_start(gate[slot][:], src.to_broadcast([P, NTOK])).then_inc(gate_in[slot], 16)

            router.load(sp)
            for k in range(4):
                load(0, k)
            sp.dma_start(b2[:], dram["L0_ffn_b2"]).then_inc(b2_in, 16)
            for k in range(4):
                load(1, k)
            router.store_gates(sp)
            load_gate(0, 0)
            load_gate(1, 1)
            with sp.Fori(1, E // 2) as i:
                for e in range(2):
                    load_gate(2 * i + e, e)
                    for k in range(4):
                        load(2 * i + e, k)

        def w_piece(slot, k):
            return [x[:, k, :] for x in w1[slot]] if k < 2 else [x[:, (k - 2) * 4:(k - 1) * 4, :] for x in w2[slot]]

        def raw_piece(k):
            return raw[k][:] if k < 2 else raw[k][:].rearrange("p (c d) -> p c d", d=D)

        @block.gpsimd
        def _(pool):
            def low(e, slot, k):
                pool.wait_ge(w_high, 4 * e + k + 1)
                to = w_piece(slot, k)
                pool.tensor_tensor(to[1], raw_piece(k), to[0].bitcast(F32), ALU.subtract).then_inc(w_low, 1)

            def add_up(name, pair, e, c):
                m = NTC * (2 * pair + e) + c
                if name == "first" and m < NTC:
                    pool.wait_ge(init_read, DC * (m + 1))
                for d in range(DC):
                    pool.wait_ge(y_read, m + 1)
                    acc = t.accT[:, d, c * TC:(c + 1) * TC]
                    ins = pool.tensor_tensor(acc, acc, gated[d][:], ALU.add)
                ins.then_inc(summed, 1)

            for k in range(4):
                low(0, 0, k)

            def part(name, pair):
                for e, c in ((e, c) for e in range(2) for c in range(NTC)):
                    if name == "tail":
                        if (e, c) == (0, 0):
                            add_up(name, pair, -1, NTC - 1)
                        continue
                    if not (name == "first" and e == 0 and c == 0):
                        add_up(name, pair, e if c else e - 1, (c - 1) % NTC)
                    if not (name == "last" and e == 1):
                        low(2 * pair + e + 1, 1 - e, c)

            walk(pool, part)

        @block.scalar
        def _(act):
            def high_of(e, slot, k):
                act.wait_ge(raw_in[k], 16 * (e + 1))
                wait(act, y_done, STEPS * (e - 1))
                act.copy(w_piece(slot, k)[0], raw_piece(k)).then_inc(w_high, 1)

            for k in range(4):
                high_of(0, 0, k)

            def part(name, pair):
                for e, c, k in steps(name) if name != "tail" else ():
                    s = step_no(pair, e, c, k)
                    wait_apart(act, (hidden, s + 1), (split, s - 3))
                    at = (2 * pair + e) * HC0 + k
                    b = t.bias[:, at:at + 1] if isinstance(at, int) else t.bias[:, bass.ds(at, 1)]
                    act.activation(h[k % 4][:], h_ps[k % 2][:, 0:TC], ACT.Gelu, bias=b).then_inc(activated, 1)
                    if k == 5 and not (name == "last" and e == 1):
                        high_of(2 * pair + e + 1, 1 - e, c)
                    if name == "first" and s in EXP_AT:
                        router.exponents(act, EXP_AT[s])
                    if name == "first" and s - 1 in INIT_AT:
                        c = INIT_AT[s - 1]
                        act.wait_ge(init_done, c + 1)
                        for d in range(DC):
                            ins = act.copy(t.accT[:, d, c * TC:(c + 1) * TC], spare[d][:, 0:TC])
                            ins.then_inc(init_read, 1)

            walk(act, part)

        @block.vector
        def _(dve):
            router.split_weights(dve)
            router.copy_logits(dve)

            def read_y(pair, e, c):
                m = NTC * (2 * pair + e) + c
                dve.wait_ge(y_done, HC0 * (m + 1))
                dve.wait_ge(gate_in[e % 2], 16 * (pair + 1 + e // 2))
                wait(dve, summed, m)
                for d in range(DC):
                    ins = dve.tensor_tensor(gated[d][:], y_ps[c % 2][d][:, 0:TC],
                                            gate[e % 2][:, c * TC:(c + 1) * TC], ALU.mult)
                ins.then_inc(y_read, 1)

            def part(name, pair):
                for e, c, k in steps(name):
                    if name == "tail":
                        if (e, c, k) == (0, 0, 0):
                            read_y(pair, -1, NTC - 1)
                        continue
                    s = step_no(pair, e, c, k)
                    if name == "first" and s in COPY_AT:
                        router.copy_gates(dve, COPY_AT[s])
                    dve.wait_ge(activated, s + 1)
                    wait(dve, y_done, s - 3)
                    dve.tensor_copy(h_parts[k % 4][0][:], h[k % 4][:]).then_inc(high, 1)
                    dve.wait_ge(high, s + 1)
                    dve.tensor_tensor(h_parts[k % 4][1][:], h[k % 4][:], h_parts[k % 4][0][:].bitcast(F32),
                                      ALU.subtract).then_inc(split, 1)
                    if k == 2 and not (name == "first" and e == 0 and c <= 1):
                        read_y(pair, e if c else e - 1, (c - 1) % NTC)
                    if name == "first" and (e, c, k) == (0, 2, 0):
                        read_y(pair, 0, 0)
                    if name == "first" and s in STAGE_AT:
                        router.stage(dve, STAGE_AT[s])

            walk(dve, part)

        @block.tensor
        def _(pe):
            router.logits(pe)
            router.turn_logits(pe)

            def start_sums(c):
                if c == 0:
                    pe.wait_ge(b2_in, 16)
                    pe.wait_ge(router.gatesT_ready, NTC)
                wait(pe, init_read, DC * c)
                for d in range(DC):
                    ins = pe.matmul(spare[d][:, 0:TC], b2[:, d * P:(d + 1) * P],
                                    t.gatesT[:, c * TC:(c + 1) * TC], start=True, stop=True)
                ins.then_inc(init_done, 1)

            def hidden_of(pair, e, c, k):
                s = step_no(pair, e, c, k)
                if c == 0 and k == 0:
                    pe.wait_ge(w_low, 4 * (2 * pair + e + 1))
                wait(pe, activated, s - 1)
                for d in range(DC):
                    ins = three_pass(pe, h_ps[k % 2][:, 0:TC], [x[:, d, k * P:(k + 1) * P] for x in w1[e]],
                                     [x[:, d, c * TC:(c + 1) * TC] for x in t.xT], d == 0, d == DC - 1)
                ins.then_inc(hidden, 1)

            def output_of(pair, e, c, k):
                s = step_no(pair, e, c, k)
                m = NTC * (2 * pair + e) + c
                pe.wait_ge(split, s + 1)
                if k == 0:
                    wait(pe, y_read, m - 1)
                for d in range(DC):
                    ins = three_pass(pe, y_ps[c % 2][d][:, 0:TC], [x[:, k, d * P:(d + 1) * P] for x in w2[e % 2]],
                                     [x[:] for x in h_parts[k % 4]], k == 0, k == HC0 - 1)
                ins.then_inc(y_done, 1)

            def part(name, pair):
                for e, c, k in steps(name):
                    s = STEPS * e + HC0 * c + k
                    if name != "tail":
                        hidden_of(pair, e, c, k)
                    back = STEPS * e + HC0 * c + k - LAG_Y
                    if name == "first" and back < 0 or name == "tail" and back >= 0:
                        continue
                    output_of(pair, back // STEPS, back % STEPS // HC0, back % HC0)
                    if name == "first" and s in TURN_AT:
                        router.turn_gates(pe, TURN_AT[s])
                    if name == "first" and s in INIT_AT:
                        start_sums(INIT_AT[s])

            walk(pe, part)


def close_layer0(nc, t, inputs):
    with ExitStack() as ctx:
        def sem(name):
            return ctx.enter_context(nc.semaphore("c_" + name))

        stats = [ctx.enter_context(nc.sbuf_tensor(f"c_stats{k}", [S, 6], F32)) for k in range(2)]
        mv = [ctx.enter_context(nc.sbuf_tensor(f"c_mv{k}", [S, 2], F32)) for k in range(4)]
        var_eps = ctx.enter_context(nc.sbuf_tensor("c_var_eps", [S, 4], F32))
        rstd = ctx.enter_context(nc.sbuf_tensor("c_rstd", [S, 4], F32))
        xn = [ctx.enter_context(nc.sbuf_tensor(f"c_xn{k}", [S, D], F32)) for k in range(2)]
        y_ps = [ctx.enter_context(nc.psum_tensor(f"c_ps_y{k}", [S, D], F32)) for k in range(3)]
        x_ps = [ctx.enter_context(nc.psum_tensor(f"c_ps_x{k}", [P, DC, S], F32)) for k in range(3)]
        y_turned, x_done, stats_done = sem("y_turned"), sem("x_done"), sem("stats_done")
        mv_done, eps_done, root_done, xn_done = sem("mv_done"), sem("eps_done"), sem("root_done"), sem("xn_done")
        x_turned, high_done, low_done = sem("x_turned"), sem("high_done"), sem("low_done")
        weights_low, q_low = sem("weights_low"), sem("q_low")
        inputs.stage(ctx)
        block = ctx.enter_context(nc.Block())
        L2, L3 = 2, 3

        @block.sync
        def _(sp):
            inputs.load(sp)
            sp.wait_ge(inputs.rows_in, 32)

        @block.tensor
        def _(pe):
            for b in range(B + L2):
                if b < B:
                    if b >= 3:
                        pe.wait_ge(x_done, b - 2)
                    for d in range(DC):
                        ins = pe.transpose(y_ps[b % 3][:, d * P:(d + 1) * P], t.accT[:, d, b * S:(b + 1) * S],
                                           t.ident[:])
                    ins.then_inc(y_turned, 1)
                if b >= L2:
                    c = b - L2
                    pe.wait_ge(xn_done, c + 1)
                    if c >= 3:
                        pe.wait_ge(low_done, c - 2)
                    for d in range(DC):
                        ins = pe.transpose(x_ps[c % 3][:, d, :], xn[c % 2][:, d * P:(d + 1) * P],
                                           t.ident[0:S, 0:S])
                    ins.then_inc(x_turned, 1)

        @block.vector
        def _(dve):
            for b in range(B + L3):
                if b < B:
                    dve.wait_ge(y_turned, b + 1)
                    dve.scalar_tensor_tensor(out=t.x[:, b, :], in0=y_ps[b % 3][:], scalar=t.tanh_g[:, 2:3],
                                             in1=t.x[:, b, :], op0=ALU.mult, op1=ALU.add).then_inc(x_done, 1)
                    dve.wait_ge(x_done, b + 1)
                    dve.bn_stats(stats[b % 2][:], t.x[:, b, :]).then_inc(stats_done, 1)
                    dve.wait_ge(stats_done, b + 1)
                    if b >= 4:
                        dve.wait_ge(xn_done, b - 3)
                    dve.bn_aggr(mv[b % 4][:], stats[b % 2][:]).then_inc(mv_done, 1)
                if 1 <= b <= B:
                    c = b - 1
                    dve.wait_ge(root_done, c + 1)
                    if c >= 2:
                        dve.wait_ge(x_turned, c - 1)
                    dve.tensor_scalar(xn[c % 2][:], t.x[:, c, :], mv[c % 4][:, 0:1], rstd[:, c % 4:c % 4 + 1],
                                      ALU.subtract, ALU.mult).then_inc(xn_done, 1)
                if b >= L3:
                    c = b - L3
                    cols = slice(c * S, (c + 1) * S)
                    dve.wait_ge(high_done, c + 1)
                    dve.tensor_tensor(t.xT[1][:, :, cols], x_ps[c % 3][:], t.xT[0][:, :, cols].bitcast(F32),
                                      ALU.subtract).then_inc(low_done, 1)
            inputs.split_low(dve, "q", q_low)

        @block.gpsimd
        def _(pool):
            for b in range(B):
                k = b % 4
                pool.wait_ge(mv_done, b + 1)
                pool.tensor_scalar(var_eps[:, k:k + 1], mv[k][:, 1:2], LN_EPS, None, ALU.add).then_inc(eps_done, 1)
                pool.wait_ge(eps_done, b + 1)
                pool.tensor_tensor(rstd[:, k:k + 1], var_eps[:, k:k + 1], t.minus_half[:, 0:1],
                                   ALU.pow).then_inc(root_done, 1)
            inputs.split_context_low(pool)
            for k in "kvo":
                inputs.split_low(pool, k, weights_low)

        @block.scalar
        def _(act):
            inputs.split_context_high(act)
            for k in "kqvo":
                inputs.split_high(act, k)
            for b in range(B):
                act.wait_ge(x_turned, b + 1)
                act.copy(t.xT[0][:, :, b * S:(b + 1) * S], x_ps[b % 3][:]).then_inc(high_done, 1)


def experts1(nc, t, dram, out):
    NE = E + 1
    STEPS = NE * HC1
    W = DC * HID1 + HC1 * D
    n = "e1_"
    with ExitStack() as ctx:
        def sb(name, shape, dt=F32):
            return ctx.enter_context(nc.sbuf_tensor(n + name, shape, dt))

        def ps(name):
            return ctx.enter_context(nc.psum_tensor(n + name, [P, 512], F32))

        def sem(name):
            return ctx.enter_context(nc.semaphore(n + name))

        w = [sb(f"w_{p}", [P, NE, W], F32R) for p in ("hi", "lo")]
        raw = [sb(f"w_raw{k}", [P, W]) for k in range(2)]
        b2 = sb("b2_rows", [E, D])
        gate = [sb(f"gate{k}", [P, E, TC]) for k in range(2)]
        h = [sb(f"hidden{k}", [P, TC]) for k in range(3)]
        hg = [sb(f"gated{k}", [P, TC]) for k in range(3)]
        h_parts = [[sb(f"hidden{k}{p}", [P, TC], F32R) for p in ("hi", "lo")] for k in range(3)]
        yT = sb("yT", [P, DC, TC])
        h_ps = [ps(f"ps_hidden{k}") for k in range(3)]
        y_ps = [[ps(f"ps_y{k}{d}") for d in range(DC)] for k in range(2)]
        o_ps = ps("ps_out")
        raw_in = [sem(f"raw_in{k}") for k in range(2)]
        w_high, w_low, b2_in = sem("w_high"), sem("w_low"), sem("b2_loaded")
        gate_in = [sem(f"gate_loaded{k}") for k in range(2)]
        hidden, activated, gated, high, split = (
            sem("hidden_done"), sem("activated"), sem("gated"), sem("hidden_high"), sem("hidden_split"))
        y_done, y_read, turned, x_done, stored = (
            sem("y_done"), sem("y_read"), sem("turned"), sem("x_done"), sem("stored"))
        router = Router(nc, ctx, t, dram, 1, h_ps)

        with nc.Block() as block:
            @block.sync
            def _(sp):
                def load(e):
                    if e >= 2:
                        sp.wait_ge(w_low, e - 1)
                    r = raw[e % 2]
                    a = dram["L1_ffn_up_w"][e] if e < E else dram["L1_ffn_sh_up_w"]
                    b = dram["L1_ffn_down_w"][e] if e < E else dram["L1_ffn_sh_down_w"]
                    sp.dma_start(r[:, 0:DC * HID1].rearrange("p (c n) -> p c n", c=DC),
                                 a.rearrange("(c p) n -> p c n", p=P)).then_inc(raw_in[e % 2], 16)
                    sp.dma_start(r[:, DC * HID1:W].rearrange("p (c n) -> p c n", c=HC1),
                                 b.rearrange("(c p) n -> p c n", p=P)).then_inc(raw_in[e % 2], 16)

                router.load(sp)
                sp.dma_start(b2[:], dram["L1_ffn_down_b"]).then_inc(b2_in, 16)
                for e in range(NE):
                    load(e)
                router.store_gates(sp)

            @block.gpsimd
            def _(pool):
                for e in range(NE):
                    pool.wait_ge(w_high, e + 1)
                    pool.tensor_tensor(w[1][:, e, :], raw[e % 2][:], w[0][:, e, :].bitcast(F32),
                                       ALU.subtract).then_inc(w_low, 1)

            @block.scalar
            def _(act):
                def high_of(e):
                    act.wait_ge(raw_in[e % 2], 32 * (e // 2 + 1))
                    act.copy(w[0][:, e, :], raw[e % 2][:]).then_inc(w_high, 1)

                for e in range(NE):
                    if e == 4:
                        router.exponents(act, 0)
                    high_of(e)

            @block.vector
            def _(dve):
                router.split_weights(dve)
                router.copy_logits(dve)
                for k in range(Router.LAST + 1):
                    router.stage(dve, k)
                router.copy_gates(dve, range(NTC))

            @block.tensor
            def _(pe):
                router.logits(pe)
                router.turn_logits(pe)
                router.turn_gates(pe, range(NTC))

        block = ctx.enter_context(nc.Block())
        up = [x[:, :, 0:DC * HID1].rearrange("p e (c n) -> p e c n", c=DC) for x in w]
        down = [x[:, :, DC * HID1:W].rearrange("p e (c n) -> p e c n", c=HC1) for x in w]
        OUT_STEPS = [6, 8, 10, 12]

        def walk(eng, part):
            part("first", 0)
            part("middle", 1)
            part("middle", 2)
            part("last", NTC - 1)
            part("tail", NTC)

        steps = [(e, k) for e in range(NE) for k in range(HC1)]

        @block.sync
        def _(sp):
            def load_gates(c):
                wait(sp, gated, E * HC1 * (c - 1))
                sp.dma_start(gate[c % 2][:], dram["gates"][None, :, c * TC:(c + 1) * TC].to_broadcast([P, E, TC]))\
                    .then_inc(gate_in[c % 2], 16)

            for c in range(NTC):
                load_gates(c)
            for b in range(B):
                sp.wait_ge(x_done, b + 1)
                sp.dma_start(out[b], t.x[:, b, :]).then_inc(stored, 16)
            sp.wait_ge(stored, 16 * B)

        @block.scalar
        def _(act):
            def read_y(c):
                act.wait_ge(y_done, STEPS * (c + 1))
                wait(act, turned, BPC * c)
                at = BIAS_COLS["sh_down"][0]
                for d in range(DC):
                    ins = act.activation(yT[:, d, :], y_ps[c % 2][d][:, 0:TC], ACT.Identity,
                                         bias=t.bias[:, at + d:at + d + 1])
                ins.then_inc(y_read, 1)

            def part(name, c):
                for e, k in steps if name != "tail" else ():
                    s = STEPS * c + HC1 * e + k
                    act.wait_ge(hidden, s + 1)
                    wait(act, split, s - 2)
                    at = BIAS_COLS["up_b"][0] + HC1 * e + k if e < E else BIAS_COLS["sh_up"][0] + k
                    act.activation(h[s % 3][:], h_ps[s % 3][:, 0:TC], ACT.Silu,
                                   bias=t.bias[:, at:at + 1]).then_inc(activated, 1)
                    if (e, k) == (1, 1) and c > 0:
                        read_y(c - 1)
                if name == "tail":
                    read_y(c - 1)

            walk(act, part)

        @block.vector
        def _(dve):
            def finish(b):
                dve.wait_ge(turned, b + 1)
                dve.scalar_tensor_tensor(out=t.x[:, b, :], in0=o_ps[0:S, 0:D], scalar=t.tanh_g[:, 3:4],
                                         in1=t.x[:, b, :], op0=ALU.mult, op1=ALU.add).then_inc(x_done, 1)

            def part(name, c):
                for e, k in steps if name != "tail" else ():
                    s = STEPS * c + HC1 * e + k
                    dve.wait_ge(activated, s + 1)
                    wait(dve, y_done, s - 2)
                    src = h[s % 3]
                    if e < E:
                        if e == 0 and k == 0:
                            dve.wait_ge(gate_in[c % 2], 16 * (c // 2 + 1))
                        src = hg[s % 3]
                        dve.tensor_tensor(src[:], h[s % 3][:], gate[c % 2][:, e, :], ALU.mult).then_inc(gated, 1)
                        dve.wait_ge(gated, E * HC1 * c + HC1 * e + k + 1)
                    dve.tensor_copy(h_parts[s % 3][0][:], src[:]).then_inc(high, 1)
                    dve.wait_ge(high, s + 1)
                    dve.tensor_tensor(h_parts[s % 3][1][:], src[:], h_parts[s % 3][0][:].bitcast(F32),
                                      ALU.subtract).then_inc(split, 1)
                    if c > 0 and HC1 * e + k - 1 in OUT_STEPS:
                        finish(BPC * (c - 1) + OUT_STEPS.index(HC1 * e + k - 1))
                if name == "tail":
                    for j in range(BPC):
                        finish(BPC * (c - 1) + j)

            walk(dve, part)

        @block.tensor
        def _(pe):
            pe.wait_ge(b2_in, 16)

            def hidden_of(c, e, k):
                s = STEPS * c + HC1 * e + k
                wait(pe, activated, s - 2)
                for d in range(DC):
                    ins = three_pass(pe, h_ps[s % 3][:, 0:TC], [x[:, e, d, k * P:(k + 1) * P] for x in up],
                                     [x[:, d, c * TC:(c + 1) * TC] for x in t.xT], d == 0, d == DC - 1)
                ins.then_inc(hidden, 1)

            def output_of(c, e, k):
                s = STEPS * c + HC1 * e + k
                if e == 0 and k == 0:
                    wait(pe, y_read, c - 1)
                    for d in range(DC):
                        pe.matmul(y_ps[c % 2][d][:, 0:TC], b2[:, d * P:(d + 1) * P],
                                  t.gatesT[:, c * TC:(c + 1) * TC], start=True, stop=False)
                pe.wait_ge(split, s + 1)
                for d in range(DC):
                    ins = three_pass(pe, y_ps[c % 2][d][:, 0:TC], [x[:, e, k, d * P:(d + 1) * P] for x in down],
                                     [x[:] for x in h_parts[s % 3]], False, (e, k) == (NE - 1, HC1 - 1))
                ins.then_inc(y_done, 1)

            def turn(b):
                c, j = b // BPC, b % BPC
                pe.wait_ge(y_read, c + 1)
                wait(pe, x_done, b)
                for d in range(DC):
                    ins = pe.transpose(o_ps[0:S, d * P:(d + 1) * P], yT[:, d, j * S:(j + 1) * S], t.ident[:])
                ins.then_inc(turned, 1)

            def part(name, c):
                for e, k in steps:
                    at = HC1 * e + k
                    if name != "tail":
                        hidden_of(c, e, k)
                    back = at - LAG_Y
                    if not (name == "first" and back < 0 or name == "tail" and back >= 0):
                        output_of(c + back // STEPS, back % STEPS // HC1, back % HC1)
                    if name not in ("first", "tail") and at in OUT_STEPS:
                        turn(BPC * (c - 1) + OUT_STEPS.index(at))
                if name == "tail":
                    for j in range(BPC):
                        turn(BPC * (c - 1) + j)

            walk(pe, part)


def flamingo_layers(nc, dram, out):
    t = Core()
    with ExitStack() as persistent:
        allocate_persistent(nc, persistent, t)
        with ExitStack() as ctx:
            inputs = AttentionInputs(nc, ctx, t, dram, 0)
            prepare(nc, t, dram, inputs)
            attention(nc, t, dram, 0, inputs)
        with ExitStack() as ctx:
            t.accT = ctx.enter_context(nc.sbuf_tensor("accT", [P, DC, NTOK], F32))
            with ExitStack() as gates:
                t.gatesT = gates.enter_context(nc.sbuf_tensor("gatesT0", [E, NTOK], F32))
                experts0(nc, t, dram)
            inputs = AttentionInputs(nc, ctx, t, dram, 1)
            close_layer0(nc, t, inputs)
            attention(nc, t, dram, 1, inputs)
        with ExitStack() as ctx:
            t.gatesT = ctx.enter_context(nc.sbuf_tensor("gatesT1", [E, NTOK], F32))
            experts1(nc, t, dram, out)


_PLAIN = ["x", "g_xattn", "g_ffn"] + [f"L{l}_xattn_W{k}" for l in range(2) for k in "qkvo"] + [
    "L0_ffn_w1", "L0_ffn_w2", "L0_ffn_b2", "L1_ffn_up_w", "L1_ffn_down_w", "L1_ffn_down_b",
    "L1_ffn_sh_up_w", "L1_ffn_sh_down_w"]
_ROWS = ["L0_xattn_bv", "L0_xattn_bo", "L0_xattn_ln_gamma", "L0_xattn_ln_beta", "L1_xattn_bv", "L1_xattn_bo"]


def kernel(**inputs):
    import numpy as _np
    import concourse.bacc as _bacc
    from concourse import mybir as _mybir
    from concourse.bass_utils import run_bass_kernel_spmd as _run

    a = {k: _np.asarray(v) for k, v in inputs.items()}
    sent = {k: a[k] for k in _PLAIN}
    for k in _ROWS:
        sent[k] = a[k].reshape(1, -1)
    sent["ctxT"] = a["ctx_1024"].transpose(0, 2, 1)
    sent["mask"] = a["mask_Bx1x1xS2_ff0"].reshape(B, SC)
    columns = {"b1": "L0_ffn_b1", "bq0": "L0_xattn_bq", "bk0": "L0_xattn_bk", "bq1": "L1_xattn_bq",
               "bk1": "L1_xattn_bk", "up_b": "L1_ffn_up_b", "sh_up": "L1_ffn_sh_up_b", "sh_down": "L1_ffn_sh_down_b"}
    sent["bias_cols"] = _np.concatenate([a[columns[k]].reshape(-1, P).T for k in BIAS_COLS], axis=1)
    sent["router0"] = _np.concatenate([a["L0_ffn_router_w"], a["L0_ffn_lang_w"]], axis=0).T
    sent["router_bias"] = _np.concatenate([a["L0_ffn_router_b"], a["L0_ffn_lang_b"]]).reshape(1, NR)
    sent["router1"] = a["L1_ffn_gate_w"].T

    nc = _bacc.Bacc("TRN2", target_bir_lowering=False, num_devices=1)
    arrays, dram = {}, {}
    for name, v in sent.items():
        v = _np.ascontiguousarray(v)
        arrays[f"in_{name}_dram"] = v
        dram[name] = nc.dram_tensor(f"in_{name}_dram", v.shape, _mybir.dt.from_np(v.dtype), kind="ExternalInput").ap()
    dram["gates"] = nc.dram_tensor("gates_scratch", (E, NTOK), _mybir.dt.float32, kind="Internal").ap()
    out = nc.dram_tensor("out_0_dram", (B, S, D), _mybir.dt.float32, kind="ExternalOutput").ap()
    flamingo_layers(nc, dram, out)
    r = _run(nc, [arrays], core_ids=[0])
    return r.results[0]["out_0_dram"]
```

```python
from contextlib import ExitStack

import concourse.bass as bass
from concourse import mybir

F32 = mybir.dt.float32
F32R = mybir.dt.float32r
U32 = mybir.dt.uint32
ALU = mybir.AluOpType
ACT = mybir.ActivationFunctionType
AX = mybir.AxisListType

P = 128
B, S, D = 16, 100, 256
NTOK = B * S
SC = 361
H = 16
DC = D // P
DK0, DK1 = 64, D // H
N0 = H * DK0
CH0 = N0 // P
KT = 3
KR = (SC + KT - 1) // KT
CW = 364
CM = 362
E = 8
HID0, HID1 = 1024, 256
HC0, HC1 = HID0 // P, HID1 // P
TC = 400
NTC = NTOK // TC
BPC = TC // S
LN_EPS = 1e-5
NR = E + 4

BIAS_COLS = {}
_at = 0
for _name, _n in (("b1", E * HC0), ("bq0", CH0), ("bk0", CH0), ("bq1", DC), ("bk1", DC),
                  ("up_b", E * HC1), ("sh_up", HC1), ("sh_down", DC)):
    BIAS_COLS[_name] = (_at, _n)
    _at += _n
NBIAS = _at


def span(name):
    at, n = BIAS_COLS[name]
    return at, at + n


def wait(eng, sem, value):
    if isinstance(value, int) and value <= 0:
        return
    eng.wait_ge(sem, value)


def wait_apart(eng, *waits):
    waits = [(sem, v if isinstance(v, int) else eng.snap(eng.to_reg(v))) for sem, v in waits if not isinstance(v, int) or v > 0]
    if not all(isinstance(v, int) for _, v in waits):
        eng.wait_ge(waits[0][0], 1)
    for sem, value in waits:
        eng.wait_ge(sem, value)


def three_pass(pe, out, left, right, first, last):
    pe.matmul(out, left[0], right[0], start=first, stop=False)
    pe.matmul(out, left[0], right[1], start=False, stop=False)
    return pe.matmul(out, left[1], right[0], start=False, stop=last)


class Core:
    pass


def allocate_persistent(nc, ctx, t):
    def sb(name, shape, dt=F32):
        return ctx.enter_context(nc.sbuf_tensor(name, shape, dt))

    t.x = sb("x_rows", [S, B, D])
    t.xT = [sb(f"xnormT_{k}", [P, DC, NTOK], F32R) for k in ("hi", "lo")]
    t.ident = sb("identity", [P, P])
    t.bias = sb("bias_cols", [P, NBIAS])
    t.bq0s = sb("bq0_scaled", [P, CH0])
    t.bq1s = sb("bq1_scaled", [P, DC])
    t.gate_rows = sb("g_rows", [S, 4])
    t.tanh_g = sb("tanh_g", [S, 4])
    t.minus_half = sb("minus_half", [S, B])
    t.mv0 = sb("mean_var0", [S, B, 2])
    t.rstd0 = sb("rstd0", [S, B])
    t.xn = sb("xnorm_rows", [S, D])
    t.router_w = [[sb(f"router{layer}_w_{k}", [P, DC, nr], F32R) for k in ("hi", "lo")]
                  for layer, nr in enumerate((NR, E))]
    t.router_bias = sb("router_bias_rows", [S, NR])
    t.iota = sb("iota", [S, E])
    t.raw_in = [ctx.enter_context(nc.semaphore(f"raw_in{k}")) for k in range(4)]


def prepare(nc, t, dram, inputs):
    with ExitStack() as ctx:
        def sem(name):
            return ctx.enter_context(nc.semaphore(name))

        x_in = [sem(f"pre_x_loaded{k}") for k in range(2)]
        g_in, bias_in = sem("pre_g_loaded"), sem("pre_bias_loaded")
        pool_own, dve_own, act_own = sem("pre_pool_own"), sem("pre_dve_own"), sem("pre_act_own")
        rstd_ready, xn_ready = sem("pre_rstd_ready"), sem("pre_xn_ready")
        turned, high_ready, low_ready = sem("pre_turned"), sem("pre_high"), sem("pre_low")
        stats_ready, ident_ready = sem("pre_stats_ready"), sem("pre_ident_ready")
        weights_low, q_low = sem("pre_weights_low"), sem("pre_q_low")
        stats = ctx.enter_context(nc.sbuf_tensor("pre_stats", [S, B, 6], F32))
        var_eps = ctx.enter_context(nc.sbuf_tensor("pre_var_eps", [S, B], F32))
        xn = [ctx.enter_context(nc.sbuf_tensor(f"pre_xn{k}", [S, D], F32)) for k in range(4)]
        ps = [ctx.enter_context(nc.psum_tensor(f"pre_ps{k}", [P, DC, S], F32)) for k in range(4)]
        router_raw = [ctx.enter_context(nc.sbuf_tensor(f"pre_router{k}", list(t.router_w[k][0].shape), F32))
                      for k in range(2)]
        router_in, router_high, router_low = sem("pre_router_loaded"), sem("pre_router_high"), sem("pre_router_low")
        inputs.stage(ctx)
        NB = B // 2
        block = ctx.enter_context(nc.Block())

        @block.sync
        def _(sp):
            for k in range(2):
                half = slice(k * NB, (k + 1) * NB)
                sp.dma_start(t.x[:, half, :], dram["x"][half].rearrange("b s d -> s b d")).then_inc(x_in[k], 16)
            sp.dma_start(t.gate_rows[:, 0:2], dram["g_xattn"].rearrange("(a g) -> a g", a=1)
                         .to_broadcast([S, 2])).then_inc(g_in, 16)
            sp.dma_start(t.gate_rows[:, 2:4], dram["g_ffn"].rearrange("(a g) -> a g", a=1)
                         .to_broadcast([S, 2])).then_inc(g_in, 16)
            sp.dma_start(t.bias[:], dram["bias_cols"]).then_inc(bias_in, 16)
            inputs.load(sp)
            for k in range(2):
                sp.dma_start(router_raw[k][:], dram[f"router{k}"].rearrange("(c p) e -> p c e", p=P))\
                    .then_inc(router_in, 16)
            sp.dma_start(t.router_bias[:], dram["router_bias"].to_broadcast([S, NR])).then_inc(router_in, 16)
            sp.wait_ge(inputs.rows_in, 64)

        @block.gpsimd
        def _(pool):
            pool.memset(t.ident[:], 0.0).then_inc(pool_own, 1)
            pool.memset(t.minus_half[:], -0.5).then_inc(pool_own, 1)
            pool.wait_ge(pool_own, 2)
            pool.affine_select(out=t.ident[:], in_=t.ident[:], compare_op=ALU.not_equal, fill=1.0,
                               base=0, pattern=[[-1, P]], channel_multiplier=1).then_inc(ident_ready, 1)
            for k in range(2):
                half = slice(k * NB, (k + 1) * NB)
                pool.wait_ge(stats_ready, k + 1)
                pool.tensor_scalar(var_eps[:, half], t.mv0[:, half, 1], LN_EPS, None, ALU.add)\
                    .then_inc(pool_own, 1)
                pool.wait_ge(pool_own, k + 3)
                pool.tensor_tensor(t.rstd0[:, half], var_eps[:, half], t.minus_half[:, half], ALU.pow)\
                    .then_inc(rstd_ready, 1)
            inputs.split_context_low(pool)
            for k in "kvo":
                inputs.split_low(pool, k, weights_low)

        @block.scalar
        def _(act):
            act.wait_ge(g_in, 32)
            act.activation(t.tanh_g[:], t.gate_rows[:], ACT.Tanh).then_inc(act_own, 1)
            act.wait_ge(bias_in, 16)
            q0, n0 = BIAS_COLS["bq0"]
            q1, n1 = BIAS_COLS["bq1"]
            act.mul(t.bq0s[:], t.bias[:, q0:q0 + n0], DK0 ** -0.5).then_inc(act_own, 1)
            act.mul(t.bq1s[:], t.bias[:, q1:q1 + n1], -(DK1 ** -0.5)).then_inc(act_own, 1)
            inputs.split_context_high(act)
            inputs.split_high(act, "k")
            inputs.split_high(act, "q")
            for b in range(B):
                if b == B // 4:
                    inputs.split_high(act, "v")
                if b == B // 2:
                    inputs.split_high(act, "o")
                act.wait_ge(turned, b + 1)
                act.copy(t.xT[0][:, :, b * S:(b + 1) * S], ps[b % 4][:]).then_inc(high_ready, 1)

        @block.vector
        def _(dve):
            for k in range(2):
                dve.wait_ge(x_in[k], 16)
                for b in range(k * NB, (k + 1) * NB):
                    dve.bn_stats(stats[:, b, :], t.x[:, b, :]).then_inc(dve_own, 1)
                for b in range(k * NB, (k + 1) * NB):
                    dve.wait_ge(dve_own, b + 1)
                    ins = dve.bn_aggr(t.mv0[:, b, :], stats[:, b, :])
                ins.then_inc(stats_ready, 1)
            for b in range(B + 2):
                if b % NB == 0 and b < B:
                    dve.wait_ge(rstd_ready, b // NB + 1)
                    dve.wait_ge(stats_ready, b // NB + 1)
                if b < B:
                    if b >= 4:
                        dve.wait_ge(turned, b - 3)
                    dve.tensor_scalar(xn[b % 4][:], t.x[:, b, :], t.mv0[:, b, 0:1], t.rstd0[:, b:b + 1],
                                      ALU.subtract, ALU.mult).then_inc(xn_ready, 1)
                if b >= 2:
                    c = b - 2
                    dve.wait_ge(high_ready, c + 1)
                    cols = slice(c * S, (c + 1) * S)
                    dve.tensor_tensor(t.xT[1][:, :, cols], ps[c % 4][:], t.xT[0][:, :, cols].bitcast(F32),
                                      ALU.subtract).then_inc(low_ready, 1)
            inputs.split_low(dve, "q", q_low)
            for e in range(E):
                dve.memset(t.iota[:, e:e + 1], float(e))
            dve.wait_ge(router_in, 48)
            for k in range(2):
                dve.tensor_copy(t.router_w[k][0][:], router_raw[k][:]).then_inc(router_high, 1)
            for k in range(2):
                dve.wait_ge(router_high, k + 1)
                dve.tensor_tensor(t.router_w[k][1][:], router_raw[k][:], t.router_w[k][0][:].bitcast(F32),
                                  ALU.subtract).then_inc(router_low, 1)

        @block.tensor
        def _(pe):
            pe.wait_ge(ident_ready, 1)
            for b in range(B):
                pe.wait_ge(xn_ready, b + 1)
                if b >= 4:
                    pe.wait_ge(low_ready, b - 3)
                for c in range(DC):
                    ins = pe.transpose(ps[b % 4][:, c, :], xn[b % 4][:, c * P:(c + 1) * P], t.ident[0:S, 0:S])
                ins.then_inc(turned, 1)


LAG_T, LAG_V = 2, 3
RING = 3
PAIRS = B // 2
HALF = (slice(0, P // 2), slice(P // 2, P))


class Job:

    def __init__(self, part, kind, batch, args, step):
        self.part, self.kind, self.batch, self.args, self.step = part, kind, batch, args, step


def side_jobs0(batch, h, odd):
    nxt, prev = batch + 1, batch - 1
    jobs = []
    if h == 0:
        jobs.append(("K", batch, (CH0 - 1,)))
    if h in (1, 7) and not odd:
        jobs.append(("Q", batch, (CH0 - 1, h // 7)))
    if h == 4:
        jobs.append(("OT", prev, (1,)))
    if h == 12:
        jobs.append(("OT", batch, (0,)))
    if h >= 2 and h % 2 == 0:
        jobs.append(("K", nxt, (h // 2 - 1,)))
    if h in (3, 5, 7):
        jobs.append(("V", batch, (1, (h - 3) // 2)))
    if h in (11, 13, 15):
        jobs.append(("V", nxt, (0, (h - 11) // 2)))
    if h == 9:
        jobs.append(("OP", prev, ()))
    if odd and h >= 3 and h % 2 == 1:
        jobs.append(("Q", nxt, ((h - 3) // 2, None)))
    if h == 15:
        jobs.append(("XT", prev, ()))
    return jobs


def side_jobs1(batch, h, odd):
    nxt, prev = batch + 1, batch - 1
    jobs = []
    if h in (2, 4):
        jobs.append(("K", nxt, (h // 2 - 1,)))
    if h in (6, 7, 8):
        jobs.append(("V", nxt, (h - 6,)))
    if h == 5:
        jobs.append(("OT", prev, (0,)))
    if h == 9:
        jobs.append(("OP", prev, ()))
    if h == 14:
        jobs.append(("XT", prev, ()))
    if odd and h in (1, 3):
        jobs.append(("Q", nxt, (h // 2, None)))
    return jobs


PARTS = ("prologue", "first", "middle", "last", "tail")
PAIR_OF = {"prologue": 0, "first": 0, "last": PAIRS - 1, "tail": PAIRS}


class Plan:

    def __init__(self, side_jobs, prologue, act_kinds, dve_kinds):
        self.kinds = {"act": act_kinds, "dve": dve_kinds}
        self.jobs, count = [], {"all": 0, "act": 0, "dve": 0}
        for part in PARTS:
            if part == "last":
                for key in count:
                    count[key] += (PAIRS - 3) * self.per[key]
            before = dict(count)
            for where, (kind, batch, args) in self._listed(part, side_jobs, prologue):
                job = Job(part, kind, batch, args, where)
                job.n, job.n_act, job.n_dve = count["all"], count["act"], count["dve"]
                count["all"] += 1
                count["act"] += kind in act_kinds
                count["dve"] += kind in dve_kinds
                self.jobs.append(job)
            if part == "middle":
                self.per = {key: count[key] - before[key] for key in count}
                assert self.per["all"] % RING == 0

    @staticmethod
    def _listed(part, side_jobs, prologue):
        if part == "prologue":
            return [(None, j) for j in prologue]
        pair = 1 if part == "middle" else PAIR_OF[part]
        return [((local, h), j)
                for local in range(1 if part == "tail" else 2) for h in range(H)
                for j in side_jobs(local, h, local == 1) if 0 <= 2 * pair + j[1] < B]

    def of(self, part, where=None):
        return [j for j in self.jobs if j.part == part and (where is None or j.step == where)]

    def count(self, part, pair, job, who):
        n = {"act": job.n_act, "dve": job.n_dve}[who] + 1
        if part == "middle":
            return pair * self.per[who] + (n - self.per[who])
        return n + (PAIRS - 3) * self.per[who] if part in ("last", "tail") and job.part == "middle" else n

    def number(self, part, pair, job):
        return pair * self.per["all"] + (job.n + 1 - self.per["all"]) if part == "middle" else job.n + 1

    def before(self, job, far=RING):
        k = self.jobs.index(job) - far
        return self.jobs[k] if k >= 0 else None

    def latest(self, part, where, kind, *args):
        if isinstance(where, Job):
            known = self.jobs[:self.jobs.index(where)]
        else:
            known = [j for j in self.jobs if PARTS.index(j.part) < PARTS.index(part)
                     or j.part == part and j.step < where]
        return [j for j in known if j.kind == kind and j.args[:len(args)] == args][-1]


class AttentionInputs:

    def __init__(self, nc, ctx, t, dram, layer):
        L0 = layer == 0
        n = f"a{layer}_"
        nch = CH0 if L0 else DC
        width = nch * P

        def sb(name, shape, dt=F32):
            return ctx.enter_context(nc.sbuf_tensor(n + name, shape, dt))

        def parts(name, shape):
            return [sb(f"{name}_{k}", shape, F32R) for k in ("hi", "lo")]

        def sem(name):
            return ctx.enter_context(nc.semaphore(n + name))

        self.nc, self.t, self.dram, self.n = nc, t, dram, n
        self.L0, self.nch, self.width, self.pre = L0, nch, width, f"L{layer}_xattn_"
        self.wq, self.wk, self.wv = (parts(w, [P, DC, width]) for w in ("wq", "wk", "wv"))
        self.wo = parts("wo", [P, nch, D])
        self.ctx_raw = sb("ctx_raw", [P, DC, SC])
        self.cT = [parts(f"ctxT{k}", [P, DC, CW]) for k in range(2)]
        self.bv_rows, self.bo_rows = sb("bv_rows", [S, width]), sb("bo_rows", [S, D])
        if L0:
            self.gamma, self.beta = sb("gamma_rows", [S, D]), sb("beta_rows", [S, D])
        self.w_in = {k: sem(f"w{k}_loaded") for k in "kqvo"}
        self.w_high, self.rows_in = sem("weights_high"), sem("rows_loaded")
        self.ctx_in, self.ctx_high, self.ctx_low = sem("ctx_loaded"), sem("ctx_high"), sem("ctx_low")
        self.scale = {"k": 1.0, "q": DK0 ** -0.5 if L0 else -(DK1 ** -0.5), "v": 1.0, "o": 1.0}
        self.parts = {"k": self.wk, "q": self.wq, "v": self.wv, "o": self.wo}

    def stage(self, ctx):
        self.raw = {k: ctx.enter_context(self.nc.sbuf_tensor(f"{self.n}raw_w{k}", list(w[0].shape), F32))
                    for k, w in self.parts.items()}

    def load(self, sp):
        sp.dma_start(self.ctx_raw[:], self.dram["ctxT"][0].rearrange("(c p) s -> p c s", p=P))\
            .then_inc(self.ctx_in, 16)
        for k, raw in self.raw.items():
            sp.dma_start(raw[:], self.dram[self.pre + "W" + k].rearrange("(c p) n -> p c n", p=P))\
                .then_inc(self.w_in[k], 16)
        sp.dma_start(self.bv_rows[:], self.dram[self.pre + "bv"].to_broadcast([S, self.width]))\
            .then_inc(self.rows_in, 16)
        sp.dma_start(self.bo_rows[:], self.dram[self.pre + "bo"].to_broadcast([S, D])).then_inc(self.rows_in, 16)
        if self.L0:
            sp.dma_start(self.gamma[:], self.dram["L0_xattn_ln_gamma"].to_broadcast([S, D]))\
                .then_inc(self.rows_in, 16)
            sp.dma_start(self.beta[:], self.dram["L0_xattn_ln_beta"].to_broadcast([S, D]))\
                .then_inc(self.rows_in, 16)

    def split_context_high(self, act):
        act.wait_ge(self.ctx_in, 16)
        act.copy(self.cT[0][0][:, :, 0:SC], self.ctx_raw[:]).then_inc(self.ctx_high, 1)

    def split_context_low(self, pool):
        for parts in self.cT:
            for x in parts:
                pool.memset(x[:, :, SC:CW].bitcast(F32), 0.0)
        pool.wait_ge(self.ctx_high, 1)
        pool.tensor_tensor(self.cT[0][1][:, :, 0:SC], self.ctx_raw[:], self.cT[0][0][:, :, 0:SC].bitcast(F32),
                           ALU.subtract).then_inc(self.ctx_low, 1)

    def split_high(self, act, k):
        act.wait_ge(self.w_in[k], 16)
        act.mul(self.parts[k][0][:], self.raw[k][:], self.scale[k]).then_inc(self.w_high, 1)

    def split_low(self, eng, k, done):
        eng.wait_ge(self.w_high, "kqvo".index(k) + 1)
        if self.scale[k] == 1.0:
            ins = eng.tensor_tensor(self.parts[k][1][:], self.raw[k][:], self.parts[k][0][:].bitcast(F32),
                                    ALU.subtract)
        else:
            ins = eng.scalar_tensor_tensor(out=self.parts[k][1][:], in0=self.raw[k][:], scalar=self.scale[k],
                                           in1=self.parts[k][0][:].bitcast(F32),
                                           op0=ALU.mult, op1=ALU.subtract)
        ins.then_inc(done, 1)


def attention(nc, t, dram, layer, inputs):
    L0 = layer == 0
    nch = CH0 if L0 else DC
    hpc = H // nch
    width = nch * P
    dv = DK0 if L0 else DK1
    vw = dv if L0 else dv + 1
    o_per = 2 if L0 else 1
    hpo = H // o_per
    n = f"a{layer}_"
    if L0:
        prologue = [("K", 0, (c,)) for c in range(nch - 1)] + [("Q", 0, (c, None)) for c in range(nch - 1)]
        prologue += [("V", 0, (0, k)) for k in range(KT)]
        plan = Plan(side_jobs0, prologue, ("K", "Q", "V", "OT", "XT"), ("K", "Q", "OT", "OP", "XT"))
    else:
        prologue = [("K", 0, (c,)) for c in range(nch)] + [("Q", 0, (c, None)) for c in range(nch)]
        prologue += [("V", 0, (k,)) for k in range(KT)]
        plan = Plan(side_jobs1, prologue, ("K", "Q", "V", "OT", "XT"), ("K", "OT", "OP", "XT"))

    with ExitStack() as ctx:
        def sb(name, shape, dt=F32):
            return ctx.enter_context(nc.sbuf_tensor(n + name, shape, dt))

        def ps(name):
            return ctx.enter_context(nc.psum_tensor(n + name, [P, 512], F32))

        def parts(name, shape):
            return [sb(f"{name}_{k}", shape, F32R) for k in ("hi", "lo")]

        def sem(name):
            return ctx.enter_context(nc.semaphore(n + name))

        wq, wk, wv, wo = inputs.wq, inputs.wk, inputs.wv, inputs.wo
        ctx_raw, cT, bv_rows, bo_rows = inputs.ctx_raw, inputs.cT, inputs.bv_rows, inputs.bo_rows
        ctx_in, ctx_high, ctx_low = inputs.ctx_in, inputs.ctx_high, inputs.ctx_low
        two = 1 if L0 else 2
        if not L0:
            kT = [parts(f"kT{k}", [P, nch, CM]) for k in range(2)]
        V = [sb(f"values{k}", [KR, KT, H, vw]) for k in range(two)]
        probs = [sb(f"probs{k}", [S, KT * KR]) for k in range(4)]
        pT = [sb(f"probsT{k}", [KR, KT, S]) for k in range(4)]
        minus_max = sb("minus_max", [S, 4])
        row_inv = sb("row_inv", [S, H])
        o_rows = sb("o_rows", [S, width])
        oT = parts("oT", [P, nch, S])
        stats = sb("bn_stats", [S, 2, 6])
        mv = sb("mean_var", [S, 2, 2])
        var_eps = sb("var_eps", [S, 2])
        rstd = sb("rstd", [S, 2])
        if L0:
            keys = sb("keys", [P, H, CM], F32R)
            queries_high = sb("queries_high", [P, H, 2 * S], F32R)
            queries_low = sb("queries_low", [P, nch, 2 * S], F32R)
            row_sum = sb("row_sum", [S, 2, H])
            xn_bo = sb("xn_plus_bo", [S, D])
            y = xn_bo
            z = sb("z_rows", [S, D])
            gamma, beta = inputs.gamma, inputs.beta
        else:
            y = sb("y_rows", [S, D])
            q_flat = sb("q_flat", [P, nch, 2 * S])
            q_part = parts("q_part", [P, nch, 2 * S])
            qm = [parts(f"q_masked{k}", [P, H, S]) for k in range(2)]
            head_mask = sb("head_mask", [P, hpc])
            mask_rows = [sb(f"mask_rows{k}", [S, SC]) for k in range(2)]
            mask_big = [sb(f"mask_big{k}", [S, SC]) for k in range(2)]
            logits = [sb(f"minus_logits{k}", [S, SC]) for k in range(2)]
        s_ps = [ps(f"ps_scores{k}") for k in range(2)]
        t_ps = [ps(f"ps_probsT{k}") for k in range(2)]
        o_ps = ps("ps_o")
        r_ps = [ps(f"ps_ring{k}") for k in range(RING)]

        pads = sem("pads_written")
        scores, neg_max, exped = sem("scores_done"), sem("max_ready"), sem("probs_ready")
        turned, av = sem("probs_turned"), sem("values_done")
        copied = [sem(f"probsT_copied{k}") for k in range(1 if L0 else 2)]
        o_inv, o_scaled, o_biased = sem("o_inverse"), sem("o_scaled"), sem("o_biased")
        job_done, job_act, job_dve = sem("job_done"), sem("job_act_read"), sem("job_dve_read")
        chain, pool_chain = sem("dve_chain"), sem("pool_chain")
        x_ready, x_stats, x_rstd, xn_ready = sem("x_ready"), sem("x_stats"), sem("x_rstd"), sem("xn_ready")
        if L0:
            scaled, base_norm, base_ready = sem("rows_scaled"), sem("base_norm"), sem("base_ready")
            y_stats, y_rstd, z_ready = sem("y_stats"), sem("y_rstd"), sem("z_ready")
        else:
            mask_in = [sem(f"mask_loaded{k}") for k in range(2)]
            mask_ready, q_high, q_parts, q_masked = (
                sem("mask_ready"), sem("q_high"), sem("q_parts"), sem("q_masked"))

        def G(pair, local, h):
            return 2 * H * pair + H * local + h

        def copied_at(pair, local, h):
            if L0:
                return copied[0], G(pair, local, h) + 1
            k = H * local + h
            return copied[k % 2], H * pair + k // 2 + 1

        def walk(eng, part):
            part("prologue", 0)
            part("first", 0)
            with eng.Fori(1, PAIRS - 1) as i:
                part("middle", i)
            part("last", PAIRS - 1)
            part("tail", PAIRS)

        def steps(name):
            if name == "prologue":
                return []
            return [(local, h) for local in range(1 if name == "tail" else 2) for h in range(H)]

        def lagged(name, local, h, lag):
            k = H * local + h - lag
            if name == "first" and k < 0 or name == "tail" and k >= 0:
                return None
            return (k // H, k % H)

        def xcols(b, m=S):
            return slice(b * S, b * S + m) if isinstance(b, int) else bass.ds(b * S, m)

        def brow(b):
            return t.x[:, b, :] if isinstance(b, int) else t.x[:, bass.ds(b, 1), :].rearrange("s a d -> s (a d)")

        def prev_of(name, pair, local):
            return None if name == "first" and local == 0 else 2 * pair + local - 1

        SPLIT_AT = 14 if L0 else 12
        n_pads = 4 + (0 if L0 else 2)
        block = ctx.enter_context(nc.Block())

        @block.sync
        def _(sp):
            def load_context(b):
                wait(sp, ctx_high, b)
                wait(sp, ctx_low, b)
                src = dram["ctxT"][b] if isinstance(b, int) else \
                    dram["ctxT"][bass.ds(b, 1)].rearrange("a d s -> (a d) s")
                sp.dma_start(ctx_raw[:], src.rearrange("(c p) s -> p c s", p=P)).then_inc(ctx_in, 16)

            def load_mask(b, k):
                wait(sp, mask_ready, b - 1)
                src = dram["mask"][b:b + 1, :] if isinstance(b, int) else dram["mask"][bass.ds(b, 1), :]
                sp.dma_start(mask_rows[k][:], src.to_broadcast([S, SC])).then_inc(mask_in[k], 16)

            load_context(1)
            if not L0:
                load_mask(0, 0)
                load_mask(1, 1)
            with sp.Fori(1, PAIRS) as i:
                for k in range(2):
                    load_context(2 * i + k)
                    if not L0:
                        load_mask(2 * i + k, k)

        @block.tensor
        def _(pe):
            def job(name, pair, j):
                b = 2 * pair + j.batch
                bank, old = r_ps[j.n % RING], plan.before(j)
                if old is not None:
                    who = "dve" if old.kind in plan.kinds["dve"] else "act"
                    pe.wait_ge({"act": job_act, "dve": job_dve}[who], plan.count(name, pair, old, who))
                c_parts = cT[j.batch % 2]
                if j.kind in "KV":
                    pe.wait_ge(ctx_low, b + 1)
                if j.kind == "K":
                    (c,) = j.args
                    for d in range(DC):
                        ins = three_pass(pe, bank[:, 0:CM], [w[:, d, c * P:(c + 1) * P] for w in wk],
                                         [x[:, d, 0:CM] for x in c_parts], d == 0, d == DC - 1)
                elif j.kind == "V":
                    k = j.args[-1]
                    at, m = (j.args[0] * 512, 512) if L0 else (0, width)
                    for d in range(DC):
                        ins = three_pass(pe, bank[0:KR, 0:m], [x[:, d, k * KR:(k + 1) * KR] for x in c_parts],
                                         [w[:, d, at:at + m] for w in wv], d == 0, d == DC - 1)
                elif j.kind == "Q":
                    c, half = j.args
                    m = 2 * S if half is None else S
                    cols = xcols(b + (half or 0), m)
                    for d in range(DC):
                        ins = three_pass(pe, bank[:, 0:m], [w[:, d, c * P:(c + 1) * P] for w in wq],
                                         [x[:, d, cols] for x in t.xT], d == 0, d == DC - 1)
                elif j.kind == "OT":
                    c0, m = (4 * j.args[0], 4) if L0 else (0, DC)
                    pe.wait_ge(o_biased, o_per * b + j.args[0] + 1)
                    for c in range(m):
                        ins = pe.transpose(bank[:, c * S:(c + 1) * S],
                                           o_rows[:, (c0 + c) * P:(c0 + c + 1) * P], t.ident[0:S, 0:S])
                elif j.kind == "OP":
                    ot = plan.latest(name, j, "OT")
                    if plan.jobs.index(ot) > plan.jobs.index(old):
                        pe.wait_ge(job_dve, plan.count(name, pair, ot, "dve"))
                    for c in range(nch):
                        ins = three_pass(pe, bank[0:S, 0:D], [o[:, c, :] for o in oT],
                                         [w[:, c, :] for w in wo], c == 0, c == nch - 1)
                elif j.kind == "XT":
                    pe.wait_ge(xn_ready, b + 1)
                    for c in range(DC):
                        ins = pe.transpose(bank[:, c * S:(c + 1) * S], t.xn[:, c * P:(c + 1) * P],
                                           t.ident[0:S, 0:S])
                ins.then_inc(job_done, 1)

            def scores_of(name, pair, local, h):
                c, g = h // hpc, G(pair, local, h)
                if h % hpc == 0:
                    k_job = plan.latest(name, (local, h), "K", c)
                    pe.wait_ge(job_dve, plan.count(name, pair, k_job, "dve"))
                    if L0:
                        q_job = plan.latest(name, (local, h), "Q", c)
                        pe.wait_ge(job_dve, plan.count(name, pair, q_job, "dve"))
                    else:
                        pe.wait_ge(q_masked, 2 * nch * pair + nch * local + c + 1)
                wait(pe, exped if L0 else neg_max, g - 1)
                out = s_ps[h % 2][0:S, 0:CM]
                if L0:
                    rows, cols = HALF[h % 2], slice(local * S, (local + 1) * S)
                    pe.matmul(out, queries_high[:, h, cols], keys[:, h, :], start=True, stop=False)
                    pe.matmul(out, queries_low[rows, c, cols], keys[rows, h, :], start=False, stop=True)\
                        .then_inc(scores, 1)
                else:
                    three_pass(pe, out, [x[:, h, :] for x in qm[local]], [x[:, c, :] for x in kT[local]],
                               True, True).then_inc(scores, 1)

            def turn(name, pair, local, h):
                pe.wait_ge(exped, G(pair, local, h) + 1)
                back = lagged(name, local, h, 2)
                if back is not None:
                    pe.wait_ge(*copied_at(pair, *back))
                for k in range(KT):
                    ins = pe.transpose(t_ps[h % 2][0:KR, k * S:(k + 1) * S],
                                       probs[h % 4][:, k * KR:(k + 1) * KR], t.ident[0:S, 0:S])
                ins.then_inc(turned, 1)

            def values(name, pair, local, h):
                pe.wait_ge(*copied_at(pair, local, h))
                if h % hpo == 0:
                    wait(pe, o_scaled, o_per * (2 * pair + local) + h // hpo)
                if h == 0 or L0 and h == 8:
                    v_job = plan.latest(name, (local, h), "V", *((h // 8, KT - 1) if L0 else (KT - 1,)))
                    pe.wait_ge(job_act, plan.count(name, pair, v_job, "act"))
                v = V[0] if L0 else V[local % 2]
                at = (h % hpo) * vw
                for k in range(KT):
                    ins = pe.matmul(o_ps[0:S, at:at + vw], pT[h % 4][:, k, :], v[:, k, h, :],
                                    start=k == 0, stop=k == KT - 1)
                ins.then_inc(av, 1)

            def part(name, pair):
                for j in plan.of(name) if name == "prologue" else ():
                    job(name, pair, j)
                for local, h in steps(name):
                    if name != "tail":
                        scores_of(name, pair, local, h)
                    if name == "first" and (local, h) == (0, LAG_T):
                        pe.wait_ge(pads, n_pads)
                    if (back := lagged(name, local, h, LAG_T)) is not None:
                        turn(name, pair, *back)
                    for j in plan.of(name, (local, h)):
                        job(name, pair, j)
                    if (back := lagged(name, local, h, LAG_V)) is not None:
                        values(name, pair, *back)

            walk(pe, part)

        @block.gpsimd
        def _(pool):
            if not L0:
                pool.memset(head_mask[:], 1.0).then_inc(pool_chain, 1)
                pool.wait_ge(pool_chain, 1)
                pool.affine_select(out=head_mask[:], in_=head_mask[:], compare_op=ALU.is_ge, fill=0.0, base=0,
                                   pattern=[[-dv, hpc]], channel_multiplier=1).then_inc(pool_chain, 1)
                pool.wait_ge(pool_chain, 2)
                pool.affine_select(out=head_mask[:], in_=head_mask[:], compare_op=ALU.is_ge, fill=0.0,
                                   base=dv - 1, pattern=[[dv, hpc]], channel_multiplier=-1).then_inc(pool_chain, 1)
                pool.wait_ge(pool_chain, 3)
            for k in range(4):
                pool.memset(probs[k][:, SC:KT * KR], 0.0).then_inc(pads, 1)
            if not L0:
                for v in V:
                    pool.memset(v[:, :, :, dv:vw], 1.0).then_inc(pads, 1)
            if L0:
                pool.tensor_scalar(gamma[:], gamma[:], t.tanh_g[:, 0:1], None, ALU.mult).then_inc(scaled, 1)
                pool.tensor_scalar(beta[:], beta[:], t.tanh_g[:, 0:1], None, ALU.mult).then_inc(scaled, 1)
                pool.wait_ge(scaled, 2)
            base = 0 if L0 else 3

            def split_low(b, k):
                pool.wait_ge(ctx_high, b + 1)
                pool.tensor_tensor(cT[k][1][:, :, 0:SC], ctx_raw[:], cT[k][0][:, :, 0:SC].bitcast(F32),
                                   ALU.subtract).then_inc(ctx_low, 1)

            def inverse_root(k, stats_sem, out_sem, b, links):
                wait_apart(pool, (stats_sem, b + 1))
                pool.tensor_scalar(var_eps[:, k:k + 1], mv[:, k, 1:2], LN_EPS, None, ALU.add).then_inc(pool_chain, 1)
                pool.wait_ge(pool_chain, links + 1)
                pool.tensor_tensor(rstd[:, k:k + 1], var_eps[:, k:k + 1], t.minus_half[:, 0:1],
                                   ALU.pow).then_inc(out_sem, 1)

            def add_bv(pair, local, half):
                cols = slice(half * 512, half * 512 + 512) if L0 else slice(0, width)
                pool.wait_ge(o_scaled, o_per * (2 * pair + local) + half + 1)
                pool.tensor_tensor(o_rows[:, cols], o_rows[:, cols], bv_rows[:, cols], ALU.add).then_inc(o_biased, 1)

            def mask_queries(pair, local):
                for c in range(nch):
                    pool.wait_ge(q_parts, nch * pair + c + 1)
                    wait(pool, scores, G(pair, local, 0) - H)
                    for k in range(2):
                        src = q_part[k][:, c, local * S:(local + 1) * S].bitcast(F32)
                        ins = pool.tensor_tensor(
                            qm[local][k][:, c * hpc:(c + 1) * hpc, :],
                            src[:, None, :].to_broadcast([P, hpc, S]),
                            head_mask[:, :, None].to_broadcast([P, hpc, S]), ALU.mult)
                    ins.then_inc(q_masked, 1)

            def enlarge_mask(b, k, loads):
                wait_apart(pool, (mask_in[k], 16 * loads), (neg_max, H * (b - 1)))
                pool.tensor_scalar(mask_big[k][:], mask_rows[k][:], 1e9, None, ALU.mult).then_inc(mask_ready, 1)

            def part(name, pair):
                if name == "prologue":
                    if not L0:
                        enlarge_mask(0, 0, 1)
                        mask_queries(0, 0)
                    split_low(1, 1)
                    if not L0:
                        mask_queries(0, 1)
                    return
                for local, h in steps(name):
                    b = 2 * pair + local
                    p = prev_of(name, pair, local)
                    if h == 3 and p is not None:
                        add_bv(pair, local - 1, o_per - 1)
                    if L0 and h == 6 and p is not None:
                        pool.wait_ge(base_norm, p + 1)
                        pool.tensor_tensor(xn_bo[:], xn_bo[:], bo_rows[:], ALU.add).then_inc(base_ready, 1)
                    if L0 and h == 10 and p is not None:
                        inverse_root(0, y_stats, y_rstd, p, base + 4 * p)
                    if L0 and h == 11 and name != "tail":
                        add_bv(pair, local, 0)
                    if L0 and h == 11 and p is not None:
                        pool.wait_ge(z_ready, p + 1)
                        pool.tensor_tensor(z[:], z[:], gamma[:], ALU.mult).then_inc(pool_chain, 1)
                        pool.wait_ge(pool_chain, base + 4 * p + 2)
                        pool.tensor_tensor(z[:], z[:], beta[:], ALU.add).then_inc(pool_chain, 1)
                        pool.wait_ge(pool_chain, base + 4 * p + 3)
                        pool.tensor_tensor(brow(p), brow(p), z[:], ALU.add).then_inc(x_ready, 1)
                    if h == (13 if L0 else 11) and p is not None:
                        inverse_root(1, x_stats, x_rstd, p, base + 4 * p + 3 if L0 else base + p)
                    if name != "tail" and not L0:
                        if h == 5 and local == 1 and name != "last":
                            mask_queries(pair + 1, 0)
                        if h == 5 and local == 0 and name != "first":
                            mask_queries(pair, 1)
                        if h == 8 and not (name == "last" and local == 1):
                            enlarge_mask(b + 1, 1 - local, pair + 1 + local)
                    if h == SPLIT_AT and name not in ("last", "tail"):
                        split_low(b + 2, local)

            walk(pool, part)

        @block.scalar
        def _(act):
            biases = {"K": t.bias[:, slice(*span(f"bk{layer}"))], "Q": t.bq0s if L0 else t.bq1s}

            def split_high(b, k):
                act.wait_ge(ctx_in, 16 * (b + 1))
                if not isinstance(b, int) or b >= 2:
                    act.wait_ge(scores, H * (b - 2) + 9)
                act.copy(cT[k][0][:, :, 0:SC], ctx_raw[:]).then_inc(ctx_high, 1)

            def probabilities(name, pair, local, h):
                g = G(pair, local, h)
                act.wait_ge(neg_max, g + 1)
                wait(act, turned, g - 3)
                if L0:
                    act.activation(probs[h % 4][:, 0:SC], s_ps[h % 2][0:S, 0:SC], ACT.Exp,
                                   bias=minus_max[:, h % 4:h % 4 + 1],
                                   accum_out=row_sum[:, local, h:h + 1]).then_inc(exped, 1)
                else:
                    act.activation(probs[h % 4][:, 0:SC], logits[h % 2][:], ACT.Exp,
                                   bias=minus_max[:, h % 4:h % 4 + 1], scale=-1.0).then_inc(exped, 1)

            def copy_turned(pair, local, h):
                g = G(pair, local, h)
                act.wait_ge(turned, g + 1)
                wait(act, av, g - 3)
                act.copy(pT[h % 4][:], t_ps[h % 2][0:KR, 0:KT * S].rearrange("k (t s) -> k t s", s=S))\
                   .then_inc(copied[1], 1)

            def read(name, pair, j):
                b = 2 * pair + j.batch
                if j.kind not in plan.kinds["act"]:
                    return
                bank = r_ps[j.n % RING]
                act.wait_ge(job_done, plan.number(name, pair, j))
                if j.kind == "K":
                    (c,) = j.args
                    for side, rows in enumerate(HALF) if L0 else ():
                        ins = act.activation(keys[rows, 2 * c + side, :], bank[rows, 0:CM], ACT.Identity,
                                             bias=biases["K"][rows, c:c + 1])
                    if not L0:
                        ins = act.activation(kT[j.batch % 2][0][:, c, :], bank[:, 0:CM], ACT.Identity,
                                             bias=biases["K"][:, c:c + 1])
                elif j.kind == "Q":
                    c, half = j.args
                    m = 2 * S if half is None else S
                    at = S * (half or 0)
                    if not L0:
                        wait(act, q_parts, nch * (pair + int(j.batch == 2) - 1) + c + 1)
                    for side, rows in enumerate(HALF) if L0 else ():
                        for to in HALF:
                            ins = act.activation(queries_high[to, 2 * c + side, at:at + m], bank[rows, 0:m],
                                                 ACT.Identity, bias=biases["Q"][rows, c:c + 1])
                    if not L0:
                        ins = act.activation(q_flat[:, c, at:at + m], bank[:, 0:m], ACT.Identity,
                                             bias=biases["Q"][:, c:c + 1])
                elif j.kind == "V":
                    k = j.args[-1]
                    h0, m = (8 * j.args[0], 8) if L0 else (0, H)
                    ins = act.copy(V[0 if L0 else j.batch % 2][:, k, h0:h0 + m, 0:dv],
                                   bank[0:KR, 0:m * dv].rearrange("k (h v) -> k h v", v=dv))
                elif j.kind == "OT":
                    c0, m = (4 * j.args[0], 4) if L0 else (0, DC)
                    ins = act.copy(oT[0][:, c0:c0 + m, :], bank[:, 0:m * S].rearrange("p (c s) -> p c s", s=S))
                elif j.kind == "XT":
                    ins = act.copy(t.xT[0][:, :, xcols(b)], bank[:, 0:DC * S].rearrange("p (c s) -> p c s", s=S))
                ins.then_inc(job_act, 1)

            def part(name, pair):
                if name == "prologue":
                    split_high(1, 1)
                    for j in plan.of(name):
                        read(name, pair, j)
                    return
                for local, h in steps(name):
                    back = lagged(name, local, h, LAG_T)
                    if not L0 and back is not None and back[1] % 2:
                        copy_turned(pair, *back)
                    if name != "tail":
                        probabilities(name, pair, local, h)
                    for j in plan.of(name, (local, h)):
                        read(name, pair, j)
                    if h == SPLIT_AT and name not in ("last", "tail"):
                        split_high(2 * pair + local + 2, local)

            walk(act, part)

        @block.vector
        def _(dve):
            biases = {"K": t.bias[:, slice(*span(f"bk{layer}"))], "Q": t.bq0s if L0 else t.bq1s}
            CH = 2 if L0 else 1

            def link(ins, b, k):
                ins.then_inc(chain, 1)
                wait_apart(dve, (chain, CH * b + k + 1))

            def maximum(name, pair, local, h):
                g = G(pair, local, h)
                if L0:
                    dve.wait_ge(scores, g + 1)
                    wait(dve, exped, g - 3)
                    ins = dve.tensor_reduce(minus_max[:, h % 4:h % 4 + 1], s_ps[h % 2][0:S, 0:SC], AX.X, ALU.max,
                                            negate=True)
                else:
                    wait_apart(dve, (scores, g + 1), (exped, g - 1),
                               *([(mask_ready, 2 * pair + local + 1)] if h == 0 else []))
                    ins = dve.tensor_tensor_reduce(logits[h % 2][:], s_ps[h % 2][0:S, 0:SC], mask_big[local][:],
                                                   1.0, 3.0e38, ALU.add, ALU.min, minus_max[:, h % 4:h % 4 + 1])
                ins.then_inc(neg_max, 1)

            def copy_turned(pair, local, h):
                g = G(pair, local, h)
                dve.wait_ge(turned, g + 1)
                wait(dve, av, g - 3)
                dve.tensor_copy(pT[h % 4][:], t_ps[h % 2][0:KR, 0:KT * S].rearrange("k (t s) -> k t s", s=S))\
                   .then_inc(copied[0], 1)

            def scale_o(pair, local, half):
                m, b = hpo, 2 * pair + local
                dve.wait_ge(av, H * b + hpo * (half + 1))
                wait(dve, o_scaled, o_per * b + half)
                o = o_ps[0:S, 0:m * vw].rearrange("s (h v) -> s h v", v=vw)
                sums = row_sum[:, local % 2, half * m:(half + 1) * m] if L0 else o[:, :, dv]
                dve.reciprocal(row_inv[:, 0:m], sums).then_inc(o_inv, 1)
                dve.wait_ge(o_inv, o_per * b + half + 1)
                to = o_rows[:, half * m * dv:(half + 1) * m * dv].rearrange("s (h v) -> s h v", v=dv)
                dve.tensor_tensor(to, o[:, :, 0:dv], row_inv[:, 0:m, None].to_broadcast([S, m, dv]),
                                  ALU.mult).then_inc(o_scaled, 1)

            def read(name, pair, j):
                b = 2 * pair + j.batch
                bank = r_ps[j.n % RING]
                if j.kind == "Q" and not L0:
                    c = j.args[0]
                    k = nch * (pair + int(j.batch == 2)) + c
                    dve.wait_ge(job_act, plan.count(name, pair, j, "act"))
                    wait(dve, q_masked, 2 * nch * (pair + int(j.batch == 2)))
                    dve.tensor_copy(q_part[0][:, c, :], q_flat[:, c, :]).then_inc(q_high, 1)
                    dve.wait_ge(q_high, k + 1)
                    dve.tensor_tensor(q_part[1][:, c, :], q_flat[:, c, :], q_part[0][:, c, :].bitcast(F32),
                                      ALU.subtract).then_inc(q_parts, 1)
                    return
                if j.kind not in plan.kinds["dve"]:
                    return
                if j.kind == "OP":
                    dve.wait_ge(job_done, plan.number(name, pair, j))
                else:
                    dve.wait_ge(job_act, plan.count(name, pair, j, "act"))
                if j.kind == "K":
                    (c,) = j.args
                    for side, rows in enumerate(HALF) if L0 else ():
                        ins = dve.scalar_tensor_tensor(
                            out=keys[HALF[1 - side], 2 * c + side, :], in0=bank[rows, 0:CM],
                            scalar=biases["K"][rows, c:c + 1], in1=keys[rows, 2 * c + side, :].bitcast(F32),
                            op0=ALU.add, op1=ALU.subtract)
                    if not L0:
                        k = kT[j.batch % 2]
                        ins = dve.scalar_tensor_tensor(out=k[1][:, c, :], in0=bank[:, 0:CM],
                                                       scalar=biases["K"][:, c:c + 1],
                                                       in1=k[0][:, c, :].bitcast(F32),
                                                       op0=ALU.add, op1=ALU.subtract)
                elif j.kind == "Q":
                    c, half = j.args
                    m = 2 * S if half is None else S
                    at = S * (half or 0)
                    for side, rows in enumerate(HALF):
                        ins = dve.scalar_tensor_tensor(
                            out=queries_low[rows, c, at:at + m], in0=bank[rows, 0:m], scalar=biases["Q"][rows, c:c + 1],
                            in1=queries_high[rows, 2 * c + side, at:at + m].bitcast(F32),
                            op0=ALU.add, op1=ALU.subtract)
                elif j.kind == "OT":
                    c0, m = (4 * j.args[0], 4) if L0 else (0, DC)
                    ins = dve.tensor_tensor(oT[1][:, c0:c0 + m, :],
                                            bank[:, 0:m * S].rearrange("p (c s) -> p c s", s=S),
                                            oT[0][:, c0:c0 + m, :].bitcast(F32), ALU.subtract)
                elif j.kind == "OP":
                    if L0:
                        dve.wait_ge(base_ready, b + 1)
                    ins = dve.tensor_tensor(y[:], bank[0:S, 0:D], (xn_bo if L0 else bo_rows)[:], ALU.add)
                    ins.then_inc(job_dve, 1)
                    dve.wait_ge(job_dve, plan.count(name, pair, j, "dve"))
                    if not L0:
                        dve.scalar_tensor_tensor(out=brow(b), in0=y[:], scalar=t.tanh_g[:, 1:2], in1=brow(b),
                                                 op0=ALU.mult, op1=ALU.add).then_inc(x_ready, 1)
                    return
                elif j.kind == "XT":
                    ins = dve.tensor_tensor(t.xT[1][:, :, xcols(b)],
                                            bank[:, 0:DC * S].rearrange("p (c s) -> p c s", s=S),
                                            t.xT[0][:, :, xcols(b)].bitcast(F32), ALU.subtract)
                ins.then_inc(job_dve, 1)

            def mean_var(k, rows, b, at, out):
                link(dve.bn_stats(stats[:, k, :], rows), b, at)
                dve.bn_aggr(mv[:, k, :], stats[:, k, :]).then_inc(out, 1)

            def part(name, pair):
                if name == "prologue":
                    for j in plan.of(name):
                        read(name, pair, j)
                    return
                for n_step, (local, h) in enumerate(steps(name)):
                    p = prev_of(name, pair, local)
                    if L0 and (back := lagged(name, local, h, LAG_V + 1)) is not None and back[1] % hpo == hpo - 1:
                        scale_o(pair, back[0], back[1] // hpo)
                    if name != "tail":
                        maximum(name, pair, local, h)
                    back = lagged(name, local, h, LAG_T)
                    if back is not None and (L0 or back[1] % 2 == 0):
                        copy_turned(pair, *back)
                    for j in plan.of(name, steps(name)[n_step - 1]) if L0 and n_step else ():
                        read(name, pair, j)
                    if not L0 and (back := lagged(name, local, h, LAG_V)) is not None and back[1] == H - 1:
                        scale_o(pair, back[0], 0)
                    if p is not None:
                        if L0 and h == 5:
                            m = t.mv0[:, p, 0:1] if isinstance(p, int) else \
                                t.mv0[:, bass.ds(p, 1), 0:1].rearrange("s a c -> s (a c)")
                            r = t.rstd0[:, p:p + 1] if isinstance(p, int) else t.rstd0[:, bass.ds(p, 1)]
                            dve.tensor_scalar(xn_bo[:], brow(p), m, r, ALU.subtract, ALU.mult)\
                               .then_inc(base_norm, 1)
                        if L0 and h == 10:
                            mean_var(0, y[:], p, 0, y_stats)
                        if L0 and h == 11:
                            dve.wait_ge(y_rstd, p + 1)
                            dve.tensor_scalar(z[:], y[:], mv[:, 0, 0:1], rstd[:, 0:1], ALU.subtract, ALU.mult)\
                               .then_inc(z_ready, 1)
                        if h == (13 if L0 else 11):
                            wait_apart(dve, (x_ready, p + 1))
                            mean_var(1, brow(p), p, 1 if L0 else 0, x_stats)
                        if h == (14 if L0 else 13):
                            dve.wait_ge(x_rstd, p + 1)
                            dve.tensor_scalar(t.xn[:], brow(p), mv[:, 1, 0:1], rstd[:, 1:2],
                                              ALU.subtract, ALU.mult).then_inc(xn_ready, 1)
                    if not L0 or n_step == len(steps(name)) - 1:
                        for j in plan.of(name, (local, h)):
                            read(name, pair, j)

            walk(dve, part)


class Router:

    LAST = 8

    def __init__(self, nc, ctx, t, dram, layer, banks):
        def sb(name, shape, dt=F32):
            return ctx.enter_context(nc.sbuf_tensor(n + name, shape, dt))

        def sem(name):
            return ctx.enter_context(nc.semaphore(n + name))

        n = f"r{layer}_"
        self.t, self.dram, self.layer, self.banks = t, dram, layer, banks
        self.nr = nr = NR if layer == 0 else E
        self.w, self.bias, self.iota = t.router_w[layer], t.router_bias, t.iota
        self.logitT = sb("logitT", [nr, NTOK])
        self.logit = sb("logit", [S, B, nr])
        self.prob = sb("prob", [S, B, E])
        self.lang = sb("lang", [S, B, 4])
        self.mix = sb("mix", [S, B, 4])
        self.one = sb("one_per_token", [S, B])
        self.inv = sb("inverse", [S, B])
        self.top = sb("top8", [S, B, E])
        self.index = sb("index", [S, B, E], U32)
        self.index_f = sb("index_f", [S, B, 2])
        self.hit = [sb(f"hit{k}", [S, B, E]) for k in range(2)]
        self.gates = sb("gates", [S, B, E])
        self.chain = sem("dve_chain")
        self.logits_done, self.logits_read, self.logit_turned = (
            sem("logits_done"), sem("logits_read"), sem("logit_turned"))
        self.ask_exp, self.exp_done = sem("ask_exp"), sem("exp_done")
        self.gates_ready, self.gates_turned, self.gatesT_ready, self.gates_out = (
            sem("gates_ready"), sem("gates_turned"), sem("gatesT_ready"), sem("gates_stored"))
        self.links = 0

    def store_gates(self, sp):
        sp.wait_ge(self.gatesT_ready, NTC)
        sp.dma_start(self.dram["gates"], self.t.gatesT[:]).then_inc(self.gates_out, 16)
        sp.wait_ge(self.gates_out, 16)

    def logits(self, pe):
        for c in range(NTC):
            if c >= 2:
                pe.wait_ge(self.logits_read, c - 1)
            for d in range(DC):
                ins = three_pass(pe, self.banks[c % 2][0:self.nr, 0:TC], [x[:, d, :] for x in self.w],
                                 [x[:, d, c * TC:(c + 1) * TC] for x in self.t.xT], d == 0, d == DC - 1)
            ins.then_inc(self.logits_done, 1)

    def turn_logits(self, pe):
        pe.wait_ge(self.logits_read, NTC)
        for b in range(B):
            ins = pe.transpose(self.banks[0][0:S, b * self.nr:(b + 1) * self.nr],
                               self.logitT[:, b * S:(b + 1) * S], self.t.ident[0:self.nr, 0:self.nr])
        ins.then_inc(self.logit_turned, 1)

    def turn_gates(self, pe, chunks):
        pe.wait_ge(self.gates_ready, 1)
        for c in chunks:
            if c >= 2:
                pe.wait_ge(self.gatesT_ready, c - 1)
            for j in range(BPC):
                ins = pe.transpose(self.banks[c % 2][0:E, j * S:(j + 1) * S], self.gates[:, BPC * c + j, :],
                                   self.t.ident[0:S, 0:S])
            ins.then_inc(self.gates_turned, 1)

    def exponents(self, act, k):
        act.wait_ge(self.ask_exp, k + 1)
        x = self.lang if self.layer == 0 and k == 0 else self.prob
        act.activation(x[:], x[:], ACT.Exp).then_inc(self.exp_done, 1)

    def copy_logits(self, dve):
        for c in range(NTC):
            dve.wait_ge(self.logits_done, c + 1)
            dve.tensor_copy(self.logitT[:, c * TC:(c + 1) * TC], self.banks[c % 2][0:self.nr, 0:TC])\
                .then_inc(self.logits_read, 1)

    def copy_gates(self, dve, chunks):
        for c in chunks:
            dve.wait_ge(self.gates_turned, c + 1)
            dve.tensor_copy(self.t.gatesT[:, c * TC:(c + 1) * TC], self.banks[c % 2][0:E, 0:TC])\
                .then_inc(self.gatesT_ready, 1)

    def link(self, dve, ins):
        ins.then_inc(self.chain, 1)
        self.links += 1
        dve.wait_ge(self.chain, self.links)

    def softmax_start(self, dve, to, x, m):
        self.link(dve, dve.tensor_reduce(self.one[:], x, AX.X, ALU.max))
        dve.tensor_tensor(to, x, self.per_token(self.one, m), ALU.subtract).then_inc(self.ask_exp, 1)

    def softmax_end(self, dve, x, m, k):
        dve.wait_ge(self.exp_done, k + 1)
        self.link(dve, dve.tensor_reduce(self.one[:], x, AX.X, ALU.add))
        self.link(dve, dve.reciprocal(self.inv[:], self.one[:]))
        self.link(dve, dve.tensor_tensor(x, x, self.per_token(self.inv, m), ALU.mult))

    @staticmethod
    def per_token(x, m):
        return x[:, :, None].to_broadcast([S, B, m])

    def stage(self, dve, k):
        L0, logit, mix, lang, prob, top = self.layer == 0, self.logit, self.mix, self.lang, self.prob, self.top
        turned = self.banks[0][0:S, 0:B * self.nr].rearrange("s (b e) -> s b e", e=self.nr)
        if k == 0:
            dve.wait_ge(self.logit_turned, 1)
            if L0:
                self.link(dve, dve.tensor_tensor(
                    logit[:], turned, self.bias[:, None, :].to_broadcast([S, B, self.nr]), ALU.add))
                self.softmax_start(dve, lang[:], logit[:, :, E:NR], 4)
            else:
                self.link(dve, dve.tensor_copy(logit[:], turned))
        if L0 and k == 1:
            self.softmax_end(dve, lang[:], 4, 0)
            self.link(dve, dve.tensor_tensor(mix[:, :, 0:3], lang[:, :, 0:3], lang[:, :, 1:4], ALU.add))
            self.link(dve, dve.tensor_copy(mix[:, :, 3:4], lang[:, :, 3:4]))
        if k == 2:
            if L0:
                for e in range(0, E, 4):
                    ins = dve.scalar_tensor_tensor(out=logit[:, :, e:e + 4], in0=mix[:], scalar=0.1,
                                                   in1=logit[:, :, e:e + 4], op0=ALU.mult, op1=ALU.add)
                self.link(dve, ins)
            self.softmax_start(dve, prob[:], logit[:, :, 0:E], E)
        if k == 3:
            self.softmax_end(dve, prob[:], E, 1 if L0 else 0)
        if k == 4:
            for b in range(B):
                ins = dve.max(top[:, b, :], prob[:, b, :])
            self.link(dve, ins)
        if k == 5:
            for b in range(B):
                ins = dve.max_index(self.index[:, b, :], top[:, b, :], prob[:, b, :])
            self.link(dve, ins)
        if k == 6:
            dve.tensor_copy(self.index_f[:], self.index[:, :, 0:2])
            self.link(dve, dve.tensor_tensor(self.one[:], top[:, :, 0], top[:, :, 1], ALU.add))
            if not L0:
                self.link(dve, dve.tensor_scalar(self.one[:], self.one[:], 1e-20, None, ALU.add))
            self.link(dve, dve.reciprocal(self.inv[:], self.one[:]))
        if k == 7:
            dve.tensor_tensor(top[:, :, 0:2], top[:, :, 0:2], self.per_token(self.inv, 2), ALU.mult)
            for i in range(2):
                ins = dve.tensor_tensor(self.hit[i][:], self.iota[:, None, :].to_broadcast([S, B, E]),
                                        self.per_token(self.index_f[:, :, i], E), ALU.is_equal)
            self.link(dve, ins)
        if k == 8:
            for i in range(2):
                ins = dve.tensor_tensor(self.hit[i][:], self.hit[i][:], self.per_token(top[:, :, i], E), ALU.mult)
            self.link(dve, ins)
            dve.tensor_tensor(self.gates[:], self.hit[0][:], self.hit[1][:], ALU.add).then_inc(self.gates_ready, 1)


LAG_Y = 2


def experts0(nc, t, dram, closing):
    STEPS = NTC * HC0
    n = "e0_"
    with ExitStack() as ctx:
        def sb(name, shape, dt=F32):
            return ctx.enter_context(nc.sbuf_tensor(n + name, shape, dt))

        def ps(name):
            return ctx.enter_context(nc.psum_tensor(n + name, [P, 512], F32))

        def sem(name):
            return ctx.enter_context(nc.semaphore(n + name))

        w1 = [[sb(f"w1_{k}{p}", [P, DC, HID0], F32R) for p in ("hi", "lo")] for k in range(2)]
        w2 = [[sb(f"w2_{k}{p}", [P, HC0, D], F32R) for p in ("hi", "lo")] for k in range(2)]
        raw = [sb(f"w_raw{k}", [P, 1024]) for k in range(4)]
        b2 = sb("b2_rows", [E, D])
        gate = [sb(f"gate{k}", [P, NTOK]) for k in range(2)]
        h = [sb(f"hidden{k}", [P, TC]) for k in range(4)]
        h_parts = [[sb(f"hidden{k}{p}", [P, TC], F32R) for p in ("hi", "lo")] for k in range(4)]
        gated = [sb(f"gated{k}", [P, TC]) for k in range(DC)]
        h_ps = [ps(f"ps_hidden{k}") for k in range(2)]
        spare = [ps(f"ps_spare{k}") for k in range(2)]
        y_ps = [[ps(f"ps_y{k}{d}") for d in range(DC)] for k in range(2)]
        raw_in = t.raw_in
        w_high, w_low, b2_in = sem("w_high"), sem("w_low"), sem("b2_loaded")
        gate_in = [sem(f"gate_loaded{k}") for k in range(2)]
        init_done, init_read = sem("init_done"), sem("init_read")
        hidden, activated, high, split = sem("hidden_done"), sem("activated"), sem("hidden_high"), sem("hidden_split")
        y_done, y_read, summed = sem("y_done"), sem("y_read"), sem("summed")
        router = Router(nc, ctx, t, dram, 0, spare)
        block = ctx.enter_context(nc.Block())
        closing.use(spare[0:1], spare[1:2])
        STAGE_AT = {0: 0, 2: 1, 3: 2, 5: 3, 6: 4, 7: 5, 8: 6, 9: 7, 10: 8}
        EXP_AT = {1: 0, 4: 1}
        TURN_AT, COPY_AT = {11: (0, 1), 12: (2, 3)}, {12: (0, 1), 13: (2, 3)}
        INIT_AT = {14 + c: c for c in range(NTC)}

        def closed_at(name, s, k):
            if name == "last" and s >= STEPS or name == "tail":
                s += 2 * STEPS if name == "tail" else 0
                b, odd = divmod(s - STEPS - 13 - k, 2)
                if odd == 0 and 0 <= b < N_CLOSED:
                    return b
            return None

        def walk(eng, part):
            part("first", 0)
            with eng.Fori(1, E // 2 - 1) as i:
                part("middle", i)
            part("last", E // 2 - 1)
            part("tail", E // 2)

        def steps(name):
            return [(e, c, k) for e in range(2) for c in range(NTC) for k in range(HC0)]

        def step_no(pair, e, c, k):
            return 2 * STEPS * pair + STEPS * e + HC0 * c + k

        @block.sync
        def _(sp):
            def load(e, k):
                wait(sp, w_low, 4 * e + k - 3)
                e_ = slice(e, e + 1) if isinstance(e, int) else bass.ds(e, 1)
                if k < 2:
                    sp.dma_start(raw[k][:], dram["L0_ffn_w1"][e_, k * P:(k + 1) * P, :]
                                 .rearrange("a p n -> (a p) n")).then_inc(raw_in[k], 16)
                else:
                    rows = slice((k - 2) * 4 * P, (k - 1) * 4 * P)
                    sp.dma_start(raw[k][:].rearrange("p (c d) -> p c d", d=D),
                                 dram["L0_ffn_w2"][e_, rows, :].rearrange("a (c p) d -> p (a c) d", p=P))\
                        .then_inc(raw_in[k], 16)

            def load_gate(e, slot):
                wait(sp, y_read, NTC * (e - 1))
                src = dram["gates"][e:e + 1, :] if isinstance(e, int) else dram["gates"][bass.ds(e, 1), :]
                sp.dma_start(gate[slot][:], src.to_broadcast([P, NTOK])).then_inc(gate_in[slot], 16)

            for k in range(4):
                load(0, k)
            sp.dma_start(b2[:], dram["L0_ffn_b2"]).then_inc(b2_in, 16)
            for k in range(4):
                load(1, k)
            router.store_gates(sp)
            load_gate(0, 0)
            load_gate(1, 1)
            with sp.Fori(1, E // 2) as i:
                for e in range(2):
                    load_gate(2 * i + e, e)
                    for k in range(4):
                        load(2 * i + e, k)

        def w_piece(slot, k):
            return [x[:, k, :] for x in w1[slot]] if k < 2 else [x[:, (k - 2) * 4:(k - 1) * 4, :] for x in w2[slot]]

        def raw_piece(k):
            return raw[k][:] if k < 2 else raw[k][:].rearrange("p (c d) -> p c d", d=D)

        @block.gpsimd
        def _(pool):
            def low(e, slot, k):
                pool.wait_ge(w_high, 4 * e + k + 1)
                to = w_piece(slot, k)
                pool.tensor_tensor(to[1], raw_piece(k), to[0].bitcast(F32), ALU.subtract).then_inc(w_low, 1)

            def add_up(name, pair, e, c):
                m = NTC * (2 * pair + e) + c
                if name == "first" and m < NTC:
                    pool.wait_ge(init_read, DC * (m + 1))
                for d in range(DC):
                    pool.wait_ge(y_read, m + 1)
                    acc = t.accT[:, d, c * TC:(c + 1) * TC]
                    ins = pool.tensor_tensor(acc, acc, gated[d][:], ALU.add)
                ins.then_inc(summed, 1)

            def roots(name, e, c, among):
                for k in among:
                    if (b := closed_at(name, STEPS * e + HC0 * c + k, 1)) is not None:
                        closing.root(pool, b)

            for k in range(4):
                low(0, 0, k)

            def part(name, pair):
                if name == "tail":
                    roots(name, 0, 0, range(2))
                    add_up(name, pair, -1, NTC - 1)
                    return
                for e, c in ((e, c) for e in range(2) for c in range(NTC)):
                    roots(name, e, c, range(3))
                    if not (name == "first" and e == 0 and c == 0):
                        add_up(name, pair, e if c else e - 1, (c - 1) % NTC)
                    roots(name, e, c, range(3, HC0))
                    if not (name == "last" and e == 1):
                        low(2 * pair + e + 1, 1 - e, c)

            walk(pool, part)

        @block.scalar
        def _(act):
            def high_of(e, slot, k):
                act.wait_ge(raw_in[k], 16 * (e + 1))
                wait(act, y_done, STEPS * (e - 1))
                act.copy(w_piece(slot, k)[0], raw_piece(k)).then_inc(w_high, 1)

            for k in range(4):
                high_of(0, 0, k)

            def part(name, pair):
                for e, c, k in steps(name):
                    if (b := closed_at(name, STEPS * e + HC0 * c + k, 4)) is not None:
                        closing.high(act, b)
                    if name == "tail":
                        continue
                    s = step_no(pair, e, c, k)
                    wait_apart(act, (hidden, s + 1), (split, s - 3))
                    at = (2 * pair + e) * HC0 + k
                    b = t.bias[:, at:at + 1] if isinstance(at, int) else t.bias[:, bass.ds(at, 1)]
                    act.activation(h[k % 4][:], h_ps[k % 2][:, 0:TC], ACT.Gelu, bias=b).then_inc(activated, 1)
                    if k == 5 and not (name == "last" and e == 1):
                        high_of(2 * pair + e + 1, 1 - e, c)
                    if name == "first" and s in EXP_AT:
                        router.exponents(act, EXP_AT[s])
                    if name == "first" and s - 1 in INIT_AT:
                        c = INIT_AT[s - 1]
                        act.wait_ge(init_done, c + 1)
                        for d in range(DC):
                            ins = act.copy(t.accT[:, d, c * TC:(c + 1) * TC], spare[d][:, 0:TC])
                            ins.then_inc(init_read, 1)

            walk(act, part)

        @block.vector
        def _(dve):
            router.copy_logits(dve)

            def close(name, s):
                if (b := closed_at(name, s, 4)) is not None:
                    closing.low(dve, b)
                if (b := closed_at(name, s, 2)) is not None:
                    closing.norm(dve, b)
                if (b := closed_at(name, s, 1)) is not None:
                    closing.add_to_x(dve, b)

            def read_y(pair, e, c):
                m = NTC * (2 * pair + e) + c
                dve.wait_ge(y_done, HC0 * (m + 1))
                dve.wait_ge(gate_in[e % 2], 16 * (pair + 1 + e // 2))
                wait(dve, summed, m)
                for d in range(DC):
                    ins = dve.tensor_tensor(gated[d][:], y_ps[c % 2][d][:, 0:TC],
                                            gate[e % 2][:, c * TC:(c + 1) * TC], ALU.mult)
                ins.then_inc(y_read, 1)

            def part(name, pair):
                for e, c, k in steps(name):
                    if name == "tail":
                        close(name, STEPS * e + HC0 * c + k)
                        if (e, c, k) == (0, 0, 1):
                            read_y(pair, -1, NTC - 1)
                        continue
                    s = step_no(pair, e, c, k)
                    if name == "first" and s in COPY_AT:
                        router.copy_gates(dve, COPY_AT[s])
                    dve.wait_ge(activated, s + 1)
                    wait(dve, y_done, s - 3)
                    dve.tensor_copy(h_parts[k % 4][0][:], h[k % 4][:]).then_inc(high, 1)
                    dve.wait_ge(high, s + 1)
                    dve.tensor_tensor(h_parts[k % 4][1][:], h[k % 4][:], h_parts[k % 4][0][:].bitcast(F32),
                                      ALU.subtract).then_inc(split, 1)
                    if k == 2 and not (name == "first" and e == 0 and c <= 1):
                        read_y(pair, e if c else e - 1, (c - 1) % NTC)
                    if name == "first" and (e, c, k) == (0, 2, 0):
                        read_y(pair, 0, 0)
                    if name == "first" and s in STAGE_AT:
                        router.stage(dve, STAGE_AT[s])
                    close(name, STEPS * e + HC0 * c + k)

            walk(dve, part)

        @block.tensor
        def _(pe):
            router.logits(pe)
            router.turn_logits(pe)

            def start_sums(c):
                if c == 0:
                    pe.wait_ge(b2_in, 16)
                    pe.wait_ge(router.gatesT_ready, NTC)
                wait(pe, init_read, DC * c)
                for d in range(DC):
                    ins = pe.matmul(spare[d][:, 0:TC], b2[:, d * P:(d + 1) * P],
                                    t.gatesT[:, c * TC:(c + 1) * TC], start=True, stop=True)
                ins.then_inc(init_done, 1)

            def hidden_of(pair, e, c, k):
                s = step_no(pair, e, c, k)
                if c == 0 and k == 0:
                    pe.wait_ge(w_low, 4 * (2 * pair + e) + 2)
                wait(pe, activated, s - 1)
                for d in range(DC):
                    ins = three_pass(pe, h_ps[k % 2][:, 0:TC], [x[:, d, k * P:(k + 1) * P] for x in w1[e]],
                                     [x[:, d, c * TC:(c + 1) * TC] for x in t.xT], d == 0, d == DC - 1)
                ins.then_inc(hidden, 1)

            def output_of(pair, e, c, k):
                s = step_no(pair, e, c, k)
                m = NTC * (2 * pair + e) + c
                pe.wait_ge(split, s + 1)
                if c == 0 and k == 0:
                    pe.wait_ge(w_low, 4 * (2 * pair + e + 1))
                if k == 0:
                    wait(pe, y_read, m - 1)
                for d in range(DC):
                    ins = three_pass(pe, y_ps[c % 2][d][:, 0:TC], [x[:, k, d * P:(d + 1) * P] for x in w2[e % 2]],
                                     [x[:] for x in h_parts[k % 4]], k == 0, k == HC0 - 1)
                ins.then_inc(y_done, 1)

            def part(name, pair):
                for e, c, k in steps(name):
                    s = STEPS * e + HC0 * c + k
                    if name != "tail":
                        hidden_of(pair, e, c, k)
                    if (b := closed_at(name, s, 0)) is not None:
                        pe.wait_ge(summed, NTC * (E - 1) + b // BPC + 1)
                        closing.turn_y(pe, b)
                    if (b := closed_at(name, s, 3)) is not None:
                        closing.turn_x(pe, b)
                    back = STEPS * e + HC0 * c + k - LAG_Y
                    if name == "first" and back < 0 or name == "tail" and back >= 0:
                        continue
                    output_of(pair, back // STEPS, back % STEPS // HC0, back % HC0)
                    if name == "first" and s in TURN_AT:
                        router.turn_gates(pe, TURN_AT[s])
                    if name == "first" and s in INIT_AT:
                        start_sums(INIT_AT[s])

            walk(pe, part)


class Closing:

    def __init__(self, nc, ctx, t):
        n = "c_"

        def sb(name, shape):
            return ctx.enter_context(nc.sbuf_tensor(n + name, shape, F32))

        def sem(name):
            return ctx.enter_context(nc.semaphore(n + name))

        self.t = t
        self.stats = [sb(f"stats{k}", [S, 6]) for k in range(2)]
        self.mv = [sb(f"mean_var{k}", [S, 2]) for k in range(4)]
        self.var_eps, self.rstd = sb("var_eps", [S, 4]), sb("rstd", [S, 4])
        self.xn = [sb(f"xnorm{k}", [S, D]) for k in range(2)]
        self.y_turned, self.x_done, self.stats_done = sem("y_turned"), sem("x_done"), sem("stats_done")
        self.mv_done, self.eps_done, self.root_done = sem("mv_done"), sem("eps_done"), sem("root_done")
        self.xn_done, self.x_turned, self.high_done, self.low_done = (
            sem("xn_done"), sem("x_turned"), sem("high_done"), sem("low_done"))

    def use(self, y_banks, x_banks):
        self.y_banks, self.x_banks = y_banks, x_banks

    def turn_y(self, pe, i):
        m = len(self.y_banks)
        wait(pe, self.x_done, i - m + 1)
        for d in range(DC):
            ins = pe.transpose(self.y_banks[i % m][0:S, d * P:(d + 1) * P],
                               self.t.accT[:, d, i * S:(i + 1) * S], self.t.ident[:])
        ins.then_inc(self.y_turned, 1)

    def add_to_x(self, dve, i):
        t = self.t
        dve.wait_ge(self.y_turned, i + 1)
        dve.scalar_tensor_tensor(out=t.x[:, i, :], in0=self.y_banks[i % len(self.y_banks)][0:S, 0:D],
                                 scalar=t.tanh_g[:, 2:3], in1=t.x[:, i, :],
                                 op0=ALU.mult, op1=ALU.add).then_inc(self.x_done, 1)
        dve.wait_ge(self.x_done, i + 1)
        dve.bn_stats(self.stats[i % 2][:], t.x[:, i, :]).then_inc(self.stats_done, 1)
        dve.wait_ge(self.stats_done, i + 1)
        wait(dve, self.xn_done, i - 3)
        dve.bn_aggr(self.mv[i % 4][:], self.stats[i % 2][:]).then_inc(self.mv_done, 1)

    def root(self, pool, i):
        k = i % 4
        pool.wait_ge(self.mv_done, i + 1)
        pool.tensor_scalar(self.var_eps[:, k:k + 1], self.mv[k][:, 1:2], LN_EPS, None, ALU.add)\
            .then_inc(self.eps_done, 1)
        pool.wait_ge(self.eps_done, i + 1)
        pool.tensor_tensor(self.rstd[:, k:k + 1], self.var_eps[:, k:k + 1], self.t.minus_half[:, 0:1],
                           ALU.pow).then_inc(self.root_done, 1)

    def norm(self, dve, i):
        dve.wait_ge(self.root_done, i + 1)
        wait(dve, self.x_turned, i - 1)
        dve.tensor_scalar(self.xn[i % 2][:], self.t.x[:, i, :], self.mv[i % 4][:, 0:1],
                          self.rstd[:, i % 4:i % 4 + 1], ALU.subtract, ALU.mult).then_inc(self.xn_done, 1)

    def turn_x(self, pe, i):
        m = len(self.x_banks)
        pe.wait_ge(self.xn_done, i + 1)
        wait(pe, self.low_done, i - m + 1)
        for d in range(DC):
            ins = pe.transpose(self.x_banks[i % m][:, d * S:(d + 1) * S], self.xn[i % 2][:, d * P:(d + 1) * P],
                               self.t.ident[0:S, 0:S])
        ins.then_inc(self.x_turned, 1)

    def turned(self, i):
        bank = self.x_banks[i % len(self.x_banks)]
        return bank[:, 0:DC * S].rearrange("p (c s) -> p c s", s=S)

    def high(self, act, i):
        act.wait_ge(self.x_turned, i + 1)
        act.copy(self.t.xT[0][:, :, i * S:(i + 1) * S], self.turned(i)).then_inc(self.high_done, 1)

    def low(self, dve, i):
        cols = slice(i * S, (i + 1) * S)
        dve.wait_ge(self.high_done, i + 1)
        dve.tensor_tensor(self.t.xT[1][:, :, cols], self.turned(i), self.t.xT[0][:, :, cols].bitcast(F32),
                          ALU.subtract).then_inc(self.low_done, 1)


N_CLOSED = 10


def close_layer0(nc, t, closing, inputs):
    with ExitStack() as ctx:
        banks = [ctx.enter_context(nc.psum_tensor(f"c_ps{k}", [P, 512], F32)) for k in range(6)]
        closing.use(banks[0:3], banks[3:6])
        weights_low, q_low = (ctx.enter_context(nc.semaphore(k)) for k in ("c_weights_low", "c_q_low"))
        inputs.stage(ctx)
        block = ctx.enter_context(nc.Block())
        L2, L3 = 2, 3

        @block.sync
        def _(sp):
            inputs.load(sp)
            sp.wait_ge(inputs.rows_in, 32)

        @block.tensor
        def _(pe):
            for b in range(N_CLOSED, B + L2):
                if b < B:
                    closing.turn_y(pe, b)
                if b - L2 >= N_CLOSED:
                    closing.turn_x(pe, b - L2)

        @block.vector
        def _(dve):
            for b in range(N_CLOSED, B + L3):
                if b < B:
                    closing.add_to_x(dve, b)
                if N_CLOSED <= b - 1 < B:
                    closing.norm(dve, b - 1)
                if b - L3 >= N_CLOSED:
                    closing.low(dve, b - L3)
            inputs.split_low(dve, "q", q_low)

        @block.gpsimd
        def _(pool):
            for b in range(N_CLOSED, B):
                closing.root(pool, b)
            inputs.split_context_low(pool)
            for k in "kvo":
                inputs.split_low(pool, k, weights_low)

        @block.scalar
        def _(act):
            inputs.split_context_high(act)
            for k in "kqvo":
                inputs.split_high(act, k)
            for b in range(N_CLOSED, B):
                closing.high(act, b)


def experts1(nc, t, dram, out):
    NE = E + 1
    STEPS = NE * HC1
    W = DC * HID1 + HC1 * D
    n = "e1_"
    with ExitStack() as ctx:
        def sb(name, shape, dt=F32):
            return ctx.enter_context(nc.sbuf_tensor(n + name, shape, dt))

        def ps(name):
            return ctx.enter_context(nc.psum_tensor(n + name, [P, 512], F32))

        def sem(name):
            return ctx.enter_context(nc.semaphore(n + name))

        w = [sb(f"w_{p}", [P, NE, W], F32R) for p in ("hi", "lo")]
        raw = [sb(f"w_raw{k}", [P, W]) for k in range(4)]
        b2 = sb("b2_rows", [E, D])
        gate = [sb(f"gate{k}", [P, E, TC]) for k in range(2)]
        h = [sb(f"hidden{k}", [P, TC]) for k in range(3)]
        hg = [sb(f"gated{k}", [P, TC]) for k in range(3)]
        h_parts = [[sb(f"hidden{k}{p}", [P, TC], F32R) for p in ("hi", "lo")] for k in range(3)]
        yT = sb("yT", [P, DC, TC])
        h_ps = [ps(f"ps_hidden{k}") for k in range(3)]
        y_ps = [[ps(f"ps_y{k}{d}") for d in range(DC)] for k in range(2)]
        o_ps = ps("ps_out")
        raw_in, raw_before = t.raw_in, 16 * E
        w_high, b2_in = sem("w_high"), sem("b2_loaded")
        w_low = {"pool": sem("w_low_pool"), "dve": sem("w_low_dve")}
        gate_in = [sem(f"gate_loaded{k}") for k in range(2)]
        hidden, activated, gated, high, split = (
            sem("hidden_done"), sem("activated"), sem("gated"), sem("hidden_high"), sem("hidden_split"))
        y_done, y_read, turned, x_done, stored = (
            sem("y_done"), sem("y_read"), sem("turned"), sem("x_done"), sem("stored"))

        def load_gates(sp, c):
            wait(sp, gated, E * HC1 * (c - 1))
            sp.dma_start(gate[c % 2][:], dram["gates"][None, :, c * TC:(c + 1) * TC].to_broadcast([P, E, TC]))\
                .then_inc(gate_in[c % 2], 16)

        ON_DVE = (2, 5, 8)

        def low_made(e):
            who = "dve" if e in ON_DVE else "pool"
            return w_low[who], sum((x in ON_DVE) == (who == "dve") for x in range(e + 1))

        def low_of(eng, e):
            eng.wait_ge(w_high, e + 1)
            eng.tensor_tensor(w[1][:, e, :], raw[e % 4][:], w[0][:, e, :].bitcast(F32), ALU.subtract)\
                .then_inc(low_made(e)[0], 1)

        router = Router(nc, ctx, t, dram, 1, h_ps)

        with nc.Block() as block:
            @block.sync
            def _(sp):
                def load(e):
                    if e >= 4:
                        sp.wait_ge(*low_made(e - 4))
                    r = raw[e % 4]
                    a = dram["L1_ffn_up_w"][e] if e < E else dram["L1_ffn_sh_up_w"]
                    b = dram["L1_ffn_down_w"][e] if e < E else dram["L1_ffn_sh_down_w"]
                    sp.dma_start(r[:, 0:DC * HID1].rearrange("p (c n) -> p c n", c=DC),
                                 a.rearrange("(c p) n -> p c n", p=P)).then_inc(raw_in[e % 4], 16)
                    sp.dma_start(r[:, DC * HID1:W].rearrange("p (c n) -> p c n", c=HC1),
                                 b.rearrange("(c p) n -> p c n", p=P)).then_inc(raw_in[e % 4], 16)

                sp.dma_start(b2[:], dram["L1_ffn_down_b"]).then_inc(b2_in, 16)
                for e in range(NE):
                    load(e)
                router.store_gates(sp)
                for c in range(2):
                    load_gates(sp, c)

            @block.gpsimd
            def _(pool):
                for e in range(NE):
                    if e not in ON_DVE:
                        low_of(pool, e)

            @block.scalar
            def _(act):
                def high_of(e):
                    act.wait_ge(raw_in[e % 4], raw_before + 32 * (e // 4 + 1))
                    act.copy(w[0][:, e, :], raw[e % 4][:]).then_inc(w_high, 1)

                for e in range(NE):
                    if e == 4:
                        router.exponents(act, 0)
                    high_of(e)

            @block.vector
            def _(dve):
                router.copy_logits(dve)
                low_of(dve, ON_DVE[0])
                for k in range(Router.LAST + 1):
                    router.stage(dve, k)
                router.copy_gates(dve, range(NTC))
                for e in ON_DVE[1:]:
                    low_of(dve, e)

            @block.tensor
            def _(pe):
                router.logits(pe)
                router.turn_logits(pe)
                router.turn_gates(pe, range(NTC))

        block = ctx.enter_context(nc.Block())
        up = [x[:, :, 0:DC * HID1].rearrange("p e (c n) -> p e c n", c=DC) for x in w]
        down = [x[:, :, DC * HID1:W].rearrange("p e (c n) -> p e c n", c=HC1) for x in w]
        OUT_STEPS = [6, 8, 10, 12]

        def walk(eng, part):
            part("first", 0)
            part("middle", 1)
            part("middle", 2)
            part("last", NTC - 1)
            part("tail", NTC)

        steps = [(i, k) for i in range(NE) for k in range(HC1)]

        def expert(i):
            return E if i == 0 else i - 1

        @block.sync
        def _(sp):
            for c in range(2, NTC):
                load_gates(sp, c)
            for b in range(B):
                sp.wait_ge(x_done, b + 1)
                sp.dma_start(out[b], t.x[:, b, :]).then_inc(stored, 16)
            sp.wait_ge(stored, 16 * B)

        @block.scalar
        def _(act):
            def read_y(c):
                act.wait_ge(y_done, STEPS * (c + 1))
                wait(act, turned, BPC * c)
                at = BIAS_COLS["sh_down"][0]
                for d in range(DC):
                    ins = act.activation(yT[:, d, :], y_ps[c % 2][d][:, 0:TC], ACT.Identity,
                                         bias=t.bias[:, at + d:at + d + 1])
                ins.then_inc(y_read, 1)

            def part(name, c):
                for i, k in steps if name != "tail" else ():
                    s, e = STEPS * c + HC1 * i + k, expert(i)
                    act.wait_ge(hidden, s + 1)
                    wait(act, split, s - 2)
                    at = BIAS_COLS["up_b"][0] + HC1 * e + k if e < E else BIAS_COLS["sh_up"][0] + k
                    act.activation(h[s % 3][:], h_ps[s % 3][:, 0:TC], ACT.Silu,
                                   bias=t.bias[:, at:at + 1]).then_inc(activated, 1)
                    if (i, k) == (1, 1) and c > 0:
                        read_y(c - 1)
                if name == "tail":
                    read_y(c - 1)

            walk(act, part)

        @block.vector
        def _(dve):
            def finish(b):
                dve.wait_ge(turned, b + 1)
                dve.scalar_tensor_tensor(out=t.x[:, b, :], in0=o_ps[0:S, 0:D], scalar=t.tanh_g[:, 3:4],
                                         in1=t.x[:, b, :], op0=ALU.mult, op1=ALU.add).then_inc(x_done, 1)

            def part(name, c):
                for i, k in steps if name != "tail" else ():
                    s, e = STEPS * c + HC1 * i + k, expert(i)
                    dve.wait_ge(activated, s + 1)
                    wait(dve, y_done, s - 2)
                    src = h[s % 3]
                    if e < E:
                        if e == 0 and k == 0:
                            dve.wait_ge(gate_in[c % 2], 16 * (c // 2 + 1))
                        src = hg[s % 3]
                        dve.tensor_tensor(src[:], h[s % 3][:], gate[c % 2][:, e, :], ALU.mult).then_inc(gated, 1)
                        dve.wait_ge(gated, E * HC1 * c + HC1 * e + k + 1)
                    dve.tensor_copy(h_parts[s % 3][0][:], src[:]).then_inc(high, 1)
                    dve.wait_ge(high, s + 1)
                    dve.tensor_tensor(h_parts[s % 3][1][:], src[:], h_parts[s % 3][0][:].bitcast(F32),
                                      ALU.subtract).then_inc(split, 1)
                    if c > 0 and HC1 * i + k - 1 in OUT_STEPS:
                        finish(BPC * (c - 1) + OUT_STEPS.index(HC1 * i + k - 1))
                if name == "tail":
                    for j in range(BPC):
                        finish(BPC * (c - 1) + j)

            walk(dve, part)

        @block.tensor
        def _(pe):
            pe.wait_ge(b2_in, 16)

            def hidden_of(c, i, k):
                s, e = STEPS * c + HC1 * i + k, expert(i)
                wait(pe, activated, s - 2)
                for d in range(DC):
                    ins = three_pass(pe, h_ps[s % 3][:, 0:TC], [x[:, e, d, k * P:(k + 1) * P] for x in up],
                                     [x[:, d, c * TC:(c + 1) * TC] for x in t.xT], d == 0, d == DC - 1)
                ins.then_inc(hidden, 1)

            def output_of(c, i, k):
                s, e = STEPS * c + HC1 * i + k, expert(i)
                if i == 0 and k == 0:
                    wait(pe, y_read, c - 1)
                    for d in range(DC):
                        pe.matmul(y_ps[c % 2][d][:, 0:TC], b2[:, d * P:(d + 1) * P],
                                  t.gatesT[:, c * TC:(c + 1) * TC], start=True, stop=False)
                pe.wait_ge(split, s + 1)
                for d in range(DC):
                    ins = three_pass(pe, y_ps[c % 2][d][:, 0:TC], [x[:, e, k, d * P:(d + 1) * P] for x in down],
                                     [x[:] for x in h_parts[s % 3]], False, (i, k) == (NE - 1, HC1 - 1))
                ins.then_inc(y_done, 1)

            def turn(b):
                c, j = b // BPC, b % BPC
                pe.wait_ge(y_read, c + 1)
                wait(pe, x_done, b)
                for d in range(DC):
                    ins = pe.transpose(o_ps[0:S, d * P:(d + 1) * P], yT[:, d, j * S:(j + 1) * S], t.ident[:])
                ins.then_inc(turned, 1)

            def part(name, c):
                for i, k in steps:
                    at = HC1 * i + k
                    if name != "tail":
                        hidden_of(c, i, k)
                    back = at - LAG_Y
                    if not (name == "first" and back < 0 or name == "tail" and back >= 0):
                        output_of(c + back // STEPS, back % STEPS // HC1, back % HC1)
                    if name not in ("first", "tail") and at in OUT_STEPS:
                        turn(BPC * (c - 1) + OUT_STEPS.index(at))
                if name == "tail":
                    for j in range(BPC):
                        turn(BPC * (c - 1) + j)

            walk(pe, part)


def flamingo_layers(nc, dram, out):
    t = Core()
    with ExitStack() as persistent:
        allocate_persistent(nc, persistent, t)
        with ExitStack() as ctx:
            inputs = AttentionInputs(nc, ctx, t, dram, 0)
            prepare(nc, t, dram, inputs)
            attention(nc, t, dram, 0, inputs)
        with ExitStack() as ctx:
            t.accT = ctx.enter_context(nc.sbuf_tensor("accT", [P, DC, NTOK], F32))
            closing = Closing(nc, ctx, t)
            with ExitStack() as gates:
                t.gatesT = gates.enter_context(nc.sbuf_tensor("gatesT0", [E, NTOK], F32))
                experts0(nc, t, dram, closing)
            inputs = AttentionInputs(nc, ctx, t, dram, 1)
            close_layer0(nc, t, closing, inputs)
            attention(nc, t, dram, 1, inputs)
        with ExitStack() as ctx:
            t.gatesT = ctx.enter_context(nc.sbuf_tensor("gatesT1", [E, NTOK], F32))
            experts1(nc, t, dram, out)


_PLAIN = ["x", "g_xattn", "g_ffn"] + [f"L{l}_xattn_W{k}" for l in range(2) for k in "qkvo"] + [
    "L0_ffn_w1", "L0_ffn_w2", "L0_ffn_b2", "L1_ffn_up_w", "L1_ffn_down_w", "L1_ffn_down_b",
    "L1_ffn_sh_up_w", "L1_ffn_sh_down_w"]
_ROWS = ["L0_xattn_bv", "L0_xattn_bo", "L0_xattn_ln_gamma", "L0_xattn_ln_beta", "L1_xattn_bv", "L1_xattn_bo"]


def kernel(**inputs):
    import numpy as _np
    import concourse.bacc as _bacc
    from concourse import mybir as _mybir
    from concourse.bass_utils import run_bass_kernel_spmd as _run

    a = {k: _np.asarray(v) for k, v in inputs.items()}
    sent = {k: a[k] for k in _PLAIN}
    for k in _ROWS:
        sent[k] = a[k].reshape(1, -1)
    sent["ctxT"] = a["ctx_1024"].transpose(0, 2, 1)
    sent["mask"] = a["mask_Bx1x1xS2_ff0"].reshape(B, SC)
    columns = {"b1": "L0_ffn_b1", "bq0": "L0_xattn_bq", "bk0": "L0_xattn_bk", "bq1": "L1_xattn_bq",
               "bk1": "L1_xattn_bk", "up_b": "L1_ffn_up_b", "sh_up": "L1_ffn_sh_up_b", "sh_down": "L1_ffn_sh_down_b"}
    sent["bias_cols"] = _np.concatenate([a[columns[k]].reshape(-1, P).T for k in BIAS_COLS], axis=1)
    sent["router0"] = _np.concatenate([a["L0_ffn_router_w"], a["L0_ffn_lang_w"]], axis=0).T
    sent["router_bias"] = _np.concatenate([a["L0_ffn_router_b"], a["L0_ffn_lang_b"]]).reshape(1, NR)
    sent["router1"] = a["L1_ffn_gate_w"].T

    nc = _bacc.Bacc("TRN2", target_bir_lowering=False, num_devices=1)
    arrays, dram = {}, {}
    for name, v in sent.items():
        v = _np.ascontiguousarray(v)
        arrays[f"in_{name}_dram"] = v
        dram[name] = nc.dram_tensor(f"in_{name}_dram", v.shape, _mybir.dt.from_np(v.dtype), kind="ExternalInput").ap()
    dram["gates"] = nc.dram_tensor("gates_scratch", (E, NTOK), _mybir.dt.float32, kind="Internal").ap()
    out = nc.dram_tensor("out_0_dram", (B, S, D), _mybir.dt.float32, kind="ExternalOutput").ap()
    flamingo_layers(nc, dram, out)
    r = _run(nc, [arrays], core_ids=[0])
    return r.results[0]["out_0_dram"]
```
